# Optimizing a Trainium2 kernel written in Bass

```python
import numpy as np
import jax
import jax.numpy as jnp

def _softmax(x, axis=-1):
    return jax.nn.softmax(x, axis=axis)

def _gelu(x):
    return jax.nn.gelu(x, approximate=True)

def _silu(x):
    return jax.nn.silu(x)

def _sigmoid(x):
    return jax.nn.sigmoid(x)

def _layernorm(x, axis=-1, eps=1e-05):
    m = jnp.mean(x, axis=axis, keepdims=True)
    v = jnp.var(x, axis=axis, keepdims=True)
    return (x - m) / jnp.sqrt(v + eps)

def _scatter_add(tgt, idx, src, axis=0):
    return tgt.at[idx].add(src)

def _segment_sum(src, seg, n):
    return jax.ops.segment_sum(src, seg, n)
kernel_name = 'mk_adj_preln_d4_adj_r2_dfd53f'

def setup_inputs(seed: int=0):
    np.random.seed(seed)
    _w = jnp.asarray

    def _rec_inputs():
        import jax
        import jax.numpy as jnp
        _gk = jax.random.key(seed)
        x = -0.0002928 + 1 * jax.random.normal(jax.random.fold_in(_gk, 1), (2048, 256), jnp.float32)
        _a = jax.random.bernoulli(jax.random.fold_in(_gk, 2), 0.000976562, (2048, 2048))
        _a = jnp.logical_or(_a, jnp.swapaxes(_a, -1, -2))
        _a = jnp.logical_or(_a, jnp.eye(2048, dtype=bool))
        adj = _a.astype(jnp.int32)
        return (x, adj)
    x, adj = _rec_inputs()

    def _L0_gnn_setup():
        import jax, jax.numpy as jnp
        import numpy as np
        EPS = 1e-08
        key = jax.random.key(seed)
        k1, k2, k3 = jax.random.split(key, 3)
        N, IN_DIM, OUT_DIM = (4096, 256, 256)
        h = jax.random.normal(k1, (N, IN_DIM), dtype=jnp.float32)
        adj = jax.random.randint(k2, (N, N), 0, 2, dtype=jnp.int32)
        W = jax.random.normal(k3, (OUT_DIM, IN_DIM), dtype=jnp.float32) * (1.0 / np.sqrt(IN_DIM))
        return {'h': h, 'adj': adj, 'W': W}
    _L0_gnn_all = _L0_gnn_setup()
    _L0_gnn_in = {k: v for k, v in _L0_gnn_all.items() if k in ('W',)}
    del _L0_gnn_all

    def _L1_gnn_setup():
        import jax, jax.numpy as jnp
        import numpy as np
        key = jax.random.key(seed)
        kX, kA, k1, k2, k3, k4 = jax.random.split(key, 6)
        N, Cin, Cout = (4096, 256, 256)
        X = jax.random.normal(kX, (N, Cin), dtype=jnp.float32)
        A = jax.random.randint(kA, (N, N), 0, 2, dtype=jnp.int32)
        bound = 1.0 / np.sqrt(Cin)
        W_nb = jax.random.uniform(k1, (Cout, Cin), jnp.float32, -bound, bound)
        b_nb = jax.random.uniform(k2, (Cout,), jnp.float32, -bound, bound)
        W_line = jax.random.uniform(k3, (Cout, Cin), jnp.float32, -bound, bound)
        b_line = jax.random.uniform(k4, (Cout,), jnp.float32, -bound, bound)
        return {'X': X, 'A': A, 'W_nb': W_nb, 'b_nb': b_nb, 'W_line': W_line, 'b_line': b_line, 'neibor_num': 64}
    _L1_gnn_all = _L1_gnn_setup()
    _L1_gnn_in = {k: v for k, v in _L1_gnn_all.items() if k in ('W_nb', 'b_nb', 'W_line', 'b_line')}
    del _L1_gnn_all

    def _L2_gnn_setup():
        import jax, jax.numpy as jnp
        import numpy as np
        N = 4096
        IN_F = 256
        OUT_F = 256
        ALPHA = 0.2
        NEG_BIG = -9000000000000000.0
        key = jax.random.key(seed)
        k1, k2, k3, k4 = jax.random.split(key, 4)
        adjacency = jax.random.randint(k1, (N, N), 0, 2, dtype=jnp.int32)
        features = jax.random.normal(k2, (N, IN_F), dtype=jnp.float32)
        W = jax.random.normal(k3, (IN_F, OUT_F), dtype=jnp.float32) * (1.0 / np.sqrt(IN_F))
        attn = jax.random.normal(k4, (2 * OUT_F, 1), dtype=jnp.float32) * 0.05
        return {'adjacency': adjacency, 'features': features, 'W': W, 'attn': attn}
    _L2_gnn_all = _L2_gnn_setup()
    _L2_gnn_in = {k: v for k, v in _L2_gnn_all.items() if k in ('W', 'attn')}
    del _L2_gnn_all

    def _L3_gnn_setup():
        import jax, jax.numpy as jnp
        import numpy as np
        N = 2048
        IN_FEAT = 256
        EMBED = 256
        HEADS = 8
        HEAD_DIM = EMBED // HEADS
        SCALING = HEAD_DIM ** (-0.5)
        key = jax.random.key(seed)
        ks = jax.random.split(key, 7)
        x = jax.random.normal(ks[0], (N, IN_FEAT), dtype=jnp.float32)
        adj = jax.random.randint(ks[1], (N, N), 0, 2, dtype=jnp.int32)
        s = 0.04
        WQ = jax.random.normal(ks[2], (EMBED, IN_FEAT), dtype=jnp.float32) * s
        WK = jax.random.normal(ks[3], (EMBED, IN_FEAT), dtype=jnp.float32) * s
        WV = jax.random.normal(ks[4], (EMBED, IN_FEAT), dtype=jnp.float32) * s
        we = jax.random.normal(ks[5], (1, HEAD_DIM), dtype=jnp.float32) * 0.1
        be = jnp.zeros((1,), dtype=jnp.float32)
        return {'x': x, 'adj': adj, 'WQ': WQ, 'WK': WK, 'WV': WV, 'we': we, 'be': be}
    _L3_gnn_all = _L3_gnn_setup()
    _L3_gnn_in = {k: v for k, v in _L3_gnn_all.items() if k in ('WQ', 'WK', 'WV', 'we', 'be')}
    del _L3_gnn_all
    return {'x': x, 'adj': adj, 'L0_gnn_W': _L0_gnn_in['W'], 'L1_gnn_W_nb': _L1_gnn_in['W_nb'], 'L1_gnn_b_nb': _L1_gnn_in['b_nb'], 'L1_gnn_W_line': _L1_gnn_in['W_line'], 'L1_gnn_b_line': _L1_gnn_in['b_line'], 'L2_gnn_W': _L2_gnn_in['W'], 'L2_gnn_attn': _L2_gnn_in['attn'], 'L3_gnn_WQ': _L3_gnn_in['WQ'], 'L3_gnn_WK': _L3_gnn_in['WK'], 'L3_gnn_WV': _L3_gnn_in['WV'], 'L3_gnn_we': _L3_gnn_in['we'], 'L3_gnn_be': _L3_gnn_in['be']}

def reference(x, adj, L0_gnn_W, L1_gnn_W_nb, L1_gnn_b_nb, L1_gnn_W_line, L1_gnn_b_line, L2_gnn_W, L2_gnn_attn, L3_gnn_WQ, L3_gnn_WK, L3_gnn_WV, L3_gnn_we, L3_gnn_be):
    import jax
    import jax.numpy as jnp

    def _L0_gnn_ref(h, adj, W):
        import jax, jax.numpy as jnp
        import numpy as np
        EPS = 1e-08
        Wh = h @ W.T
        N = Wh.shape[0]
        norms = jnp.linalg.norm(Wh, axis=1, keepdims=True)
        sim = Wh @ Wh.T / (norms * norms.T + EPS)
        mask = (adj > 0) | jnp.eye(N, dtype=bool)
        sim_masked = jnp.where(mask, sim, -jnp.inf)
        alpha = jax.nn.softmax(sim_masked, axis=1)
        return alpha @ Wh

    def _L1_gnn_ref(X, A, W_nb, b_nb, W_line, b_line, neibor_num):
        import jax, jax.numpy as jnp
        import numpy as np
        Ab = A > 0
        keep = Ab & (jnp.cumsum(Ab.astype(jnp.int32), axis=1) <= neibor_num)
        cnt = keep.sum(axis=1, keepdims=True).astype(X.dtype)
        nb_sum = keep.astype(X.dtype) @ X
        nb_mean = nb_sum / jnp.maximum(cnt, 1.0)
        xj = jax.nn.leaky_relu(nb_mean @ W_nb.T + b_nb)
        xi = jax.nn.leaky_relu(X @ W_line.T + b_line)
        return xi + jnp.where(cnt > 0, xj, jnp.zeros((), X.dtype))

    def _L2_gnn_ref(adjacency, features, W, attn):
        import jax, jax.numpy as jnp
        import numpy as np
        N = 4096
        IN_F = 256
        OUT_F = 256
        ALPHA = 0.2
        NEG_BIG = -9000000000000000.0
        h = features @ W
        a1 = attn[:OUT_F, 0]
        a2 = attn[OUT_F:, 0]
        s1 = h @ a1
        s2 = h @ a2
        e = jax.nn.leaky_relu(s1[:, None] + s2[None, :], negative_slope=ALPHA)
        e = jnp.where(adjacency > 0, e, NEG_BIG)
        attention = jax.nn.softmax(e, axis=1)
        h_prime = attention @ h
        return jax.nn.elu(h_prime)

    def _L3_gnn_ref(x, adj, WQ, WK, WV, we, be):
        import jax, jax.numpy as jnp
        import numpy as np
        N = 2048
        IN_FEAT = 256
        EMBED = 256
        HEADS = 8
        HEAD_DIM = EMBED // HEADS
        SCALING = HEAD_DIM ** (-0.5)
        n = x.shape[0]
        Q = (x @ WQ.T).reshape(n, HEADS, HEAD_DIM).transpose(1, 0, 2)
        K = (x @ WK.T).reshape(n, HEADS, HEAD_DIM).transpose(1, 0, 2)
        V = (x @ WV.T).reshape(n, HEADS, HEAD_DIM).transpose(1, 0, 2)
        energy = Q @ we.T + be
        attn = jnp.einsum('hqd,hkd->hqk', Q, K) * SCALING + energy
        attn = attn + jnp.where(adj > 0, 0.0, -jnp.inf)
        attn = jax.nn.softmax(attn, axis=-1)
        hard = (attn == jnp.max(attn, axis=-1, keepdims=True)).astype(jnp.float32) / HEADS
        out = jnp.einsum('hqk,hkd->hqd', hard, V)
        return out.transpose(1, 0, 2).reshape(n, EMBED)
    h = jnp.maximum(_layernorm(x, axis=-1), 0.0)
    x = x + _L0_gnn_ref(h, adj, L0_gnn_W)
    h = jnp.maximum(_layernorm(x, axis=-1), 0.0)
    x = x + _L1_gnn_ref(h, adj, L1_gnn_W_nb, L1_gnn_b_nb, L1_gnn_W_line, L1_gnn_b_line, 64)
    h = jnp.maximum(_layernorm(x, axis=-1), 0.0)
    x = x + _L2_gnn_ref(adj, h, L2_gnn_W, L2_gnn_attn)
    h = jnp.maximum(_layernorm(x, axis=-1), 0.0)
    x = x + _L3_gnn_ref(h, adj, L3_gnn_WQ, L3_gnn_WK, L3_gnn_WV, L3_gnn_we, L3_gnn_be)
    return x

_drawn_inputs = setup_inputs


def setup_inputs(seed=0):
    import zlib

    import numpy as np

    out = dict(_drawn_inputs(seed))
    spreads = {}
    factors = {'L1_gnn_b_nb': 3.069, 'L1_gnn_b_line': 2.719}
    for name, (base, spread) in spreads.items():
        noise = np.random.default_rng([zlib.crc32(name.encode()), seed]).standard_normal(out[name].shape)
        drawn = base * np.exp(spread * noise) if base else spread * noise
        out[name] = jnp.asarray(drawn.astype(out[name].dtype))
    for name, factor in factors.items():
        out[name] = (out[name] * factor).astype(out[name].dtype)
    return out
```

```python
from contextlib import ExitStack

import numpy as np

import concourse.bass as bass
from concourse import mybir

ALU = mybir.AluOpType
ACT = mybir.ActivationFunctionType
F32 = mybir.dt.float32
F16 = mybir.dt.float16
BF16 = mybir.dt.bfloat16
F8 = mybir.dt.float8e4
U8 = mybir.dt.uint8
U16 = mybir.dt.uint16
I32 = mybir.dt.int32
U32 = mybir.dt.uint32
AX_X = mybir.AxisListType.X
ABSMAX = bass.bass_isa.ReduceOp.absmax

P = 128
N, D, H = 2048, 256, 8
DH = D // H
T = N // P
K = D // P
CH = 512
C = N // CH
TC = CH // P
NEIGHBORS = 64
EPS = 1e-5
L0_EPS = 1e-8
NEG = -(2.0 ** 120)
SCALING = float(DH) ** -0.5

H_UP = 2.0 ** 11
W_UP = 2.0 ** 13
G_DOWN = 2.0 ** -18
UNIT_UP = 2.0 ** 13
E_UP = 2.0 ** 14
UNIT_DOWN = 0.5 / UNIT_UP ** 2
ABOVE_ONE = 1.0 + 2.0 ** -23
TINY = 2.0 ** -40
LN2 = float(np.log(2.0))

W0, WNB, WLINE, W2, WQ, WK, WV, WS, WE = range(9)

A_M = 0
A_MT = A_M + T * N
A_SG, A_K4 = A_MT, A_MT + 2 * H * N
A_G = A_MT + 2 * T * N
A_R3 = A_G + T * 2 * (D + 2) * 2
A_UB = A_R3 + 2 * K * N * 2
A_XB = A_UB + 4 * N
A_F = A_XB + 4 * N
A_X = A_F + 24576
A_W = A_X + T * D * 4
A_END = A_W + 16384


def adjacency_net(nc, x, adj, weights, attn, b_nb, b_line, we, be, out, stop):
    with ExitStack() as ctx:
        def sb(name, shape, dt):
            return ctx.enter_context(nc.sbuf_tensor(name, shape, dt))

        def sem(name):
            return ctx.enter_context(nc.semaphore(name))

        arena = sb("arena", [P, A_END], U8)
        SIZE = {F32: 4, F16: 2, BF16: 2, F8: 1, U8: 1, U16: 2, I32: 4, U32: 4}

        def at(offset, shape, dt):
            n = SIZE[dt]
            for s in shape:
                n *= s
            a = arena[:, offset:offset + n]
            if dt is not U8:
                a = a.bitcast(dt)
            if len(shape) == 2:
                a = a.rearrange("p (a b) -> p a b", a=shape[0])
            if len(shape) == 3:
                a = a.rearrange("p (a b c) -> p a b c", a=shape[0], b=shape[1])
            if len(shape) == 4:
                a = a.rearrange("p (a b c d) -> p a b c d", a=shape[0], b=shape[1], c=shape[2])
            return a

        no_edge = at(A_M, [T, N], U8)
        no_edge_T = at(A_MT, [T, N], BF16)
        no_edge_T_flat = at(A_MT, [T * N], BF16)
        G = at(A_G, [T, 2, D + 2], F16)
        xs = at(A_X, [T, D], F32)
        ws0 = at(A_W, [2, K, D], F16)
        ws1 = at(A_W + 2048, [2, K, 2 * D], F16)
        ws2 = at(A_W + 6144, [2, K, D + 2], F16)
        wsq = at(A_W + 8208, [2, K, D], F16)
        wsk = at(A_W + 10256, [2, K, D], F16)
        wsv = at(A_W + 12304, [2, K, D], F16)
        h32 = [at(A_F + 4096 * b, [TC, D], F32) for b in range(2)]
        hn = [at(A_F + 8192 + 4096 * b, [2, TC, D], F16) for b in range(2)]
        hT = [at(A_F + 16384 + 4096 * b, [2, K, CH], F16) for b in range(2)]

        ident = sb("ident", [P, P], BF16)
        ident16 = sb("ident16", [P, P], F16)
        ident32 = sb("ident32", [P, P], F32)
        off_diag = sb("off_diag", [P, P], BF16)
        ones32 = sb("ones32", [P, P], F32)
        ones16 = sb("ones16", [P, P], F16)
        head_bit = sb("head_bit", [P, H, P], BF16)
        wsc = sb("wsc", [P, 6, 9], F32)
        sc = sb("sc", [P, 8], F32)
        w12 = sb("w12", [P, K, 2], F32)
        wec = sb("wec", [P, 1], F32)
        bec = sb("bec", [P, 1], F32)
        st6 = sb("st6", [P, T, 6], F32)
        mv = sb("mv", [P, T, 2], F32)
        cols = sb("cols", [P, 8, T], F32)
        s12 = sb("s12", [P, T, 2], F32)
        tiny = sb("tiny", [P, 16], F32)
        wmax, wpow, wup, kG, kL, kI = (wsc[:, i, :] for i in range(6))
        veps, std, r2, nbias, nsq, ucol, acol, bcol = (cols[:, i, :] for i in range(8))

        psum = ctx.enter_context(nc.psum_tensor("psum", [P, 8, CH], F32))

        def tp(b, dt=F16):
            return psum[:, 2 * b:2 * b + 2, :].rearrange("p a b -> p (a b)").bitcast(dt)

        x_t = x.rearrange("(t p) d -> p t d", p=P)
        out_t = out.rearrange("(t p) d -> p t d", p=P)
        adj_t = adj.rearrange("(t p) j -> p t j", p=P)

        barrier_sem = sem("stage_done")

        def stage_end(eng, k):
            eng.drain().then_inc(barrier_sem, 1)
            eng.wait_ge(barrier_sem, 5 * k)

        wraw = at(A_F, [7, K, D], F32)
        ab = at(A_F + 14336, [2, D], F32)
        wtmp = at(A_F + 16384, [2 * D], F32)
        adjb = [at(A_UB + 8192 * b, [N], I32) for b in range(2)]
        bb = [at(A_R3 + 4096 * b, [N], BF16) for b in range(2)]
        diag_save = sb("diag_save", [P, T, P], U8)

        w_ld, x_ld = sem("weights_loaded"), sem("x_loaded")
        adj_ld = [sem("adj_loaded0"), sem("adj_loaded1")]
        consts_ok, wmax_ok, wall_ok = sem("consts_ok"), sem("weight_max"), sem("weight_max_all")
        bb_ok, m_ok, tp_ok, mt_ok = sem("mask_tile"), sem("mask_kept"), sem("mask_turned"), sem("mask_T_kept")
        wp = sem("weight_prep")
        dg = sem("diagonal")
        gate = sem("act_gate")

        def load_sync(sp):
            for i, w in enumerate(weights):
                sp.dma_start(wraw[:, i], w.rearrange("(k p) o -> p k o", p=P)).then_inc(w_ld, 16)
            a = attn.rearrange("(a d) o -> (o a) d", a=2)
            for i in range(2):
                sp.dma_start(ab[:, i], a[i].partition_broadcast(P)).then_inc(w_ld, 16)
            for i in range(4):
                sp.dma_start(wec[DH * i:DH * i + DH, :], we.rearrange("o d -> d o")).then_inc(w_ld, 16)
            sp.dma_start(bec[:], be.partition_broadcast(P)).then_inc(w_ld, 16)
            sp.dma_start(xs, x_t).then_inc(x_ld, 16)
            with sp.Fori(0, T // 2) as i:
                for b in range(2):
                    sp.wait_ge(bb_ok, i * 2 + b + 1)
                    sp.dma_start(adjb[b], adj_t[:, bass.ds(i * 2 + b, 1), :]).then_inc(adj_ld[b], 16)

        def load_pool(pool):
            nc.gpsimd.memset(ones32[:], 1.0).then_inc(consts_ok, 1)
            pool.wait_ge(consts_ok, 1)
            nc.gpsimd.affine_select(out=ident32[:], in_=ones32[:], pattern=[[-1, P]], compare_op=ALU.is_equal,
                                    fill=0.0, base=0, channel_multiplier=1).then_inc(consts_ok, 1)
            pool.wait_ge(consts_ok, 2)
            nc.gpsimd.tensor_copy(ident[:], ident32[:]).then_inc(consts_ok, 1)
            nc.gpsimd.tensor_copy(ident16[:], ident32[:]).then_inc(consts_ok, 1)
            nc.gpsimd.tensor_copy(ones16[:], ones32[:]).then_inc(consts_ok, 1)
            nc.gpsimd.tensor_scalar(off_diag[:], ident32[:], -1.0, 1.0, ALU.mult, ALU.add).then_inc(consts_ok, 1)
            for h in range(H):
                nc.gpsimd.tensor_scalar(head_bit[:, h], ident32[:], 2.0 ** h, 0.0, ALU.mult, ALU.add
                                        ).then_inc(consts_ok, 1)
            pool.wait_ge(wmax_ok, 1)
            nc.gpsimd.partition_all_reduce(wsc[:, 1, :], wsc[:, 0, :], P, ABSMAX).then_inc(wall_ok, 1)
            pool.sem_inc(m_ok, 2)
            with pool.Fori(0, T // 2) as i:
                for b in range(2):
                    pool.wait_ge(bb_ok, i * 2 + b + 3)
                    nc.gpsimd.tensor_copy(no_edge[:, bass.ds(i * 2 + b, 1), :], bb[b]).then_inc(m_ok, 1)

        def load_tensor(pe):
            pe.wait_ge(consts_ok, 3)
            pe.sem_inc(tp_ok, 2)
            with pe.Fori(0, T // 2) as i:
                for b in range(2):
                    pe.wait_ge(bb_ok, i * 2 + b + 3)
                    pe.wait_ge(mt_ok, i * 2 + b + 1)
                    for j in range(T):
                        last = pe.transpose(tp(b, BF16)[:, P * j:P * j + P], bb[b][:, P * j:P * j + P], ident[:])
                    last.then_inc(tp_ok, 1)

        def load_scalar(act):
            act.sem_inc(mt_ok, 2)
            with act.Fori(0, T // 2) as i:
                for b in range(2):
                    act.wait_ge(tp_ok, i * 2 + b + 3)
                    act.sem_inc(gate, 1)
                    act.activation(no_edge_T[:, :, bass.ds(i * 256 + b * P, P)],
                                   tp(b, BF16).rearrange("p (j i) -> p j i", j=T), ACT.Copy, scale=NEG
                                   ).then_inc(mt_ok, 1)

        def load_vector(dve):
            count = [0]

            def step(ins):
                count[0] += 1
                ins.then_inc(wp, 1)
                dve.wait_ge(wp, count[0])

            dve.wait_ge(w_ld, 16 * 14)
            step(dve.tensor_reduce(wmax[:, 0:7], wraw.rearrange("p w k o -> p w (k o)"), AX_X, ALU.max,
                                   apply_absolute_value=True))
            for k in range(K):
                for a in range(2):
                    step(dve.tensor_tensor_reduce(wtmp[:, 0:D], wraw[:, W2, k], ab[:, a], 1.0, 0.0, ALU.mult,
                                                  ALU.add, w12[:, k, a:a + 1]))
            step(dve.tensor_reduce(wmax[:, WS:WS + 1], w12[:].rearrange("p k a -> p (k a)"), AX_X, ALU.max,
                                   apply_absolute_value=True))
            dve.tensor_reduce(wmax[:, WE:WE + 1], wec[:], AX_X, ALU.max, apply_absolute_value=True
                              ).then_inc(wmax_ok, 1)
            dve.wait_ge(wall_ok, 1)
            step(dve.tensor_scalar(sc[:, 0:1], wpow[:, WE:WE + 1], 1.0, None, ALU.mult))
            step(dve.tensor_scalar(kI, wpow, TINY, None, ALU.max))
            step(dve.tensor_scalar(wpow.bitcast(U32), kI.bitcast(U32), 0x7F800000, None, ALU.bitwise_and))
            step(dve.reciprocal(kI, wpow))
            step(dve.tensor_scalar(wup, kI, W_UP, None, ALU.mult))
            step(dve.tensor_scalar(kG, wpow, 1.0 / (W_UP * H_UP * G_DOWN), None, ALU.mult))
            step(dve.tensor_scalar(kL, wpow, 1.0 / (W_UP * H_UP), None, ALU.mult))
            step(dve.tensor_scalar(kI, wup, H_UP * G_DOWN, None, ALU.mult))
            step(dve.tensor_scalar(sc[:, 1:2], wpow[:, WK:WK + 1], SCALING * 512.0, sc[:, 0:1], ALU.mult, ALU.add))
            step(dve.tensor_scalar(sc[:, 3:4].bitcast(U32), sc[:, 1:2].bitcast(U32), 0x7F800000, None,
                                   ALU.bitwise_and))
            step(dve.reciprocal(sc[:, 4:5], sc[:, 3:4]))
            step(dve.tensor_scalar(sc[:, 2:3], sc[:, 4:5], 2.0 ** 14, None, ALU.mult))
            step(dve.tensor_scalar(sc[:, 5:6], sc[:, 2:3], kL[:, WK:WK + 1], SCALING, ALU.mult, ALU.mult))
            step(dve.tensor_scalar(wec[:], wec[:], sc[:, 2:3], None, ALU.mult))
            step(dve.tensor_scalar(bec[:], bec[:], sc[:, 2:3], kI[:, WQ:WQ + 1], ALU.mult, ALU.mult))
            for w, dst in ((W0, ws0), (WNB, ws1[:, :, :, 0:D]), (WLINE, ws1[:, :, :, D:]),
                           (W2, ws2[:, :, :, 0:D]), (WQ, wsq), (WK, wsk), (WV, wsv)):
                step(dve.tensor_scalar(dst[:, 0], wraw[:, w], wup[:, w:w + 1], None, ALU.mult))
                step(dve.scalar_tensor_tensor(dst[:, 1], wraw[:, w], wup[:, w:w + 1], dst[:, 0], ALU.mult,
                                              ALU.subtract))
            step(dve.tensor_scalar(ws2[:, 0, :, D:], w12[:], wup[:, WS:WS + 1], None, ALU.mult))
            step(dve.scalar_tensor_tensor(ws2[:, 1, :, D:], w12[:], wup[:, WS:WS + 1], ws2[:, 0, :, D:],
                                          ALU.mult, ALU.subtract))
            dve.wait_ge(consts_ok, 6 + H)
            for t in range(T):
                step(dve.memset(G[:, t, 0, D:], 1.0))
                step(dve.memset(G[:, t, 1, D:], 0.0))
            dve.sem_inc(bb_ok, 2)
            with dve.Fori(0, T // 2) as i:
                for b in range(2):
                    dve.wait_ge(adj_ld[b], i * 16 + 16)
                    dve.wait_ge(tp_ok, i * 2 + b + 1)
                    dve.wait_ge(m_ok, i * 2 + b + 1)
                    dve.tensor_scalar(bb[b], adjb[b], 0, None, ALU.is_le).then_inc(bb_ok, 1)
            dve.wait_ge(mt_ok, T + 2)
            dve.sem_inc(dg, 1)
            with dve.Fori(0, T) as i:
                block = no_edge_T_flat[:, bass.ds(i * (N + P), P)]
                dve.wait_ge(dg, i * 2 + 1)
                dve.tensor_scalar(diag_save[:, bass.ds(i, 1), :], block, 1.0 / NEG, None, ALU.mult).then_inc(dg, 1)
                dve.wait_ge(dg, i * 2 + 2)
                dve.tensor_tensor(block, block, off_diag[:], ALU.mult).then_inc(dg, 1)

        class Front:
            def __init__(self, name):
                self.stats = sem(name + "_stats")
                self.h_ok = sem(name + "_h")
                self.split_ok = sem(name + "_split")
                self.turned = sem(name + "_turned")
                self.hT_ok = sem(name + "_hT")
                self.lin_ok = sem(name + "_linear")
                self.post_a = sem(name + "_post_act")
                self.post_v = sem(name + "_post_dve")
                self.a0, self.std_ok = sem(name + "_a"), sem(name + "_std")

            def vector(self, dve):
                dve.wait_ge(x_ld, 16)
                for t in range(T):
                    dve.bn_stats(st6[:, t], xs[:, t]).then_inc(self.stats, 1)
                for t in range(T):
                    dve.wait_ge(self.stats, T)
                    dve.bn_aggr(mv[:, t], st6[:, t]).then_inc(self.stats, 1)
                dve.wait_ge(self.stats, 2 * T)
                dve.tensor_scalar(veps, mv[:, :, 1], EPS, None, ALU.add).then_inc(self.stats, 1)
                dve.wait_ge(self.std_ok, 1)
                dve.reciprocal(nsq, std).then_inc(self.stats, 1)
                dve.wait_ge(self.stats, 2 * T + 2)
                dve.tensor_scalar(r2, nsq, H_UP, None, ALU.mult).then_inc(self.stats, 1)
                dve.wait_ge(self.stats, 2 * T + 3)
                dve.scalar_tensor_tensor(nbias, mv[:, :, 0], -1.0, r2, ALU.mult, ALU.mult).then_inc(self.stats, 1)

                def split(g):
                    dve.wait_ge(self.h_ok, TC * (g + 1))
                    if g >= 2:
                        dve.wait_ge(self.turned, g - 1)
                    dve.tensor_copy(hn[g % 2][:, 0], h32[g % 2]).then_inc(self.split_ok, 1)
                    dve.wait_ge(self.split_ok, 2 * g + 1)
                    dve.tensor_tensor(hn[g % 2][:, 1], h32[g % 2], hn[g % 2][:, 0], ALU.subtract
                                      ).then_inc(self.split_ok, 1)
                split(0)
                split(1)
                split(2)
                self.post_dve(dve, 0)
                split(3)
                for g in range(1, C):
                    self.post_dve(dve, g)

            def scalar(self, act):
                act.wait_ge(self.stats, 2 * T + 1)
                act.activation(std, veps, ACT.Sqrt).then_inc(self.std_ok, 1)
                act.wait_ge(self.stats, 2 * T + 4)

                def relu(g):
                    if g >= 2:
                        act.wait_ge(self.split_ok, 2 * (g - 1))
                    for t in range(TC):
                        i = TC * g + t
                        act.activation(h32[g % 2][:, t], xs[:, i], ACT.Relu, scale=r2[:, i:i + 1],
                                       bias=nbias[:, i:i + 1]).then_inc(self.h_ok, 1)

                def turn(g):
                    act.wait_ge(self.turned, g + 1)
                    if g >= 2:
                        act.wait_ge(self.lin_ok, g - 1)
                    act.activation(hT[g % 2].rearrange("p a b c -> p (a b c)"), tp(g % 2), ACT.Copy
                                   ).then_inc(self.hT_ok, 1)
                relu(0)
                relu(1)
                turn(0)
                relu(2)
                turn(1)
                self.post_act(act, 0)
                relu(3)
                turn(2)
                self.post_act(act, 1)
                turn(3)
                self.post_act(act, 2)
                self.post_act(act, 3)

            def tensor(self, pe):
                def turn(g):
                    pe.wait_ge(self.split_ok, 2 * g + 2)
                    if g >= 2:
                        pe.wait_ge(self.hT_ok, g - 1)
                    for hl in range(2):
                        for k in range(K):
                            for t in range(TC):
                                c = ((hl * K + k) * TC + t) * P
                                last = pe.transpose(tp(g % 2)[:, c:c + P], hn[g % 2][:, hl, t, P * k:P * k + P],
                                                    ident16[:])
                    last.then_inc(self.turned, 1)

                def lin(g):
                    pe.wait_ge(self.hT_ok, g + 1)
                    self.linear(pe, g).then_inc(self.lin_ok, 1)
                turn(0)
                turn(1)
                lin(0)
                turn(2)
                lin(1)
                turn(3)
                lin(2)
                lin(3)

        TERMS = ((0, 0), (0, 1), (1, 0))

        def product(pe, dst, lhs, rhs):
            n = 0
            for a, b in TERMS:
                for k in range(K):
                    last = pe.matmul(dst, lhs(a, k), rhs(b, k), start=(n == 0), stop=(n == len(TERMS) * K - 1))
                    n += 1
            return last

        def lin_bank(t):
            return psum[:, 4 + t, :]

        def linear_rows(w, n, front):
            def linear(pe, g):
                if g >= 1:
                    pe.wait_ge(front().post_a, front().copies * g)
                    if front().adds_to_x:
                        pe.wait_ge(front().post_v, front().adds_to_x * g)
                for t in range(TC):
                    last = product(pe, lin_bank(t)[:, 0:n], lambda hl, k: hT[g % 2][:, hl, k, P * t:P * t + P],
                                   lambda hl, k: w[:, hl, k, 0:n])
                return last
            return linear

        gf = at(A_UB, [T, D], F32)
        WhnT = at(A_R3, [2, K, N], F16)
        u_b = at(A_UB, [N], F32)
        whn32 = [at(A_F + 4096 * b, [TC, D], F32) for b in range(2)]
        whn = [at(A_F + 8192 + 4096 * b, [2, TC, D], F16) for b in range(2)]
        diag_u = at(A_F + 16384, [TC, P], F32)
        junk = at(A_F + 18432, [D], F32)
        l0b_v, l0b_a, l0b_t = sem("l0_unit_rows"), sem("l0_unit_kept"), sem("l0_unit_turned")
        l0n, l0n_a, l0d, l0u = sem("l0_norms"), sem("l0_sqrt"), sem("l0_diag"), sem("l0_u")
        l0u_a = sem("l0_u_kept")

        def l0_post_act(act, g):
            f = fronts[0]
            act.wait_ge(f.lin_ok, g + 1)
            act.activation(gf[:, TC * g:TC * g + TC], psum[:, 4:8, 0:D], ACT.Copy, scale=G_DOWN).then_inc(f.post_a, 1)

        def l0_post_dve(dve, g):
            f = fronts[0]
            dve.wait_ge(f.post_a, g + 1)
            i = TC * g
            dve.tensor_copy(G[:, i:i + TC, 0, 0:D], gf[:, i:i + TC]).then_inc(f.post_v, 1)
            dve.wait_ge(f.post_v, 2 * g + 1)
            dve.tensor_tensor(G[:, i:i + TC, 1, 0:D], gf[:, i:i + TC], G[:, i:i + TC, 0, 0:D], ALU.subtract
                              ).then_inc(f.post_v, 1)

        def l0_unit_vector(dve):
            for t in range(T):
                dve.wait_ge(l0n, t) if t else None
                dve.tensor_tensor_reduce(junk, gf[:, t], gf[:, t], 1.0, 0.0, ALU.mult, ALU.add, nsq[:, t:t + 1]
                                         ).then_inc(l0n, 1)
            dve.wait_ge(l0n, T)
            dve.tensor_scalar(veps, nsq, 2.0 ** -62, None, ALU.max).then_inc(l0n, 1)
            dve.tensor_scalar(tiny[:, 2:3], kG[:, W0:W0 + 1].bitcast(I32), 2.0 ** -23, -127.0, ALU.mult, ALU.add
                              ).then_inc(l0n, 1)
            dve.wait_ge(l0n_a, 2)
            dve.reciprocal(ucol, std).then_inc(l0n, 1)
            dve.wait_ge(l0n, T + 3)
            dve.tensor_scalar(tiny[:, 3:4], tiny[:, 2:3], LN2 / 2, None, ALU.mult).then_inc(l0n, 1)
            dve.wait_ge(l0n, T + 4)
            dve.tensor_scalar(acol, bcol, 0.25, tiny[:, 3:4], ALU.mult, ALU.add).then_inc(l0n, 1)
            dve.wait_ge(l0n, T + 5)
            dve.tensor_scalar(bcol, acol, -0.5 * float(np.log(L0_EPS)), None, ALU.add).then_inc(l0n, 1)
            for g in range(C):
                b = g % 2
                for t in range(TC):
                    i = TC * g + t
                    dve.tensor_scalar(whn32[b][:, t], gf[:, i], ucol[:, i:i + 1], UNIT_UP, ALU.mult, ALU.mult
                                      ).then_inc(l0b_v, 1)
                if g >= 2:
                    dve.wait_ge(l0b_t, g - 1)
                dve.wait_ge(l0b_v, 6 * g + 4)
                dve.tensor_copy(whn[b][:, 0], whn32[b]).then_inc(l0b_v, 1)
                dve.wait_ge(l0b_v, 6 * g + 5)
                dve.tensor_tensor(whn[b][:, 1], whn32[b], whn[b][:, 0], ALU.subtract).then_inc(l0b_v, 1)
                dve.wait_ge(l0b_v, 6 * g + 6)
            for g in range(C):
                if g >= 1:
                    dve.wait_ge(l0u, g)
                for t in range(TC):
                    i = TC * g + t
                    dve.tensor_scalar(diag_u[:, t], ident32[:], acol[:, i:i + 1], None, ALU.mult).then_inc(l0d, 1)

        def l0_unit_tensor(pe):
            for g in range(C):
                pe.wait_ge(l0b_v, 6 * g + 6)
                if g >= 2:
                    pe.wait_ge(l0b_a, g - 1)
                for hl in range(2):
                    for k in range(K):
                        for t in range(TC):
                            c = ((hl * K + k) * TC + t) * P
                            last = pe.transpose(tp(g % 2)[:, c:c + P], whn[g % 2][:, hl, t, P * k:P * k + P],
                                                ident16[:])
                last.then_inc(l0b_t, 1)
            for g in range(C):
                pe.wait_ge(l0d, TC * (g + 1))
                if g == 0:
                    pe.wait_ge(fronts[0].post_a, C)
                for t in range(TC):
                    last = pe.matmul(psum[:, 4 + g, P * t:P * t + P], ones32[:], diag_u[:, t], start=True, stop=True)
                last.then_inc(l0u, 1)

        def l0_unit_scalar(act):
            act.wait_ge(l0n, T + 1)
            act.activation(std, veps, ACT.Sqrt).then_inc(l0n_a, 1)
            act.activation(bcol, veps, ACT.Ln).then_inc(l0n_a, 1)
            for g in range(C):
                act.wait_ge(l0b_t, g + 1)
                act.activation(WhnT[:, :, :, CH * g:CH * g + CH], tp(g % 2).rearrange("p (a b c) -> p a b c", a=2, b=K),
                               ACT.Copy).then_inc(l0b_a, 1)
            for g in range(C):
                act.wait_ge(l0u, g + 1)
                act.wait_ge(l0b_v, 6 * C)
                act.activation(u_b[:, CH * g:CH * g + CH], psum[:, 4 + g, :], ACT.Copy).then_inc(l0u_a, 1)

        den = [at(A_F + 2048 * b, [CH], F32) for b in range(2)]
        sim = [at(A_F + 4096 + 2048 * b, [CH], F32) for b in range(2)]
        num = [at(A_F + 8192 + 2048 * b, [CH], F32) for b in range(2)]
        num_hl = [at(A_F + 12288 + 2048 * b, [2, CH], F16) for b in range(3)]
        el_tmp = at(A_F + 18432, [D + 2], F32)
        el_tmp2 = at(A_F + 18432 + 1040, [D], F32)
        el_tmp3 = at(A_F + 18432 + 2064, [D], F32)

        class Attention:

            def __init__(self, name):
                self.scores = sem(name + "_scores")
                self.den = sem(name + "_den")
                self.rec = sem(name + "_rec")
                self.sim = sem(name + "_sim")
                self.num = sem(name + "_num")
                self.hi = sem(name + "_hi")
                self.lo = sem(name + "_lo")
                self.summed = sem(name + "_summed")
                self.taken = sem(name + "_taken")
                self.ep = sem(name + "_epilogue")
                self.ep_a = sem(name + "_elu")

        A0 = Attention("l0")

        S_BANK = (4, 5, 6)

        def av_step(pe, A, c, j):
            n = c * T + j
            pe.wait_ge(A.lo, n + 4)
            if j == 0:
                pe.wait_ge(A.taken, c + 1)
            e = num_hl[j % 3]
            for t in range(TC):
                o = psum[:, t, 0:D + 1]
                pe.matmul(o, e[:, 0, P * t:P * t + P], G[:, j, 0, 0:D + 1], start=(j == 0), stop=False)
                pe.matmul(o, e[:, 0, P * t:P * t + P], G[:, j, 1, 0:D + 1], start=False, stop=False)
                last = pe.matmul(o, e[:, 1, P * t:P * t + P], G[:, j, 0, 0:D + 1], start=False, stop=(j == T - 1))
            last.then_inc(A.summed, 1)

        def l0_tensor(pe):
            A = A0
            pe.sem_inc(A.scores, 3)
            pe.sem_inc(A.summed, 3)

            with pe.Fori(0, C) as c:
                def scores(j):
                    pe.wait_ge(A.sim, c * T + j + 1)
                    dst = psum[:, S_BANK[j % 3], :]
                    pe.matmul(dst, ident[:], no_edge_T[:, j, bass.ds(c * CH, CH)], start=True, stop=False)
                    m = 0
                    for a, b in TERMS:
                        for k in range(K):
                            m += 1
                            last = pe.matmul(dst, WhnT[:, a, k, P * j:P * j + P], WhnT[:, b, k, bass.ds(c * CH, CH)],
                                             start=False, stop=(m == 3 * K))
                    last.then_inc(A.scores, 1)
                scores(0)
                scores(1)
                for j in range(T):
                    if j + 2 < T:
                        scores(j + 2)
                    av_step(pe, A, c, j)

        def l0_scalar(act):
            A = A0
            act.sem_inc(A.den, 3)
            act.sem_inc(A.num, 3)
            act.sem_inc(A.hi, 3)
            with act.Fori(0, C) as c:
                def den_(j):
                    act.wait_ge(A.sim, c * T + j + 2)
                    act.sem_inc(gate, 1)
                    act.activation(den[j % 2], u_b[:, bass.ds(c * CH, CH)], ACT.Tanh, bias=bcol[:, j:j + 1]
                                   ).then_inc(A.den, 1)
                den_(0)
                den_(1)
                for j in range(T):
                    n = c * T + j
                    act.wait_ge(A.sim, n + 4)
                    act.wait_ge(A.lo, n + 2)
                    act.activation(num[j % 2], sim[j % 2], ACT.Exp, scale=UNIT_DOWN).then_inc(A.num, 1)
                    act.wait_ge(A.summed, n + 1)
                    act.activation(num_hl[j % 3][:, 0], sim[j % 2], ACT.Exp, scale=UNIT_DOWN).then_inc(A.hi, 1)
                    if j + 2 < T:
                        den_(j + 2)

        def l0_vector(dve):
            A = A0
            dve.sem_inc(A.sim, 3)
            dve.sem_inc(A.lo, 3)
            dve.sem_inc(A.taken, 1)
            dve.sem_inc(A.ep, 1)
            with dve.Fori(0, C) as c:
                def lo_(j):
                    n = c * T + j
                    dve.wait_ge(A.hi, n + 4)
                    dve.tensor_tensor(num_hl[j % 3][:, 1], num[j % 2], num_hl[j % 3][:, 0], ALU.subtract
                                      ).then_inc(A.lo, 1)
                for j in range(T):
                    n = c * T + j
                    dve.wait_ge(A.den, n + 4)
                    dve.wait_ge(A.scores, n + 4)
                    dve.wait_ge(A.hi, n + 2)
                    dve.scalar_tensor_tensor(sim[j % 2], den[j % 2], ABOVE_ONE, psum[:, S_BANK[j % 3], :],
                                             ALU.add, ALU.mult).then_inc(A.sim, 1)
                    if j >= 1:
                        lo_(j - 1)
                lo_(T - 1)
                dve.wait_ge(A.summed, c * T + T + 3)
                for t in range(TC):
                    o = psum[:, t, :]
                    k0 = 3 * t
                    dve.wait_ge(A.ep, c * 12 + k0 + 1)
                    dve.reciprocal(tiny[:, 0:1], o[:, D:D + 1]).then_inc(A.ep, 1)
                    dve.wait_ge(A.ep, c * 12 + k0 + 2)
                    dve.tensor_scalar(tiny[:, 1:2], tiny[:, 0:1], kG[:, W0:W0 + 1], None, ALU.mult).then_inc(A.ep, 1)
                    dve.wait_ge(A.ep, c * 12 + k0 + 3)
                    x_i = xs[:, bass.ds(c * TC + t, 1), :].rearrange("p a d -> p (a d)")
                    last = dve.scalar_tensor_tensor(x_i, o[:, 0:D], tiny[:, 1:2], x_i, ALU.mult, ALU.add
                                                    ).then_inc(A.ep, 1)
                dve.wait_ge(A.ep, c * 12 + 13)
                dve.sem_inc(A.taken, 1)

        class Spread:
            def __init__(self, name):
                self.diag, self.out, self.kept = sem(name + "_diag"), sem(name + "_out"), sem(name + "_kept")

            def vector(self, dve, col):
                for g in range(C):
                    if g >= 1:
                        dve.wait_ge(self.out, g)
                    for t in range(TC):
                        i = TC * g + t
                        dve.tensor_scalar(diag[:, t], ident32[:], col(i), None, ALU.mult).then_inc(self.diag, 1)

            def tensor(self, pe):
                for g in range(C):
                    pe.wait_ge(self.diag, TC * (g + 1))
                    for t in range(TC):
                        last = pe.matmul(psum[:, 4 + g, P * t:P * t + P], ones32[:], diag[:, t], start=True,
                                         stop=True)
                    last.then_inc(self.out, 1)

            def scalar(self, act, dst):
                for g in range(C):
                    act.wait_ge(self.out, g + 1)
                    act.activation(dst[:, CH * g:CH * g + CH], psum[:, 4 + g, :], ACT.Copy).then_inc(self.kept, 1)

        diag = at(A_F + 16384, [TC, P], F32)

        gfb = [at(A_UB + 4096 * b, [TC, D], F32) for b in range(2)]
        zline = at(A_XB, [TC, D], F32)
        b_rows = at(A_XB + 4096, [2, D], F32)
        z_t = at(A_XB + 6144, [D], F32)
        b_ld = sem("bias_loaded")

        def l1_load(sp):
            sp.dma_start(b_rows[:, 0], b_nb.partition_broadcast(P)).then_inc(b_ld, 16)
            sp.dma_start(b_rows[:, 1], b_line.partition_broadcast(P)).then_inc(b_ld, 16)

        def split_post_act(i):
            def post(act, g):
                f = fronts[i]
                act.wait_ge(f.lin_ok, g + 1)
                if g >= 2:
                    act.wait_ge(f.post_v, f.per_v * (g - 1))
                act.activation(gfb[g % 2], psum[:, 4:8, 0:D], ACT.Copy, scale=G_DOWN).then_inc(f.post_a, 1)
                if i == 2:
                    act.activation(s12[:, TC * g:TC * g + TC, :], psum[:, 4:8, D:D + 2], ACT.Identity,
                                   scale=kL[:, WS:WS + 1]).then_inc(f.post_a, 1)
            return post

        def split_post_dve(i):
            def post(dve, g):
                f = fronts[i]
                n, r = f.per_v * g, TC * g
                dve.wait_ge(f.post_a, f.copies * g + 1)
                dve.tensor_copy(G[:, r:r + TC, 0, 0:D], gfb[g % 2]).then_inc(f.post_v, 1)
                dve.wait_ge(f.post_v, n + 1)
                dve.tensor_tensor(G[:, r:r + TC, 1, 0:D], gfb[g % 2], G[:, r:r + TC, 0, 0:D], ALU.subtract
                                  ).then_inc(f.post_v, 1)
                if i == 1:
                    if g == 0:
                        dve.wait_ge(b_ld, 32)
                    for t in range(TC):
                        dve.scalar_tensor_tensor(zline[:, t], psum[:, 4 + t, D:2 * D], kL[:, WLINE:WLINE + 1],
                                                 b_rows[:, 1], ALU.mult, ALU.add).then_inc(f.post_v, 1)
                    dve.wait_ge(f.post_v, n + 6)
                    dve.scalar_tensor_tensor(zline, zline, 0.01, zline, ALU.mult, ALU.max).then_inc(f.post_v, 1)
                    dve.wait_ge(f.post_v, n + 7)
                    dve.tensor_tensor(xs[:, r:r + TC], xs[:, r:r + TC], zline, ALU.add).then_inc(f.post_v, 1)
                    dve.wait_ge(f.post_v, n + 8)
            return post

        edge = [at(A_F + 4096 * b, [N], BF16) for b in range(2)]
        run = [at(A_F + 8192 + 4112 * b, [N + 2], BF16) for b in range(2)]
        keep = [at(A_R3 + 4096 * b, [N], BF16) for b in range(2)]
        keepT = [at(A_R3 + 8192 + 4096 * b, [T, P], BF16) for b in range(2)]
        cap = at(A_UB, [N], BF16)
        e_ok, run_ok, keep_ok = sem("l1_edges"), sem("l1_count"), sem("l1_keep")
        kt_ok, ktc_ok, agg_ok, l1_out = sem("l1_keep_turned"), sem("l1_keepT"), sem("l1_summed"), sem("l1_out")
        l1_c = sem("l1_consts")

        def l1_scalar(act):
            act.sem_inc(e_ok, 2)
            act.sem_inc(ktc_ok, 2)

            def edges(t, b, n):
                act.wait_ge(run_ok, n + 1)
                act.sem_inc(gate, 1)
                act.activation(edge[b], no_edge[:, bass.ds(t, 1), :].rearrange("p a j -> p (a j)"), ACT.Copy,
                               scale=-1.0, bias=1.0).then_inc(e_ok, 1)
            with act.Fori(0, T // 2) as i:
                for b in range(2):
                    edges(i * 2 + b, b, i * 2 + b)
                for b in range(2):
                    n = i * 2 + b
                    act.wait_ge(kt_ok, n + 3)
                    act.wait_ge(agg_ok, n + 1)
                    act.activation(keepT[b].rearrange("p j i -> p (j i)"), tp(b, BF16), ACT.Copy
                                   ).then_inc(ktc_ok, 1)

        def l1_vector(dve):
            dve.memset(cap, float(NEIGHBORS)).then_inc(l1_c, 1)
            for b in range(2):
                dve.memset(run[b][:, 0:1], 0.0).then_inc(l1_c, 1)
            dve.wait_ge(l1_c, 3)
            dve.sem_inc(run_ok, 2)
            dve.sem_inc(l1_out, 1)
            with dve.Fori(0, T // 2) as i:
                def count(b):
                    n = i * 2 + b
                    dve.wait_ge(e_ok, n + 3)
                    dve.wait_ge(keep_ok, n + 1)
                    dve.tensor_tensor_scan(run[b][:, 1:N + 1], edge[b], cap, 0.0, ALU.add, ALU.min
                                           ).then_inc(run_ok, 1)
                    dve.wait_ge(run_ok, n + 3)
                count(0)
                count(1)
                for b in range(2):
                    n = i * 2 + b
                    total = run[b][:, N:N + 1]
                    x_i = xs[:, bass.ds(n, 1), :].rearrange("p a d -> p (a d)")
                    o = psum[:, 4 + b, 0:D]
                    v = i * 14 + b * 7
                    dve.wait_ge(l1_out, v + 1)
                    dve.tensor_scalar(tiny[:, 0:1], total, 1.0, None, ALU.max).then_inc(l1_out, 1)
                    dve.wait_ge(l1_out, v + 2)
                    dve.reciprocal(tiny[:, 1:2], tiny[:, 0:1]).then_inc(l1_out, 1)
                    dve.wait_ge(l1_out, v + 3)
                    dve.tensor_scalar(tiny[:, 2:3], tiny[:, 1:2], kG[:, WNB:WNB + 1], None, ALU.mult
                                      ).then_inc(l1_out, 1)
                    dve.tensor_scalar(tiny[:, 3:4], total, 1.0, None, ALU.min).then_inc(l1_out, 1)
                    dve.wait_ge(l1_out, v + 5)
                    dve.wait_ge(agg_ok, n + 3)
                    dve.scalar_tensor_tensor(z_t, o, tiny[:, 2:3], b_rows[:, 0], ALU.mult, ALU.add
                                             ).then_inc(l1_out, 1)
                    dve.wait_ge(l1_out, v + 6)
                    dve.scalar_tensor_tensor(z_t, z_t, 0.01, z_t, ALU.mult, ALU.max).then_inc(l1_out, 1)
                    dve.wait_ge(l1_out, v + 7)
                    dve.scalar_tensor_tensor(x_i, z_t, tiny[:, 3:4], x_i, ALU.mult, ALU.add).then_inc(l1_out, 1)

        def l1_pool(pool):
            pool.sem_inc(keep_ok, 2)
            with pool.Fori(0, T // 2) as i:
                for b in range(2):
                    n = i * 2 + b
                    pool.wait_ge(run_ok, n + 3)
                    pool.wait_ge(kt_ok, n + 1)
                    nc.gpsimd.tensor_tensor(keep[b], run[b][:, 1:N + 1], run[b][:, 0:N], ALU.subtract
                                            ).then_inc(keep_ok, 1)

        def l1_tensor(pe):
            pe.sem_inc(kt_ok, 2)
            pe.sem_inc(agg_ok, 2)
            with pe.Fori(0, T // 2) as i:
                for b in range(2):
                    n = i * 2 + b
                    pe.wait_ge(keep_ok, n + 3)
                    pe.wait_ge(ktc_ok, n + 1)
                    for j in range(T):
                        last = pe.transpose(tp(b, BF16)[:, P * j:P * j + P], keep[b][:, P * j:P * j + P], ident[:])
                    last.then_inc(kt_ok, 1)
                for b in range(2):
                    n = i * 2 + b
                    pe.wait_ge(ktc_ok, n + 3)
                    pe.wait_ge(l1_out, i * 14 + 1)
                    for j in range(T):
                        for hl in range(2):
                            last = pe.matmul(psum[:, 4 + b, 0:D], keepT[b][:, j], G[:, j, hl, 0:D],
                                             start=(j == 0 and hl == 0), stop=(j == T - 1 and hl == 1))
                    last.then_inc(agg_ok, 1)

        s2_b = at(A_UB, [N], F32)
        a_b = at(A_R3, [N], F32)
        b_b = at(A_R3 + 8192, [N], F32)
        colsum = at(A_XB, [D + 2], F32)
        mneg = [at(A_F + 4096 * b, [N], BF16) for b in range(2)]
        mjunk = at(A_F + 8192, [N], F32)
        mxcol, s2fifth, empty = nsq, r2, nbias
        spread_s2, spread_a, spread_b = Spread("l2_s2"), Spread("l2_a"), Spread("l2_b")
        mneg_ok, mx_ok, l2p, cs_ok, csk_ok = (sem("l2_mneg"), sem("l2_max"), sem("l2_cols"), sem("l2_colsum"),
                                              sem("l2_colsum_kept"))

        def l2_pre_vector(dve):
            spread_s2.vector(dve, lambda i: s12[:, i, 1:2])
            dve.wait_ge(spread_s2.kept, C)
            for t in range(T):
                dve.wait_ge(mneg_ok, t + 1)
                if t:
                    dve.wait_ge(mx_ok, t)
                dve.tensor_tensor_reduce(mjunk, mneg[t % 2], s2_b, 1.0, 2 * NEG, ALU.add, ALU.max,
                                         mxcol[:, t:t + 1]).then_inc(mx_ok, 1)
            dve.wait_ge(mx_ok, T)
            count = [0]

            def step(ins):
                count[0] += 1
                ins.then_inc(l2p, 1)
                dve.wait_ge(l2p, count[0])
            s1 = s12[:, :, 0]
            step(dve.tensor_tensor(acol, s1, mxcol, ALU.add))
            step(dve.scalar_tensor_tensor(bcol, acol, 0.2, acol, ALU.mult, ALU.max))
            step(dve.tensor_tensor(acol, s1, bcol, ALU.subtract))
            step(dve.scalar_tensor_tensor(bcol, s1, 0.2, bcol, ALU.mult, ALU.subtract))
            step(dve.tensor_scalar(empty, mxcol, 0.5 * NEG, None, ALU.is_lt))
            step(dve.tensor_scalar(s2fifth, s12[:, :, 1], 0.2, None, ALU.mult))
            spread_a.vector(dve, lambda i: acol[:, i:i + 1])
            dve.wait_ge(spread_a.out, C)
            dve.wait_ge(spread_a.kept, C)
            spread_b.vector(dve, lambda i: bcol[:, i:i + 1])

        def l2_pre_tensor(pe):
            spread_s2.tensor(pe)
            pe.wait_ge(spread_s2.kept, C)
            for j in range(T):
                for hl in range(2):
                    last = pe.matmul(psum[:, 0, 0:D + 1], ones16[:], G[:, j, hl, 0:D + 1],
                                     start=(j == 0 and hl == 0), stop=(j == T - 1 and hl == 1))
            last.then_inc(cs_ok, 1)
            spread_a.tensor(pe)
            pe.wait_ge(spread_a.kept, C)
            spread_b.tensor(pe)

        def l2_pre_scalar(act):
            spread_s2.scalar(act, s2_b)
            for t in range(T):
                if t >= 2:
                    act.wait_ge(mx_ok, t - 1)
                act.activation(mneg[t % 2], no_edge[:, t], ACT.Copy, scale=NEG).then_inc(mneg_ok, 1)
            act.wait_ge(cs_ok, 1)
            act.activation(colsum[:, 0:D + 1], psum[:, 0, 0:D + 1], ACT.Copy).then_inc(csk_ok, 1)
            spread_a.scalar(act, a_b)
            spread_b.scalar(act, b_b)

        A2 = Attention("l2")

        def l2_tensor(pe):
            pe.sem_inc(A2.summed, 3)
            with pe.Fori(0, C) as c:
                for j in range(T):
                    av_step(pe, A2, c, j)

        def l2_scalar(act):
            A = A2
            for s in (A.den, A.num, A.hi):
                act.sem_inc(s, 3)
            with act.Fori(0, C) as c:
                def fifth(j):
                    act.wait_ge(A.rec, c * T + j + 2)
                    act.sem_inc(gate, 1)
                    act.activation(den[j % 2], b_b[:, bass.ds(c * CH, CH)], ACT.Identity, bias=s2fifth[:, j:j + 1]
                                   ).then_inc(A.den, 1)
                fifth(0)
                fifth(1)
                for j in range(T):
                    n = c * T + j
                    act.wait_ge(A.sim, n + 4)
                    act.wait_ge(A.lo, n + 2)
                    act.activation(num[j % 2], sim[j % 2], ACT.Exp).then_inc(A.num, 1)
                    act.wait_ge(A.num, n + 4)
                    act.wait_ge(A.summed, n + 1)
                    act.activation(num_hl[j % 3][:, 0], num[j % 2], ACT.Copy, scale=E_UP).then_inc(A.hi, 1)
                    if j + 2 < T:
                        fifth(j + 2)
                for t in range(TC):
                    act.wait_ge(A.ep, c * 7 * TC + t * 7 + 7)
                    act.activation(el_tmp3, el_tmp2, ACT.Exp).then_inc(A.ep_a, 1)

        def l2_vector(dve):
            A = A2
            for s in (A.rec, A.sim, A.lo):
                dve.sem_inc(s, 3)
            dve.sem_inc(A.taken, 1)
            dve.sem_inc(A.ep, 2)
            with dve.Fori(0, C) as c:
                def lo_(j):
                    n = c * T + j
                    dve.wait_ge(A.hi, n + 4)
                    dve.scalar_tensor_tensor(num_hl[j % 3][:, 1], num[j % 2], E_UP, num_hl[j % 3][:, 0], ALU.mult,
                                             ALU.subtract).then_inc(A.lo, 1)
                for j in range(T):
                    n = c * T + j
                    dve.wait_ge(A.den, n + 4)
                    dve.wait_ge(A.num, n + 2)
                    dve.scalar_tensor_tensor(sim[j % 2], a_b[:, bass.ds(c * CH, CH)], s12[:, j, 1:2], den[j % 2],
                                             ALU.add, ALU.max).then_inc(A.rec, 1)
                    dve.wait_ge(A.rec, n + 4)
                    dve.tensor_tensor(sim[j % 2], sim[j % 2],
                                      no_edge_T[:, j, bass.ds(c * CH, CH)], ALU.add
                                      ).then_inc(A.sim, 1)
                    if j >= 1:
                        lo_(j - 1)
                lo_(T - 1)
                dve.wait_ge(A.summed, c * T + T + 3)
                for t in range(TC):
                    o = psum[:, t, 0:D + 1]
                    k0 = c * 7 * TC + t * 7 + 2
                    i = c * TC + t
                    dve.wait_ge(A.ep, k0)
                    dve.scalar_tensor_tensor(el_tmp[:, 0:D + 1], colsum[:, 0:D + 1], empty[:, bass.ds(i, 1)], o,
                                             ALU.mult, ALU.add).then_inc(A.ep, 1)
                    dve.wait_ge(A.ep, k0 + 1)
                    dve.reciprocal(tiny[:, 0:1], el_tmp[:, D:D + 1]).then_inc(A.ep, 1)
                    dve.wait_ge(A.ep, k0 + 2)
                    dve.tensor_scalar(tiny[:, 1:2], tiny[:, 0:1], kG[:, W2:W2 + 1], None, ALU.mult).then_inc(A.ep, 1)
                    dve.wait_ge(A.ep, k0 + 3)
                    dve.tensor_scalar(el_tmp[:, 0:D], el_tmp[:, 0:D], tiny[:, 1:2], None, ALU.mult
                                      ).then_inc(A.ep, 1)
                    dve.wait_ge(A.ep, k0 + 4)
                    dve.tensor_scalar(el_tmp2, el_tmp[:, 0:D], 0.0, None, ALU.min).then_inc(A.ep, 1)
                    dve.wait_ge(A.ep, k0 + 5)
                    dve.scalar_tensor_tensor(el_tmp[:, 0:D], el_tmp[:, 0:D], 0.0, xs[:, bass.ds(i, 1), :].rearrange(
                        "p a d -> p (a d)"), ALU.max, ALU.add).then_inc(A.ep, 1)
                    dve.wait_ge(A.ep, k0 + 6)
                    dve.wait_ge(A.ep_a, i + 1)
                    dve.scalar_tensor_tensor(xs[:, bass.ds(i, 1), :].rearrange("p a d -> p (a d)"), el_tmp3, -1.0,
                                             el_tmp[:, 0:D], ALU.add, ALU.add).then_inc(A.ep, 1)
                dve.wait_ge(A.ep, c * 7 * TC + 7 * TC + 2)
                dve.sem_inc(A.taken, 1)

        q_c = at(A_SG, [K, 2, N], F16)
        k_c = at(A_SG + 16384, [K, 2, N], F16)
        q4 = at(A_R3, [H, N], F16)
        k4 = at(A_K4, [H, N], F16)
        q_lin = sem("f3_qk_linear")
        vf = zline

        def l3_linear(pe, g):
            f = fronts[3]
            if g >= 1:
                pe.wait_ge(f.post_a, 3 * g)
            for w, bank in ((wsq, 4), (wsk, 6)):
                for d in range(K):
                    last = product(pe, psum[:, bank + d, :], lambda hl, k: w[:, hl, k, P * d:P * d + P],
                                   lambda hl, k: hT[g % 2][:, hl, k])
            last.then_inc(q_lin, 1)
            pe.wait_ge(f.post_a, 3 * g + 1)
            for t in range(TC):
                last = product(pe, psum[:, 4 + t // 2, D * (t % 2):D * (t % 2) + D],
                               lambda hl, k: hT[g % 2][:, hl, k, P * t:P * t + P], lambda hl, k: wsv[:, hl, k])
            return last

        def l3_post_act(act, g):
            f = fronts[3]
            act.wait_ge(q_lin, g + 1)
            if g >= 1:
                act.wait_ge(f.post_v, 6 * g)
            act.activation(gfb[0].rearrange("p t d -> p (t d)"), psum[:, 4:6, :].rearrange("p a b -> p (a b)"),
                           ACT.Copy, scale=G_DOWN).then_inc(f.post_a, 1)
            act.activation(gfb[1].rearrange("p t d -> p (t d)"), psum[:, 6:8, :].rearrange("p a b -> p (a b)"),
                           ACT.Identity, scale=sc[:, 5:6], bias=wec[:, 0:1]).then_inc(f.post_a, 1)
            act.wait_ge(f.lin_ok, g + 1)
            act.activation(vf.rearrange("p t d -> p (t d)"), psum[:, 4:6, :].rearrange("p a b -> p (a b)"),
                           ACT.Copy, scale=G_DOWN).then_inc(f.post_a, 1)

        def l3_post_dve(dve, g):
            f = fronts[3]
            r = TC * g
            for i, (src, dst) in enumerate((
                    (gfb[0].rearrange("p t d -> p (t d)").rearrange("p (a b) -> p a b", a=K),
                     lambda hl: q_c[:, :, hl, CH * g:CH * g + CH]),
                    (gfb[1].rearrange("p t d -> p (t d)").rearrange("p (a b) -> p a b", a=K),
                     lambda hl: k_c[:, :, hl, CH * g:CH * g + CH]),
                    (vf, lambda hl: G[:, r:r + TC, hl, 0:D]))):
                dve.wait_ge(f.post_a, 3 * g + i + 1)
                dve.tensor_copy(dst(0), src).then_inc(f.post_v, 1)
                dve.wait_ge(f.post_v, 6 * g + 2 * i + 1)
                dve.tensor_tensor(dst(1), src, dst(0), ALU.subtract).then_inc(f.post_v, 1)

        x_save = nc.dram_tensor("x_save", (N, D), F32, kind="Internal").ap().rearrange("(t p) d -> p t d", p=P)
        lay_ld, xs_ld = sem("l3_rows_laid"), sem("l3_x_saved")

        def l3_lay_sync(sp):
            for h in range(H):
                for r in range(4):
                    sp.dma_start(k4[DH * r:DH * r + DH, h, :], k_c[DH * (h % 4):DH * (h % 4) + DH, h // 4, r % 2, :]
                                 ).then_inc(lay_ld, 16)
            sp.dma_start(x_save, xs).then_inc(xs_ld, 16)
            sp.wait_ge(xs_ld, 16)

        def l3_lay_scalar(act):
            for h in range(H):
                for r in range(4):
                    act.dma_start(q4[DH * r:DH * r + DH, h, :], q_c[DH * (h % 4):DH * (h % 4) + DH, h // 4, r // 2, :]
                                  ).then_inc(lay_ld, 16)
            act.wait_ge(lay_ld, 16 * 8 * H)

        HB = 2 * CH
        m3 = [at(A_F + 8192 * b, [N], F32) for b in range(2)]
        hb = [at(A_F + 16384 + 4096 * b, [T, P], U16) for b in range(2)]
        ms = [at(A_X + 8192 * b, [N], F32) for b in range(2)]
        bits = at(A_W, [N], U16)
        m3_tmp = at(A_W + 4096, [N], BF16)
        x_in = [at(A_W + 8192 + 1024 * b, [D], F32) for b in range(2)]
        res = [at(A_W + 10240 + 1024 * b, [D], F32) for b in range(2)]
        o_hi = at(A_W + 12288, [D], F32)
        picks = [at(A_SG + 16384 * b, [H, N], F8) for b in range(2)]
        names = ("scores", "row_max", "threshold", "picks", "packed", "bits", "unpacked", "values", "out_hi", "out",
                 "mask", "mask_tmp")
        sc_ok, tt_ok, th_ok, sg_ok, pk_ok, pe_ok, up_ok, av_ok, oa_ok, od_ok, m3_ok, m3t_ok = (
            sem("l3_" + n) for n in names)
        xt_ld, st_ok = [sem("l3_x0"), sem("l3_x1")], [sem("l3_stored0"), sem("l3_stored1")]
        gate_v, gate_t, gate_p = sem("dve_gate"), sem("pe_gate"), sem("pool_gate")
        OFF = (0, 1)

        def need(eng, s, v):
            if not isinstance(v, int) or v > 0:
                eng.wait_ge(s, v)

        def steps(eng, step):
            step(0, 0, 0)
            step(1, 0, 1)
            with eng.Fori(1, T // 2) as i:
                step(i * 2, i, 0)
                step(i * 2 + 1, i, 1)
            step(T, T // 2, 0)
            step(T + 1, T // 2, 1)

        def has(n, delay):
            return not isinstance(n, int) or 0 <= n - delay < T

        def l3_tensor(pe):
            def step(n, k, par):
                def scores(h):
                    for q in range(2):
                        s = 2 * h + q
                        buf = (s + OFF[par]) % 3
                        if s >= 3:
                            need(pe, tt_ok, n * 16 + s - 2)
                        else:
                            old = max(o for o in range(13, 16) if (o + OFF[1 - par]) % 3 == buf)
                            need(pe, tt_ok, n * 16 + old - 15)
                        for c in range(2):
                            last = pe.matmul(psum[:, 2 * buf + c, :], q4[:, h, bass.ds(n * P, P)],
                                             k4[:, h, HB * q + CH * c:HB * q + CH * c + CH], start=True, stop=True)
                        last.then_inc(sc_ok, 1)

                def pack(g):
                    need(pe, sg_ok, n * 8)
                    need(pe, pe_ok, n * 4 - 4 + g)
                    pe.sem_inc(gate_t, 1)
                    for kb in range(4):
                        for h in range(H):
                            j = 4 * g + kb
                            last = pe.matmul(psum[:, 6, P * kb:P * kb + P], picks[1 - par][:, h, P * j:P * j + P],
                                             head_bit[:, h], start=(h == 0), stop=(h == H - 1))
                    last.then_inc(pk_ok, 1)

                def values(d, h):
                    need(pe, up_ok, n * 8 - 8 * d + h + 1)
                    if h == 0:
                        need(pe, od_ok, n * 2 - 2 * d + 4)
                    for j in range(T):
                        last = pe.matmul(psum[:, 7, 64 * h:64 * h + 64], hb[h % 2][:, j].bitcast(F16),
                                         G[:, j, :, DH * h:DH * h + DH], start=(j == 0), stop=(j == T - 1))
                    last.then_inc(av_ok, 1)

                for h in range(H):
                    if has(n, 0):
                        scores(h)
                    if h == 0 and has(n, 2):
                        values(2, 6)
                        values(2, 7)
                    if has(n, 1):
                        if 1 <= h <= 4:
                            pack(h - 1)
                        if h >= 5:
                            values(1, 2 * (h - 5))
                            values(1, 2 * (h - 5) + 1)
            pe.wait_ge(lay_ld, 16 * 8 * H)
            steps(pe, step)

        def l3_vector(dve):
            def step(n, k, par):
                def row_max(h):
                    for q in range(2):
                        s = 2 * h + q
                        buf = (s + OFF[par]) % 3
                        need(dve, sc_ok, n * 16 + s + 1)
                        if q == 0:
                            need(dve, sg_ok, n * 8 + h - 1)
                        if s == 0:
                            need(dve, m3_ok, n + 1)
                        need(dve, tt_ok, n * 16 + s)
                        dve.sem_inc(gate_v, 1)
                        part = slice(HB * q, HB * q + HB)
                        dve.tensor_tensor_reduce(ms[h % 2][:, part],
                                                 psum[:, 2 * buf:2 * buf + 2, :].rearrange("p a b -> p (a b)"),
                                                 m3[par][:, part], 1.0, 2 * NEG if q == 0 else tiny[:, h % 2:h % 2 + 1],
                                                 ALU.add, ALU.max, tiny[:, 2 * q + h % 2:2 * q + h % 2 + 1]
                                                 ).then_inc(tt_ok, 1)
                    need(dve, tt_ok, n * 16 + 2 * h + 2)
                    dve.tensor_scalar(tiny[:, 4 + h % 2:5 + h % 2], tiny[:, 2 + h % 2:3 + h % 2], 0.5 * NEG, -1.0,
                                      ALU.max, ALU.mult).then_inc(th_ok, 1)

                def unpack(h):
                    need(dve, pe_ok, n * 4)
                    need(dve, av_ok, n * 8 - 8 + h - 1)
                    dve.tensor_scalar(hb[h % 2].rearrange("p j i -> p (j i)"), bits, 14 - h, 0x4000,
                                      ALU.logical_shift_left, ALU.bitwise_and).then_inc(up_ok, 1)

                def take():
                    need(dve, oa_ok, n - 1)
                    lo = psum[:, 7, :].rearrange("p (h a d) -> p h a d", h=H, a=2)[:, :, 1, :]
                    dve.scalar_tensor_tensor(o_hi.rearrange("p (h d) -> p h d", h=H), lo, sc[:, 6:7],
                                             o_hi.rearrange("p (h d) -> p h d", h=H), ALU.mult, ALU.add
                                             ).then_inc(od_ok, 1)
                    need(dve, od_ok, n * 2 - 4 + 5)
                    need(dve, xt_ld[par], k * 16)
                    need(dve, st_ok[par], k * 16)
                    dve.tensor_tensor(res[par], o_hi, x_in[par], ALU.add).then_inc(od_ok, 1)

                for h in range(H):
                    if has(n, 0):
                        row_max(h)
                    if h == 1 and has(n, 2):
                        take()
                    if h >= 4 and has(n, 1):
                        unpack(2 * (h - 4))
                        unpack(2 * (h - 4) + 1)
            dve.tensor_scalar(sc[:, 6:7], kG[:, WV:WV + 1], 1.0 / 16, None, ALU.mult).then_inc(l3c, 1)
            dve.wait_ge(l3c, 1)
            dve.sem_inc(od_ok, 4)
            steps(dve, step)

        l3c = sem("l3_const")

        def l3_scalar(act):
            def step(n, k, par):
                def sign(h):
                    need(act, th_ok, n * 8 + h + 1)
                    if h == 0:
                        need(act, pk_ok, n * 4 - 4)
                    act.sem_inc(gate, 1)
                    act.activation(picks[par][:, h], ms[h % 2], ACT.Sign, bias=tiny[:, 4 + h % 2:5 + h % 2],
                                   saturate=False                                   ).then_inc(sg_ok, 1)

                def to_bits(g):
                    need(act, pk_ok, n * 4 - 4 + g + 1)
                    need(act, up_ok, n * 8 - 8)
                    act.activation(bits[:, CH * g:CH * g + CH], psum[:, 6, :], ACT.Copy, bias=float(2 ** H - 1)
                                   ).then_inc(pe_ok, 1)

                for h in range(H):
                    if 1 <= h <= 4 and has(n, 1):
                        to_bits(h - 1)
                    if has(n, 0):
                        sign(h)
                    if h == 1 and has(n, 2):
                        need(act, av_ok, n * 8 - 8)
                        need(act, od_ok, n * 2 - 4 + 4)
                        hi = psum[:, 7, :].rearrange("p (h a d) -> p h a d", h=H, a=2)[:, :, 0, :]
                        act.activation(o_hi.rearrange("p (h d) -> p h d", h=H), hi, ACT.Identity, scale=sc[:, 6:7]
                                       ).then_inc(oa_ok, 1)
            act.wait_ge(l3c, 1)
            steps(act, step)

        def l3_pool(pool):
            def mask(n, par):
                need(pool, tt_ok, n * 16 - 16)
                need(pool, m3_ok, n)
                nc.gpsimd.tensor_copy(m3_tmp, no_edge[:, bass.ds(n, 1), :].rearrange("p a j -> p (a j)")
                                      ).then_inc(m3t_ok, 1)
                need(pool, m3t_ok, n + 1)
                pool.sem_inc(gate_p, 1)
                nc.gpsimd.tensor_scalar(m3[par], m3_tmp, NEG, bec[:, 0:1], ALU.mult, ALU.add).then_inc(m3_ok, 1)
            mask(0, 0)
            mask(1, 1)
            with pool.Fori(1, T // 2) as i:
                mask(i * 2, 0)
                mask(i * 2 + 1, 1)

        def l3_sync(sp):
            for s in st_ok:
                sp.sem_inc(s, 16)
            with sp.Fori(0, T // 2) as i:
                for par in range(2):
                    n = i * 2 + par
                    sp.wait_ge(od_ok, n * 2 + 2)
                    sp.dma_start(x_in[par], x_save[:, bass.ds(n, 1), :]).then_inc(xt_ld[par], 16)
                    sp.wait_ge(od_ok, n * 2 + 6)
                    sp.dma_start(out_t[:, bass.ds(n, 1), :], res[par]).then_inc(st_ok[par], 16)
            for s in st_ok:
                sp.wait_ge(s, 16 + 16 * (T // 2))

        fronts = {}

        def new_front(i, name, copies, adds_to_x, w, n, pa, pv, linear=None):
            f = Front(name)
            f.copies, f.adds_to_x = copies, adds_to_x
            f.post_act, f.post_dve = pa, pv
            f.linear = linear or linear_rows(w, n, lambda: fronts[i])
            fronts[i] = f

        new_front(0, "f0", 1, 0, ws0, D, l0_post_act, l0_post_dve)
        new_front(1, "f1", 1, 8, ws1, 2 * D, split_post_act(1), split_post_dve(1))
        new_front(2, "f2", 2, 0, ws2, D + 2, split_post_act(2), split_post_dve(2))
        new_front(3, "f3", 3, 0, None, 0, l3_post_act, l3_post_dve, l3_linear)
        fronts[1].per_v, fronts[2].per_v = 8, 2

        block = ctx.enter_context(nc.Block())

        def finish_sync(sp):
            sp.dma_start(out_t, xs).then_inc(x_ld, 16)
            sp.wait_ge(x_ld, 32)

        def restore_vector(dve):
            dve.wait_ge(dg, 2 * T + 1)
            with dve.Fori(0, T) as i:
                dve.tensor_scalar(no_edge_T_flat[:, bass.ds(i * (N + P), P)], diag_save[:, bass.ds(i, 1), :], NEG, None,
                                  ALU.mult).then_inc(dg, 1)

        def front_stage(i):
            return dict(vector=fronts[i].vector, scalar=fronts[i].scalar, tensor=fronts[i].tensor)

        stages = [
            dict(sync=load_sync, pool=load_pool, vector=load_vector, scalar=load_scalar, tensor=load_tensor),
            front_stage(0),
            dict(vector=l0_unit_vector, scalar=l0_unit_scalar, tensor=l0_unit_tensor),
            dict(vector=l0_vector, scalar=l0_scalar, tensor=l0_tensor),
            dict(sync=l1_load, vector=lambda e: (restore_vector(e), fronts[1].vector(e)), scalar=fronts[1].scalar,
                 tensor=fronts[1].tensor),
            dict(pool=l1_pool, vector=l1_vector, scalar=l1_scalar, tensor=l1_tensor),
            front_stage(2),
            dict(vector=l2_pre_vector, scalar=l2_pre_scalar, tensor=l2_pre_tensor),
            dict(vector=l2_vector, scalar=l2_scalar, tensor=l2_tensor),
            front_stage(3),
            dict(sync=l3_lay_sync, scalar=l3_lay_scalar),
            dict(sync=l3_sync, pool=l3_pool, vector=l3_vector, scalar=l3_scalar, tensor=l3_tensor),
        ]
        if stop:
            stages = stages[:stop]

        def run_stages(eng, name):
            for k, s in enumerate(stages):
                if name in s:
                    s[name](eng)
                stage_end(eng, k + 1)

        @block.sync
        def _(sp):
            run_stages(sp, "sync")
            if stop:
                finish_sync(sp)

        @block.gpsimd
        def _(pool):
            run_stages(pool, "pool")

        @block.vector
        def _(dve):
            run_stages(dve, "vector")

        @block.scalar
        def _(act):
            run_stages(act, "scalar")

        @block.tensor
        def _(pe):
            run_stages(pe, "tensor")


def kernel(**inputs):
    import numpy as np
    import concourse.bacc as bacc
    from concourse.bass_utils import run_bass_kernel_spmd

    nc = bacc.Bacc("TRN2", target_bir_lowering=False, num_devices=1)
    arrays = {}

    def given(name, array):
        arrays[name] = np.ascontiguousarray(array)
        return nc.dram_tensor(name, array.shape, mybir.dt.from_np(array.dtype), kind="ExternalInput").ap()

    g = {k: np.asarray(v) for k, v in inputs.items()}
    x, adj = given("x", g["x"]), given("adj", g["adj"])
    weights = [given("w0_T", g["L0_gnn_W"].T), given("w_nb_T", g["L1_gnn_W_nb"].T),
               given("w_line_T", g["L1_gnn_W_line"].T), given("w2", g["L2_gnn_W"]),
               given("wq_T", g["L3_gnn_WQ"].T), given("wk_T", g["L3_gnn_WK"].T), given("wv_T", g["L3_gnn_WV"].T)]
    attn, b_nb, b_line = given("attn", g["L2_gnn_attn"]), given("b_nb", g["L1_gnn_b_nb"]), given("b_line", g["L1_gnn_b_line"])
    we, be = given("we", g["L3_gnn_we"]), given("be", g["L3_gnn_be"])
    out = nc.dram_tensor("out", (N, D), F32, kind="ExternalOutput").ap()
    adjacency_net(nc, x, adj, weights, attn, b_nb, b_line, we, be, out, 0)
    r = run_bass_kernel_spmd(nc, [arrays], core_ids=[0])
    return r.results[0]["out"]
```

```python
from contextlib import ExitStack

import numpy as np

import concourse.bass as bass
from concourse import mybir

ALU = mybir.AluOpType
ACT = mybir.ActivationFunctionType
F32 = mybir.dt.float32
F16 = mybir.dt.float16
BF16 = mybir.dt.bfloat16
F8 = mybir.dt.float8e4
U8 = mybir.dt.uint8
U16 = mybir.dt.uint16
I32 = mybir.dt.int32
U32 = mybir.dt.uint32
AX_X = mybir.AxisListType.X
ABSMAX = bass.bass_isa.ReduceOp.absmax

P = 128
N, D, H = 2048, 256, 8
DH = D // H
T = N // P
K = D // P
CH = 512
C = N // CH
TC = CH // P
NEIGHBORS = 64
EPS = 1e-5
L0_EPS = 1e-8
NEG = -(2.0 ** 120)
SCALING = float(DH) ** -0.5

H_UP = 2.0 ** 11
W_UP = 2.0 ** 13
G_DOWN = 2.0 ** -18
UNIT_UP = 2.0 ** 13
E_UP = 2.0 ** 14
UNIT_DOWN = 0.5 / UNIT_UP ** 2
ABOVE_ONE = 1.0 + 2.0 ** -23
TINY = 2.0 ** -40
LN2 = float(np.log(2.0))

W0, WNB, WLINE, W2, WQ, WK, WV, WS, WE = range(9)

A_M = 0
A_MT = A_M + T * N
A_SG, A_K4 = A_MT, A_MT + 2 * H * N
A_G = A_MT + 2 * T * N
A_R3 = A_G + T * 2 * (D + 2) * 2
A_UB = A_R3 + 2 * K * N * 2
A_XB = A_UB + 4 * N
A_F = A_XB + 4 * N
A_X = A_F + 24576
A_W = A_X + T * D * 4
A_D = A_W + 16384
A_END = A_D + 2048


def adjacency_net(nc, x, adj, weights, attn, b_nb, b_line, we, be, out, stop):
    with ExitStack() as ctx:
        def sb(name, shape, dt):
            return ctx.enter_context(nc.sbuf_tensor(name, shape, dt))

        def sem(name):
            return ctx.enter_context(nc.semaphore(name))

        arena = sb("arena", [P, A_END], U8)
        SIZE = {F32: 4, F16: 2, BF16: 2, F8: 1, U8: 1, U16: 2, I32: 4, U32: 4}

        def at(offset, shape, dt):
            n = SIZE[dt]
            for s in shape:
                n *= s
            a = arena[:, offset:offset + n]
            if dt is not U8:
                a = a.bitcast(dt)
            if len(shape) == 2:
                a = a.rearrange("p (a b) -> p a b", a=shape[0])
            if len(shape) == 3:
                a = a.rearrange("p (a b c) -> p a b c", a=shape[0], b=shape[1])
            if len(shape) == 4:
                a = a.rearrange("p (a b c d) -> p a b c d", a=shape[0], b=shape[1], c=shape[2])
            return a

        no_edge = at(A_M, [T, N], U8)
        no_edge_T = at(A_MT, [T, N], BF16)
        diag_blocks = at(A_MT, [T, N + P], BF16)[:, :, 0:P]
        G = at(A_G, [T, 2, D + 2], F16)
        xs = at(A_X, [T, D], F32)
        ws0 = at(A_W, [2, K, D], F16)
        ws1 = at(A_W + 2048, [2, K, 2 * D], F16)
        ws2 = at(A_W + 6144, [2, K, D + 2], F16)
        wsq = at(A_W + 8208, [2, K, D], F16)
        wsk = at(A_W + 10256, [2, K, D], F16)
        wsv = at(A_W + 12304, [2, K, D], F16)
        h32 = [at(A_F + 4096 * b, [TC, D], F32) for b in range(2)]
        hn = [at(A_F + 8192 + 4096 * b, [2, TC, D], F16) for b in range(2)]
        hT = [at(A_F + 16384 + 4096 * b, [2, K, CH], F16) for b in range(2)]

        ident = sb("ident", [P, P], BF16)
        ident16 = sb("ident16", [P, P], F16)
        ident32 = sb("ident32", [P, P], F32)
        off_diag = sb("off_diag", [P, P], BF16)
        ones32 = sb("ones32", [P, P], F32)
        ones16 = sb("ones16", [P, P], F16)
        head_bit = sb("head_bit", [P, H, P], BF16)
        wsc = sb("wsc", [P, 6, 9], F32)
        sc = sb("sc", [P, 8], F32)
        w12 = sb("w12", [P, K, 2], F32)
        wec = sb("wec", [P, 1], F32)
        bec = sb("bec", [P, 1], F32)
        st6 = sb("st6", [P, T, 6], F32)
        mv = sb("mv", [P, T, 2], F32)
        cols = sb("cols", [P, 8, T], F32)
        s12 = sb("s12", [P, T, 2], F32)
        tiny = sb("tiny", [P, 16], F32)
        wmax, wpow, wup, kG, kL, kI = (wsc[:, i, :] for i in range(6))
        veps, std, r2, nbias, nsq, ucol, acol, bcol = (cols[:, i, :] for i in range(8))

        psum = ctx.enter_context(nc.psum_tensor("psum", [P, 8, CH], F32))

        def tp(b, dt=F16):
            return psum[:, 2 * b:2 * b + 2, :].rearrange("p a b -> p (a b)").bitcast(dt)

        x_t = x.rearrange("(t p) d -> p t d", p=P)
        out_t = out.rearrange("(t p) d -> p t d", p=P)
        adj_t = adj.rearrange("(t p) j -> p t j", p=P)

        barrier_sem = sem("stage_done")

        def stage_end(eng, k):
            eng.drain().then_inc(barrier_sem, 1)
            eng.wait_ge(barrier_sem, 5 * k)

        wraw = at(A_F, [7, K, D], F32)
        ab = at(A_F + 14336, [2, D], F32)
        wtmp = at(A_F + 16384, [2 * D], F32)
        adjb = [at(o, [N], I32) for o in (A_UB, A_XB, A_R3 + 8192, A_G)]
        bb = [at(A_R3 + 4096 * b, [N], BF16) for b in range(2)]
        diag_save = at(A_D, [T, P], U8)

        w_ld, x_ld = sem("weights_loaded"), sem("x_loaded")
        adj_ld = [sem(f"adj_loaded{b}") for b in range(4)]
        consts_ok, wmax_ok, wall_ok = sem("consts_ok"), sem("weight_max"), sem("weight_max_all")
        bb_ok, m_ok, tp_ok, mt_ok = sem("mask_tile"), [sem("mask_kept_even"), sem("mask_kept_odd")], sem("mask_turned"), sem("mask_T_kept")
        wp = sem("weight_prep")
        dg = sem("diagonal")
        gate, gate_pool = sem("act_gate"), sem("pool_gate")

        def load_sync(sp):
            with sp.Fori(0, T // 4) as i:
                for b in range(4):
                    sp.wait_ge(bb_ok, i * 4 + b + 1)
                    sp.dma_start(adjb[b], adj_t[:, bass.ds(i * 4 + b, 1), :]).then_inc(adj_ld[b], 16)
            sp.dma_start(xs, x_t).then_inc(x_ld, 16)

        def load_weights(eng):
            for i, w in enumerate(weights):
                eng.dma_start(wraw[:, i], w.rearrange("(k p) o -> p k o", p=P)).then_inc(w_ld, 16)
            a = attn.rearrange("(a d) o -> (o a) d", a=2)
            for i in range(2):
                eng.dma_start(ab[:, i], a[i].partition_broadcast(P)).then_inc(w_ld, 16)
            for i in range(4):
                eng.dma_start(wec[DH * i:DH * i + DH, :], we.rearrange("o d -> d o")).then_inc(w_ld, 16)
            eng.dma_start(bec[:], be.partition_broadcast(P)).then_inc(w_ld, 16)

        def keep_tile(eng, copy, i, b):
            n = i * 4 + b
            eng.wait_ge(bb_ok, n + 5)
            eng.sem_inc(gate if b % 2 == 0 else gate_pool, 1)
            copy(no_edge[:, bass.ds(n, 1), :].rearrange("p a j -> p (a j)"), bb[b % 2]).then_inc(m_ok[b % 2], 1)

        def load_pool(pool):
            nc.gpsimd.memset(ones32[:], 1.0).then_inc(consts_ok, 1)
            pool.wait_ge(consts_ok, 1)
            nc.gpsimd.affine_select(out=ident32[:], in_=ones32[:], pattern=[[-1, P]], compare_op=ALU.is_equal,
                                    fill=0.0, base=0, channel_multiplier=1).then_inc(consts_ok, 1)
            pool.wait_ge(consts_ok, 2)
            nc.gpsimd.tensor_copy(ident[:], ident32[:]).then_inc(consts_ok, 1)
            nc.gpsimd.tensor_copy(ident16[:], ident32[:]).then_inc(consts_ok, 1)
            nc.gpsimd.tensor_copy(ones16[:], ones32[:]).then_inc(consts_ok, 1)
            nc.gpsimd.tensor_scalar(off_diag[:], ident32[:], -1.0, 1.0, ALU.mult, ALU.add).then_inc(consts_ok, 1)
            for h in range(H):
                nc.gpsimd.tensor_scalar(head_bit[:, h], ident32[:], 2.0 ** h, 0.0, ALU.mult, ALU.add
                                        ).then_inc(consts_ok, 1)
            pool.wait_ge(wmax_ok, 1)
            nc.gpsimd.partition_all_reduce(wsc[:, 1, :], wsc[:, 0, :], P, ABSMAX).then_inc(wall_ok, 1)
            pool.sem_inc(m_ok[1], 1)
            with pool.Fori(0, T // 4) as i:
                for b in (1, 3):
                    keep_tile(pool, nc.gpsimd.tensor_copy, i, b)

        def load_tensor(pe):
            pe.wait_ge(consts_ok, 3)
            pe.sem_inc(tp_ok, 2)
            with pe.Fori(0, T // 2) as i:
                for b in range(2):
                    pe.wait_ge(bb_ok, i * 2 + b + 5)
                    pe.wait_ge(mt_ok, i * 2 + b + 1)
                    for j in range(T):
                        last = pe.transpose(tp(b, BF16)[:, P * j:P * j + P], bb[b][:, P * j:P * j + P], ident[:])
                    last.then_inc(tp_ok, 1)

        def load_scalar(act):
            load_weights(act)
            act.sem_inc(mt_ok, 2)
            act.sem_inc(m_ok[0], 1)

            def copy(dst, src):
                return act.activation(dst, src, ACT.Copy)
            with act.Fori(0, T // 4) as i:
                for b in range(4):
                    if b % 2 == 0:
                        keep_tile(act, copy, i, b)
                    act.wait_ge(tp_ok, i * 4 + b + 3)
                    act.sem_inc(gate, 1)
                    act.activation(no_edge_T[:, :, bass.ds(i * 512 + b * P, P)],
                                   tp(b % 2, BF16).rearrange("p (j i) -> p j i", j=T), ACT.Copy, scale=NEG
                                   ).then_inc(mt_ok, 1)

        def load_vector(dve):
            count = [0]

            def step(ins):
                count[0] += 1
                ins.then_inc(wp, 1)
                dve.wait_ge(wp, count[0])

            dve.wait_ge(w_ld, 16 * 14)
            step(dve.tensor_reduce(wmax[:, 0:7], wraw.rearrange("p w k o -> p w (k o)"), AX_X, ALU.max,
                                   apply_absolute_value=True))
            for k in range(K):
                for a in range(2):
                    step(dve.tensor_tensor_reduce(wtmp[:, 0:D], wraw[:, W2, k], ab[:, a], 1.0, 0.0, ALU.mult,
                                                  ALU.add, w12[:, k, a:a + 1]))
            step(dve.tensor_reduce(wmax[:, WS:WS + 1], w12[:].rearrange("p k a -> p (k a)"), AX_X, ALU.max,
                                   apply_absolute_value=True))
            dve.tensor_reduce(wmax[:, WE:WE + 1], wec[:], AX_X, ALU.max, apply_absolute_value=True
                              ).then_inc(wmax_ok, 1)
            dve.sem_inc(bb_ok, 4)
            with dve.Fori(0, T // 4) as i:
                for b in range(4):
                    n = i * 4 + b
                    dve.wait_ge(adj_ld[b], i * 16 + 16)
                    dve.wait_ge(tp_ok, n + 1)
                    dve.wait_ge(m_ok[b % 2], i * 2 + b // 2 + 1)
                    dve.tensor_scalar(bb[b % 2], adjb[b], 0, None, ALU.is_le).then_inc(bb_ok, 1)
            dve.wait_ge(wall_ok, 1)
            step(dve.tensor_scalar(sc[:, 0:1], wpow[:, WE:WE + 1], 1.0, None, ALU.mult))
            step(dve.tensor_scalar(kI, wpow, TINY, None, ALU.max))
            step(dve.tensor_scalar(wpow.bitcast(U32), kI.bitcast(U32), 0x7F800000, None, ALU.bitwise_and))
            step(dve.reciprocal(kI, wpow))
            step(dve.tensor_scalar(wup, kI, W_UP, None, ALU.mult))
            step(dve.tensor_scalar(kG, wpow, 1.0 / (W_UP * H_UP * G_DOWN), None, ALU.mult))
            step(dve.tensor_scalar(kL, wpow, 1.0 / (W_UP * H_UP), None, ALU.mult))
            step(dve.tensor_scalar(kI, wup, H_UP * G_DOWN, None, ALU.mult))
            step(dve.tensor_scalar(sc[:, 1:2], wpow[:, WK:WK + 1], SCALING * 512.0, sc[:, 0:1], ALU.mult, ALU.add))
            step(dve.tensor_scalar(sc[:, 3:4].bitcast(U32), sc[:, 1:2].bitcast(U32), 0x7F800000, None,
                                   ALU.bitwise_and))
            step(dve.reciprocal(sc[:, 4:5], sc[:, 3:4]))
            step(dve.tensor_scalar(sc[:, 2:3], sc[:, 4:5], 2.0 ** 14, None, ALU.mult))
            step(dve.tensor_scalar(sc[:, 5:6], sc[:, 2:3], kL[:, WK:WK + 1], SCALING, ALU.mult, ALU.mult))
            step(dve.tensor_scalar(wec[:], wec[:], sc[:, 2:3], None, ALU.mult))
            step(dve.tensor_scalar(bec[:], bec[:], sc[:, 2:3], kI[:, WQ:WQ + 1], ALU.mult, ALU.mult))
            for w, dst in ((W0, ws0), (WNB, ws1[:, :, :, 0:D]), (WLINE, ws1[:, :, :, D:]),
                           (W2, ws2[:, :, :, 0:D]), (WQ, wsq), (WK, wsk), (WV, wsv)):
                step(dve.tensor_scalar(dst[:, 0], wraw[:, w], wup[:, w:w + 1], None, ALU.mult))
                step(dve.scalar_tensor_tensor(dst[:, 1], wraw[:, w], wup[:, w:w + 1], dst[:, 0], ALU.mult,
                                              ALU.subtract))
            step(dve.tensor_scalar(ws2[:, 0, :, D:], w12[:], wup[:, WS:WS + 1], None, ALU.mult))
            step(dve.scalar_tensor_tensor(ws2[:, 1, :, D:], w12[:], wup[:, WS:WS + 1], ws2[:, 0, :, D:],
                                          ALU.mult, ALU.subtract))
            step(dve.memset(G[:, :, 0, D:], 1.0))
            step(dve.memset(G[:, :, 1, D:], 0.0))
            dve.wait_ge(consts_ok, 6 + H)
            dve.wait_ge(mt_ok, T + 2)
            dve.tensor_scalar(diag_save, diag_blocks, 1.0 / NEG, None, ALU.mult).then_inc(dg, 1)
            dve.wait_ge(dg, 1)
            dve.tensor_tensor(diag_blocks, diag_blocks, off_diag[:].unsqueeze(1).to_broadcast([P, T, P]), ALU.mult
                              ).then_inc(dg, 1)

        class Front:
            def __init__(self, name):
                self.stats = sem(name + "_stats")
                self.h_ok = sem(name + "_h")
                self.split_ok = sem(name + "_split")
                self.turned = sem(name + "_turned")
                self.hT_ok = sem(name + "_hT")
                self.lin_ok = sem(name + "_linear")
                self.post_a = sem(name + "_post_act")
                self.post_v = sem(name + "_post_dve")
                self.a0, self.std_ok = sem(name + "_a"), sem(name + "_std")

            def vector(self, dve):
                dve.wait_ge(x_ld, 16)
                for t in range(T):
                    dve.bn_stats(st6[:, t], xs[:, t]).then_inc(self.stats, 1)
                for t in range(T):
                    dve.wait_ge(self.stats, T)
                    dve.bn_aggr(mv[:, t], st6[:, t]).then_inc(self.stats, 1)
                dve.wait_ge(self.stats, 2 * T)
                dve.tensor_scalar(veps, mv[:, :, 1], EPS, None, ALU.add).then_inc(self.stats, 1)
                dve.wait_ge(self.std_ok, 1)
                dve.reciprocal(nsq, std).then_inc(self.stats, 1)
                dve.wait_ge(self.stats, 2 * T + 2)
                dve.tensor_scalar(r2, nsq, H_UP, None, ALU.mult).then_inc(self.stats, 1)
                dve.wait_ge(self.stats, 2 * T + 3)
                dve.scalar_tensor_tensor(nbias, mv[:, :, 0], -1.0, r2, ALU.mult, ALU.mult).then_inc(self.stats, 1)

                def split(g):
                    dve.wait_ge(self.h_ok, TC * (g + 1))
                    if g >= 2:
                        dve.wait_ge(self.turned, g - 1)
                    dve.tensor_copy(hn[g % 2][:, 0], h32[g % 2]).then_inc(self.split_ok, 1)
                    dve.wait_ge(self.split_ok, 2 * g + 1)
                    dve.tensor_tensor(hn[g % 2][:, 1], h32[g % 2], hn[g % 2][:, 0], ALU.subtract
                                      ).then_inc(self.split_ok, 1)
                split(0)
                split(1)
                split(2)
                self.post_dve(dve, 0)
                split(3)
                for g in range(1, C):
                    self.post_dve(dve, g)

            def scalar(self, act):
                act.wait_ge(self.stats, 2 * T + 1)
                act.activation(std, veps, ACT.Sqrt).then_inc(self.std_ok, 1)
                act.wait_ge(self.stats, 2 * T + 4)

                def relu(g):
                    if g >= 2:
                        act.wait_ge(self.split_ok, 2 * (g - 1))
                    for t in range(TC):
                        i = TC * g + t
                        act.activation(h32[g % 2][:, t], xs[:, i], ACT.Relu, scale=r2[:, i:i + 1],
                                       bias=nbias[:, i:i + 1]).then_inc(self.h_ok, 1)

                def turn(g):
                    act.wait_ge(self.turned, g + 1)
                    if g >= 2:
                        act.wait_ge(self.lin_ok, g - 1)
                    act.activation(hT[g % 2].rearrange("p a b c -> p (a b c)"), tp(g % 2), ACT.Copy
                                   ).then_inc(self.hT_ok, 1)
                relu(0)
                relu(1)
                turn(0)
                relu(2)
                turn(1)
                self.post_act(act, 0)
                relu(3)
                turn(2)
                self.post_act(act, 1)
                turn(3)
                self.post_act(act, 2)
                self.post_act(act, 3)

            def tensor(self, pe):
                def turn(g):
                    pe.wait_ge(self.split_ok, 2 * g + 2)
                    if g >= 2:
                        pe.wait_ge(self.hT_ok, g - 1)
                    for hl in range(2):
                        for k in range(K):
                            for t in range(TC):
                                c = ((hl * K + k) * TC + t) * P
                                last = pe.transpose(tp(g % 2)[:, c:c + P], hn[g % 2][:, hl, t, P * k:P * k + P],
                                                    ident16[:])
                    last.then_inc(self.turned, 1)

                def lin(g):
                    pe.wait_ge(self.hT_ok, g + 1)
                    self.linear(pe, g).then_inc(self.lin_ok, 1)
                turn(0)
                turn(1)
                lin(0)
                turn(2)
                lin(1)
                turn(3)
                lin(2)
                lin(3)

        TERMS = ((0, 0), (0, 1), (1, 0))

        def product(pe, dst, lhs, rhs):
            n = 0
            for a, b in TERMS:
                for k in range(K):
                    last = pe.matmul(dst, lhs(a, k), rhs(b, k), start=(n == 0), stop=(n == len(TERMS) * K - 1))
                    n += 1
            return last

        def lin_bank(t):
            return psum[:, 4 + t, :]

        def linear_rows(w, n, front):
            def linear(pe, g):
                if g >= 1:
                    pe.wait_ge(front().post_a, front().copies * g)
                    if front().adds_to_x:
                        pe.wait_ge(front().post_v, front().adds_to_x * g)
                for t in range(TC):
                    last = product(pe, lin_bank(t)[:, 0:n], lambda hl, k: hT[g % 2][:, hl, k, P * t:P * t + P],
                                   lambda hl, k: w[:, hl, k, 0:n])
                return last
            return linear

        gf = at(A_UB, [T, D], F32)
        WhnT = at(A_R3, [2, K, N], F16)
        u_b = at(A_UB, [N], F32)
        whn32 = [at(A_F + 4096 * b, [TC, D], F32) for b in range(2)]
        whn = [at(A_F + 8192 + 4096 * b, [2, TC, D], F16) for b in range(2)]
        diag_u = at(A_F + 16384, [TC, P], F32)
        junk = at(A_F + 18432, [D], F32)
        l0b_v, l0b_a, l0b_t = sem("l0_unit_rows"), sem("l0_unit_kept"), sem("l0_unit_turned")
        l0n, l0n_a, l0d, l0u = sem("l0_norms"), sem("l0_sqrt"), sem("l0_diag"), sem("l0_u")
        l0u_a = sem("l0_u_kept")

        def l0_post_act(act, g):
            f = fronts[0]
            act.wait_ge(f.lin_ok, g + 1)
            act.activation(gf[:, TC * g:TC * g + TC], psum[:, 4:8, 0:D], ACT.Copy, scale=G_DOWN).then_inc(f.post_a, 1)

        def l0_post_dve(dve, g):
            f = fronts[0]
            dve.wait_ge(f.post_a, g + 1)
            i = TC * g
            dve.tensor_copy(G[:, i:i + TC, 0, 0:D], gf[:, i:i + TC]).then_inc(f.post_v, 1)
            dve.wait_ge(f.post_v, 2 * g + 1)
            dve.tensor_tensor(G[:, i:i + TC, 1, 0:D], gf[:, i:i + TC], G[:, i:i + TC, 0, 0:D], ALU.subtract
                              ).then_inc(f.post_v, 1)

        def l0_unit_vector(dve):
            for t in range(T):
                dve.wait_ge(l0n, t) if t else None
                dve.tensor_tensor_reduce(junk, gf[:, t], gf[:, t], 1.0, 0.0, ALU.mult, ALU.add, nsq[:, t:t + 1]
                                         ).then_inc(l0n, 1)
            dve.wait_ge(l0n, T)
            dve.tensor_scalar(veps, nsq, 2.0 ** -62, None, ALU.max).then_inc(l0n, 1)
            dve.tensor_scalar(tiny[:, 2:3], kG[:, W0:W0 + 1].bitcast(I32), 2.0 ** -23, -127.0, ALU.mult, ALU.add
                              ).then_inc(l0n, 1)
            dve.wait_ge(l0n_a, 2)
            dve.reciprocal(ucol, std).then_inc(l0n, 1)
            dve.wait_ge(l0n, T + 3)
            dve.tensor_scalar(tiny[:, 3:4], tiny[:, 2:3], LN2 / 2, None, ALU.mult).then_inc(l0n, 1)
            dve.wait_ge(l0n, T + 4)
            dve.tensor_scalar(acol, bcol, 0.25, tiny[:, 3:4], ALU.mult, ALU.add).then_inc(l0n, 1)
            dve.wait_ge(l0n, T + 5)
            dve.tensor_scalar(bcol, acol, -0.5 * float(np.log(L0_EPS)), None, ALU.add).then_inc(l0n, 1)
            for g in range(C):
                b = g % 2
                for t in range(TC):
                    i = TC * g + t
                    dve.tensor_scalar(whn32[b][:, t], gf[:, i], ucol[:, i:i + 1], UNIT_UP, ALU.mult, ALU.mult
                                      ).then_inc(l0b_v, 1)
                if g >= 2:
                    dve.wait_ge(l0b_t, g - 1)
                dve.wait_ge(l0b_v, 6 * g + 4)
                dve.tensor_copy(whn[b][:, 0], whn32[b]).then_inc(l0b_v, 1)
                dve.wait_ge(l0b_v, 6 * g + 5)
                dve.tensor_tensor(whn[b][:, 1], whn32[b], whn[b][:, 0], ALU.subtract).then_inc(l0b_v, 1)
                dve.wait_ge(l0b_v, 6 * g + 6)
            for g in range(C):
                if g >= 1:
                    dve.wait_ge(l0u, g)
                for t in range(TC):
                    i = TC * g + t
                    dve.tensor_scalar(diag_u[:, t], ident32[:], acol[:, i:i + 1], None, ALU.mult).then_inc(l0d, 1)

        def l0_unit_tensor(pe):
            for g in range(C):
                pe.wait_ge(l0b_v, 6 * g + 6)
                if g >= 2:
                    pe.wait_ge(l0b_a, g - 1)
                for hl in range(2):
                    for k in range(K):
                        for t in range(TC):
                            c = ((hl * K + k) * TC + t) * P
                            last = pe.transpose(tp(g % 2)[:, c:c + P], whn[g % 2][:, hl, t, P * k:P * k + P],
                                                ident16[:])
                last.then_inc(l0b_t, 1)
            for g in range(C):
                pe.wait_ge(l0d, TC * (g + 1))
                if g == 0:
                    pe.wait_ge(fronts[0].post_a, C)
                for t in range(TC):
                    last = pe.matmul(psum[:, 4 + g, P * t:P * t + P], ones32[:], diag_u[:, t], start=True, stop=True)
                last.then_inc(l0u, 1)

        def l0_unit_scalar(act):
            act.wait_ge(l0n, T + 1)
            act.activation(std, veps, ACT.Sqrt).then_inc(l0n_a, 1)
            act.activation(bcol, veps, ACT.Ln).then_inc(l0n_a, 1)
            for g in range(C):
                act.wait_ge(l0b_t, g + 1)
                act.activation(WhnT[:, :, :, CH * g:CH * g + CH], tp(g % 2).rearrange("p (a b c) -> p a b c", a=2, b=K),
                               ACT.Copy).then_inc(l0b_a, 1)
            for g in range(C):
                act.wait_ge(l0u, g + 1)
                act.wait_ge(l0b_v, 6 * C)
                act.activation(u_b[:, CH * g:CH * g + CH], psum[:, 4 + g, :], ACT.Copy).then_inc(l0u_a, 1)

        den = [at(A_F + 2048 * b, [CH], F32) for b in range(2)]
        sim = [at(A_F + 4096 + 2048 * b, [CH], F32) for b in range(2)]
        num = [at(A_F + 8192 + 2048 * b, [CH], F32) for b in range(2)]
        num_hl = [at(A_F + 12288 + 2048 * b, [2, CH], F16) for b in range(3)]
        el_tmp = at(A_F + 18432, [D + 2], F32)
        el_tmp2 = at(A_F + 18432 + 1040, [D], F32)
        el_tmp3 = at(A_F + 18432 + 2064, [D], F32)

        class Attention:

            def __init__(self, name):
                self.scores = sem(name + "_scores")
                self.den = sem(name + "_den")
                self.rec = sem(name + "_rec")
                self.sim = sem(name + "_sim")
                self.num = sem(name + "_num")
                self.hi = sem(name + "_hi")
                self.lo = sem(name + "_lo")
                self.summed = sem(name + "_summed")
                self.taken = sem(name + "_taken")
                self.ep = sem(name + "_epilogue")
                self.ep_a = sem(name + "_elu")

        A0 = Attention("l0")

        S_BANK = (4, 5, 6)

        def av_step(pe, A, c, j):
            n = c * T + j
            pe.wait_ge(A.lo, n + 4)
            if j == 0:
                pe.wait_ge(A.taken, c + 1)
            e = num_hl[j % 3]
            for t in range(TC):
                o = psum[:, t, 0:D + 1]
                pe.matmul(o, e[:, 0, P * t:P * t + P], G[:, j, 0, 0:D + 1], start=(j == 0), stop=False)
                pe.matmul(o, e[:, 0, P * t:P * t + P], G[:, j, 1, 0:D + 1], start=False, stop=False)
                last = pe.matmul(o, e[:, 1, P * t:P * t + P], G[:, j, 0, 0:D + 1], start=False, stop=(j == T - 1))
            last.then_inc(A.summed, 1)

        def l0_tensor(pe):
            A = A0
            pe.sem_inc(A.scores, 3)
            pe.sem_inc(A.summed, 3)

            with pe.Fori(0, C) as c:
                def scores(j):
                    pe.wait_ge(A.sim, c * T + j + 1)
                    dst = psum[:, S_BANK[j % 3], :]
                    pe.matmul(dst, ident[:], no_edge_T[:, j, bass.ds(c * CH, CH)], start=True, stop=False)
                    m = 0
                    for a, b in TERMS:
                        for k in range(K):
                            m += 1
                            last = pe.matmul(dst, WhnT[:, a, k, P * j:P * j + P], WhnT[:, b, k, bass.ds(c * CH, CH)],
                                             start=False, stop=(m == 3 * K))
                    last.then_inc(A.scores, 1)
                scores(0)
                scores(1)
                for j in range(T):
                    if j + 2 < T:
                        scores(j + 2)
                    av_step(pe, A, c, j)

        def l0_scalar(act):
            A = A0
            act.sem_inc(A.den, 3)
            act.sem_inc(A.num, 3)
            act.sem_inc(A.hi, 3)
            with act.Fori(0, C) as c:
                def den_(j):
                    act.wait_ge(A.sim, c * T + j + 2)
                    act.sem_inc(gate, 1)
                    act.activation(den[j % 2], u_b[:, bass.ds(c * CH, CH)], ACT.Tanh, bias=bcol[:, j:j + 1]
                                   ).then_inc(A.den, 1)
                den_(0)
                den_(1)
                for j in range(T):
                    n = c * T + j
                    act.wait_ge(A.sim, n + 4)
                    act.wait_ge(A.lo, n + 2)
                    act.activation(num[j % 2], sim[j % 2], ACT.Exp, scale=UNIT_DOWN).then_inc(A.num, 1)
                    act.wait_ge(A.summed, n + 1)
                    act.activation(num_hl[j % 3][:, 0], sim[j % 2], ACT.Exp, scale=UNIT_DOWN).then_inc(A.hi, 1)
                    if j + 2 < T:
                        den_(j + 2)

        def l0_vector(dve):
            A = A0
            dve.sem_inc(A.sim, 3)
            dve.sem_inc(A.lo, 3)
            dve.sem_inc(A.taken, 1)
            dve.sem_inc(A.ep, 1)
            with dve.Fori(0, C) as c:
                def lo_(j):
                    n = c * T + j
                    dve.wait_ge(A.hi, n + 4)
                    dve.tensor_tensor(num_hl[j % 3][:, 1], num[j % 2], num_hl[j % 3][:, 0], ALU.subtract
                                      ).then_inc(A.lo, 1)
                for j in range(T):
                    n = c * T + j
                    dve.wait_ge(A.den, n + 4)
                    dve.wait_ge(A.scores, n + 4)
                    dve.wait_ge(A.hi, n + 2)
                    dve.scalar_tensor_tensor(sim[j % 2], den[j % 2], ABOVE_ONE, psum[:, S_BANK[j % 3], :],
                                             ALU.add, ALU.mult).then_inc(A.sim, 1)
                    if j >= 1:
                        lo_(j - 1)
                lo_(T - 1)
                dve.wait_ge(A.summed, c * T + T + 3)
                for t in range(TC):
                    o = psum[:, t, :]
                    k0 = 3 * t
                    dve.wait_ge(A.ep, c * 12 + k0 + 1)
                    dve.reciprocal(tiny[:, 0:1], o[:, D:D + 1]).then_inc(A.ep, 1)
                    dve.wait_ge(A.ep, c * 12 + k0 + 2)
                    dve.tensor_scalar(tiny[:, 1:2], tiny[:, 0:1], kG[:, W0:W0 + 1], None, ALU.mult).then_inc(A.ep, 1)
                    dve.wait_ge(A.ep, c * 12 + k0 + 3)
                    x_i = xs[:, bass.ds(c * TC + t, 1), :].rearrange("p a d -> p (a d)")
                    last = dve.scalar_tensor_tensor(x_i, o[:, 0:D], tiny[:, 1:2], x_i, ALU.mult, ALU.add
                                                    ).then_inc(A.ep, 1)
                dve.wait_ge(A.ep, c * 12 + 13)
                dve.sem_inc(A.taken, 1)

        class Spread:
            def __init__(self, name):
                self.diag, self.out, self.kept = sem(name + "_diag"), sem(name + "_out"), sem(name + "_kept")

            def vector(self, dve, col):
                for g in range(C):
                    if g >= 1:
                        dve.wait_ge(self.out, g)
                    for t in range(TC):
                        i = TC * g + t
                        dve.tensor_scalar(diag[:, t], ident32[:], col(i), None, ALU.mult).then_inc(self.diag, 1)

            def tensor(self, pe):
                for g in range(C):
                    pe.wait_ge(self.diag, TC * (g + 1))
                    for t in range(TC):
                        last = pe.matmul(psum[:, 4 + g, P * t:P * t + P], ones32[:], diag[:, t], start=True,
                                         stop=True)
                    last.then_inc(self.out, 1)

            def scalar(self, act, dst):
                for g in range(C):
                    act.wait_ge(self.out, g + 1)
                    act.activation(dst[:, CH * g:CH * g + CH], psum[:, 4 + g, :], ACT.Copy).then_inc(self.kept, 1)

        diag = at(A_F + 16384, [TC, P], F32)

        gfb = [at(A_UB + 4096 * b, [TC, D], F32) for b in range(2)]
        zline = at(A_XB, [TC, D], F32)
        b_rows = at(A_XB + 4096, [2, D], F32)
        z_t = at(A_XB + 6144, [D], F32)
        b_ld = sem("bias_loaded")

        def l1_load(sp):
            sp.dma_start(b_rows[:, 0], b_nb.partition_broadcast(P)).then_inc(b_ld, 16)
            sp.dma_start(b_rows[:, 1], b_line.partition_broadcast(P)).then_inc(b_ld, 16)

        def split_post_act(i):
            def post(act, g):
                f = fronts[i]
                act.wait_ge(f.lin_ok, g + 1)
                if g >= 2:
                    act.wait_ge(f.post_v, f.per_v * (g - 1))
                act.activation(gfb[g % 2], psum[:, 4:8, 0:D], ACT.Copy, scale=G_DOWN).then_inc(f.post_a, 1)
                if i == 2:
                    act.activation(s12[:, TC * g:TC * g + TC, :], psum[:, 4:8, D:D + 2], ACT.Identity,
                                   scale=kL[:, WS:WS + 1]).then_inc(f.post_a, 1)
            return post

        def split_post_dve(i):
            def post(dve, g):
                f = fronts[i]
                n, r = f.per_v * g, TC * g
                dve.wait_ge(f.post_a, f.copies * g + 1)
                dve.tensor_copy(G[:, r:r + TC, 0, 0:D], gfb[g % 2]).then_inc(f.post_v, 1)
                dve.wait_ge(f.post_v, n + 1)
                dve.tensor_tensor(G[:, r:r + TC, 1, 0:D], gfb[g % 2], G[:, r:r + TC, 0, 0:D], ALU.subtract
                                  ).then_inc(f.post_v, 1)
                if i == 1:
                    if g == 0:
                        dve.wait_ge(b_ld, 32)
                    for t in range(TC):
                        dve.scalar_tensor_tensor(zline[:, t], psum[:, 4 + t, D:2 * D], kL[:, WLINE:WLINE + 1],
                                                 b_rows[:, 1], ALU.mult, ALU.add).then_inc(f.post_v, 1)
                    dve.wait_ge(f.post_v, n + 6)
                    dve.scalar_tensor_tensor(zline, zline, 0.01, zline, ALU.mult, ALU.max).then_inc(f.post_v, 1)
                    dve.wait_ge(f.post_v, n + 7)
                    dve.tensor_tensor(xs[:, r:r + TC], xs[:, r:r + TC], zline, ALU.add).then_inc(f.post_v, 1)
                    dve.wait_ge(f.post_v, n + 8)
            return post

        edge = [at(A_F + 4096 * b, [N], BF16) for b in range(2)]
        run = [at(A_F + 8192 + 4112 * b, [N + 2], BF16) for b in range(2)]
        keep = [at(A_R3 + 4096 * b, [N], BF16) for b in range(2)]
        keepT = [at(A_R3 + 8192 + 4096 * b, [T, P], BF16) for b in range(2)]
        cap = at(A_UB, [N], BF16)
        e_ok, run_ok, keep_ok = sem("l1_edges"), sem("l1_count"), sem("l1_keep")
        kt_ok, ktc_ok, agg_ok = sem("l1_keep_turned"), sem("l1_keepT"), sem("l1_summed")
        l1_c, l1_share, l1_out = sem("l1_consts"), sem("l1_share"), sem("l1_out")
        share = sb("share", [P, 2, 3], F32)

        def need(eng, s, v):
            if not isinstance(v, int) or v > 0:
                eng.wait_ge(s, v)

        def has(n, delay):
            return not isinstance(n, int) or 0 <= n - delay < T

        def l1_steps(eng, step):
            for n in range(4):
                step(n, n % 2)
            with eng.Fori(2, T // 2) as i:
                step(i * 2, 0)
                step(i * 2 + 1, 1)
            step(T, 0)
            step(T + 1, 1)

        def l1_scalar(act):
            def step(n, b):
                if has(n, 0):
                    need(act, run_ok, n - 1)
                    act.sem_inc(gate, 1)
                    act.activation(edge[b], no_edge[:, bass.ds(n, 1), :].rearrange("p a j -> p (a j)"), ACT.Copy,
                                   scale=-1.0, bias=1.0).then_inc(e_ok, 1)
                if has(n, 1):
                    need(act, kt_ok, n)
                    need(act, agg_ok, n - 2)
                    act.activation(keepT[1 - b].rearrange("p j i -> p (j i)"), tp(1 - b, BF16), ACT.Copy
                                   ).then_inc(ktc_ok, 1)
            l1_steps(act, step)

        def l1_vector(dve):
            def step(n, b):
                total = run[b][:, N:N + 1]
                if has(n, 0):
                    need(dve, e_ok, n + 1)
                    need(dve, keep_ok, n - 1)
                    need(dve, l1_share, n * 4 - 4)
                    dve.tensor_tensor_scan(run[b][:, 1:N + 1], edge[b], cap, 0.0, ALU.add, ALU.min
                                           ).then_inc(run_ok, 1)
                if has(n, 2):
                    need(dve, agg_ok, n - 1)
                    need(dve, l1_share, n * 4 - 4)
                    need(dve, l1_out, n * 3 - 6)
                    dve.scalar_tensor_tensor(z_t, psum[:, 4 + b, 0:D], share[:, b, 1:2], b_rows[:, 0], ALU.mult,
                                             ALU.add).then_inc(l1_out, 1)
                if has(n, 0):
                    need(dve, run_ok, n + 1)
                    dve.tensor_scalar(share[:, b, 0:1], total, 1.0, None, ALU.max).then_inc(l1_share, 1)
                if has(n, 2):
                    need(dve, l1_out, n * 3 - 5)
                    dve.scalar_tensor_tensor(z_t, z_t, 0.01, z_t, ALU.mult, ALU.max).then_inc(l1_out, 1)
                if has(n, 0):
                    need(dve, l1_share, n * 4 + 1)
                    dve.reciprocal(share[:, b, 0:1], share[:, b, 0:1]).then_inc(l1_share, 1)
                if has(n, 2):
                    x_i = xs[:, bass.ds(n - 2, 1), :].rearrange("p a d -> p (a d)")
                    need(dve, l1_out, n * 3 - 4)
                    dve.scalar_tensor_tensor(x_i, z_t, share[:, b, 2:3], x_i, ALU.mult, ALU.add).then_inc(l1_out, 1)
                if has(n, 0):
                    need(dve, l1_share, n * 4 + 2)
                    dve.tensor_scalar(share[:, b, 1:2], share[:, b, 0:1], kG[:, WNB:WNB + 1], None, ALU.mult
                                      ).then_inc(l1_share, 1)
                    need(dve, l1_out, n * 3 - 3)
                    dve.tensor_scalar(share[:, b, 2:3], total, 1.0, None, ALU.min).then_inc(l1_share, 1)
            dve.memset(cap, float(NEIGHBORS)).then_inc(l1_c, 1)
            for b in range(2):
                dve.memset(run[b][:, 0:1], 0.0).then_inc(l1_c, 1)
            dve.wait_ge(l1_c, 3)
            l1_steps(dve, step)

        def l1_pool(pool):
            def step(n, b):
                if has(n, 0):
                    need(pool, run_ok, n + 1)
                    need(pool, kt_ok, n - 1)
                    nc.gpsimd.tensor_tensor(keep[b], run[b][:, 1:N + 1], run[b][:, 0:N], ALU.subtract
                                            ).then_inc(keep_ok, 1)
            l1_steps(pool, step)

        def l1_tensor(pe):
            def step(n, b):
                if has(n, 1):
                    need(pe, keep_ok, n)
                    need(pe, ktc_ok, n - 2)
                    for j in range(T):
                        last = pe.transpose(tp(1 - b, BF16)[:, P * j:P * j + P], keep[1 - b][:, P * j:P * j + P],
                                            ident[:])
                    last.then_inc(kt_ok, 1)
                if has(n, 2):
                    need(pe, ktc_ok, n - 1)
                    need(pe, l1_out, n * 3 - 11)
                    for j in range(T):
                        for hl in range(2):
                            last = pe.matmul(psum[:, 4 + b, 0:D], keepT[b][:, j], G[:, j, hl, 0:D],
                                             start=(j == 0 and hl == 0), stop=(j == T - 1 and hl == 1))
                    last.then_inc(agg_ok, 1)
            l1_steps(pe, step)

        s2_b = at(A_UB, [N], F32)
        a_b = at(A_R3, [N], F32)
        b_b = at(A_R3 + 8192, [N], F32)
        colsum = at(A_XB, [D + 2], F32)
        mneg = [at(A_F + 4096 * b, [N], BF16) for b in range(2)]
        mjunk = at(A_F + 8192, [N], F32)
        mxcol, s2fifth, empty = nsq, r2, nbias
        spread_s2, spread_a, spread_b = Spread("l2_s2"), Spread("l2_a"), Spread("l2_b")
        mneg_ok, mx_ok, l2p, cs_ok, csk_ok = (sem("l2_mneg"), sem("l2_max"), sem("l2_cols"), sem("l2_colsum"),
                                              sem("l2_colsum_kept"))

        def l2_pre_vector(dve):
            spread_s2.vector(dve, lambda i: s12[:, i, 1:2])
            dve.wait_ge(spread_s2.kept, C)
            for t in range(T):
                dve.wait_ge(mneg_ok, t + 1)
                if t:
                    dve.wait_ge(mx_ok, t)
                dve.tensor_tensor_reduce(mjunk, mneg[t % 2], s2_b, 1.0, 2 * NEG, ALU.add, ALU.max,
                                         mxcol[:, t:t + 1]).then_inc(mx_ok, 1)
            dve.wait_ge(mx_ok, T)
            count = [0]

            def step(ins):
                count[0] += 1
                ins.then_inc(l2p, 1)
                dve.wait_ge(l2p, count[0])
            s1 = s12[:, :, 0]
            step(dve.tensor_tensor(acol, s1, mxcol, ALU.add))
            step(dve.scalar_tensor_tensor(bcol, acol, 0.2, acol, ALU.mult, ALU.max))
            step(dve.tensor_tensor(acol, s1, bcol, ALU.subtract))
            step(dve.scalar_tensor_tensor(bcol, s1, 0.2, bcol, ALU.mult, ALU.subtract))
            step(dve.tensor_scalar(empty, mxcol, 0.5 * NEG, None, ALU.is_lt))
            step(dve.tensor_scalar(s2fifth, s12[:, :, 1], 0.2, None, ALU.mult))
            spread_a.vector(dve, lambda i: acol[:, i:i + 1])
            dve.wait_ge(spread_a.out, C)
            dve.wait_ge(spread_a.kept, C)
            spread_b.vector(dve, lambda i: bcol[:, i:i + 1])

        def l2_pre_tensor(pe):
            spread_s2.tensor(pe)
            pe.wait_ge(spread_s2.kept, C)
            for j in range(T):
                for hl in range(2):
                    last = pe.matmul(psum[:, 0, 0:D + 1], ones16[:], G[:, j, hl, 0:D + 1],
                                     start=(j == 0 and hl == 0), stop=(j == T - 1 and hl == 1))
            last.then_inc(cs_ok, 1)
            spread_a.tensor(pe)
            pe.wait_ge(spread_a.kept, C)
            spread_b.tensor(pe)

        def l2_pre_scalar(act):
            spread_s2.scalar(act, s2_b)
            for t in range(T):
                if t >= 2:
                    act.wait_ge(mx_ok, t - 1)
                act.activation(mneg[t % 2], no_edge[:, t], ACT.Copy, scale=NEG).then_inc(mneg_ok, 1)
            act.wait_ge(cs_ok, 1)
            act.activation(colsum[:, 0:D + 1], psum[:, 0, 0:D + 1], ACT.Copy).then_inc(csk_ok, 1)
            spread_a.scalar(act, a_b)
            spread_b.scalar(act, b_b)

        A2 = Attention("l2")

        def l2_tensor(pe):
            pe.sem_inc(A2.summed, 3)
            with pe.Fori(0, C) as c:
                for j in range(T):
                    av_step(pe, A2, c, j)

        def l2_scalar(act):
            A = A2
            for s in (A.den, A.num, A.hi):
                act.sem_inc(s, 3)
            with act.Fori(0, C) as c:
                def fifth(j):
                    act.wait_ge(A.rec, c * T + j + 2)
                    act.sem_inc(gate, 1)
                    act.activation(den[j % 2], b_b[:, bass.ds(c * CH, CH)], ACT.Identity, bias=s2fifth[:, j:j + 1]
                                   ).then_inc(A.den, 1)
                fifth(0)
                fifth(1)
                for j in range(T):
                    n = c * T + j
                    act.wait_ge(A.sim, n + 4)
                    act.wait_ge(A.lo, n + 2)
                    act.activation(num[j % 2], sim[j % 2], ACT.Exp).then_inc(A.num, 1)
                    act.wait_ge(A.num, n + 4)
                    act.wait_ge(A.summed, n + 1)
                    act.activation(num_hl[j % 3][:, 0], num[j % 2], ACT.Copy, scale=E_UP).then_inc(A.hi, 1)
                    if j + 2 < T:
                        fifth(j + 2)
                for t in range(TC):
                    act.wait_ge(A.ep, c * 7 * TC + t * 7 + 7)
                    act.activation(el_tmp3, el_tmp2, ACT.Exp).then_inc(A.ep_a, 1)

        def l2_vector(dve):
            A = A2
            for s in (A.rec, A.sim, A.lo):
                dve.sem_inc(s, 3)
            dve.sem_inc(A.taken, 1)
            dve.sem_inc(A.ep, 2)
            with dve.Fori(0, C) as c:
                def lo_(j):
                    n = c * T + j
                    dve.wait_ge(A.hi, n + 4)
                    dve.scalar_tensor_tensor(num_hl[j % 3][:, 1], num[j % 2], E_UP, num_hl[j % 3][:, 0], ALU.mult,
                                             ALU.subtract).then_inc(A.lo, 1)
                for j in range(T):
                    n = c * T + j
                    dve.wait_ge(A.den, n + 4)
                    dve.wait_ge(A.num, n + 2)
                    dve.scalar_tensor_tensor(sim[j % 2], a_b[:, bass.ds(c * CH, CH)], s12[:, j, 1:2], den[j % 2],
                                             ALU.add, ALU.max).then_inc(A.rec, 1)
                    dve.wait_ge(A.rec, n + 4)
                    dve.tensor_tensor(sim[j % 2], sim[j % 2],
                                      no_edge_T[:, j, bass.ds(c * CH, CH)], ALU.add
                                      ).then_inc(A.sim, 1)
                    if j >= 1:
                        lo_(j - 1)
                lo_(T - 1)
                dve.wait_ge(A.summed, c * T + T + 3)
                for t in range(TC):
                    o = psum[:, t, 0:D + 1]
                    k0 = c * 7 * TC + t * 7 + 2
                    i = c * TC + t
                    dve.wait_ge(A.ep, k0)
                    dve.scalar_tensor_tensor(el_tmp[:, 0:D + 1], colsum[:, 0:D + 1], empty[:, bass.ds(i, 1)], o,
                                             ALU.mult, ALU.add).then_inc(A.ep, 1)
                    dve.wait_ge(A.ep, k0 + 1)
                    dve.reciprocal(tiny[:, 0:1], el_tmp[:, D:D + 1]).then_inc(A.ep, 1)
                    dve.wait_ge(A.ep, k0 + 2)
                    dve.tensor_scalar(tiny[:, 1:2], tiny[:, 0:1], kG[:, W2:W2 + 1], None, ALU.mult).then_inc(A.ep, 1)
                    dve.wait_ge(A.ep, k0 + 3)
                    dve.tensor_scalar(el_tmp[:, 0:D], el_tmp[:, 0:D], tiny[:, 1:2], None, ALU.mult
                                      ).then_inc(A.ep, 1)
                    dve.wait_ge(A.ep, k0 + 4)
                    dve.tensor_scalar(el_tmp2, el_tmp[:, 0:D], 0.0, None, ALU.min).then_inc(A.ep, 1)
                    dve.wait_ge(A.ep, k0 + 5)
                    dve.scalar_tensor_tensor(el_tmp[:, 0:D], el_tmp[:, 0:D], 0.0, xs[:, bass.ds(i, 1), :].rearrange(
                        "p a d -> p (a d)"), ALU.max, ALU.add).then_inc(A.ep, 1)
                    dve.wait_ge(A.ep, k0 + 6)
                    dve.wait_ge(A.ep_a, i + 1)
                    dve.scalar_tensor_tensor(xs[:, bass.ds(i, 1), :].rearrange("p a d -> p (a d)"), el_tmp3, -1.0,
                                             el_tmp[:, 0:D], ALU.add, ALU.add).then_inc(A.ep, 1)
                dve.wait_ge(A.ep, c * 7 * TC + 7 * TC + 2)
                dve.sem_inc(A.taken, 1)

        q_c = at(A_SG, [K, 2, N], F16)
        k_c = at(A_SG + 16384, [K, 2, N], F16)
        q4 = at(A_R3, [H, N], F16)
        k4 = at(A_K4, [H, N], F16)
        q_lin = sem("f3_qk_linear")
        vf = zline

        def l3_linear(pe, g):
            f = fronts[3]
            if g >= 1:
                pe.wait_ge(f.post_a, 3 * g)
            for w, bank in ((wsq, 4), (wsk, 6)):
                for d in range(K):
                    last = product(pe, psum[:, bank + d, :], lambda hl, k: w[:, hl, k, P * d:P * d + P],
                                   lambda hl, k: hT[g % 2][:, hl, k])
            last.then_inc(q_lin, 1)
            pe.wait_ge(f.post_a, 3 * g + 1)
            for t in range(TC):
                last = product(pe, psum[:, 4 + t // 2, D * (t % 2):D * (t % 2) + D],
                               lambda hl, k: hT[g % 2][:, hl, k, P * t:P * t + P], lambda hl, k: wsv[:, hl, k])
            return last

        def l3_post_act(act, g):
            f = fronts[3]
            act.wait_ge(q_lin, g + 1)
            if g >= 1:
                act.wait_ge(f.post_v, 6 * g)
            act.activation(gfb[0].rearrange("p t d -> p (t d)"), psum[:, 4:6, :].rearrange("p a b -> p (a b)"),
                           ACT.Copy, scale=-G_DOWN).then_inc(f.post_a, 1)
            act.activation(gfb[1].rearrange("p t d -> p (t d)"), psum[:, 6:8, :].rearrange("p a b -> p (a b)"),
                           ACT.Identity, scale=sc[:, 5:6], bias=wec[:, 0:1]).then_inc(f.post_a, 1)
            act.wait_ge(f.lin_ok, g + 1)
            act.activation(vf.rearrange("p t d -> p (t d)"), psum[:, 4:6, :].rearrange("p a b -> p (a b)"),
                           ACT.Copy, scale=G_DOWN).then_inc(f.post_a, 1)

        def l3_post_dve(dve, g):
            f = fronts[3]
            r = TC * g
            for i, (src, dst) in enumerate((
                    (gfb[0].rearrange("p t d -> p (t d)").rearrange("p (a b) -> p a b", a=K),
                     lambda hl: q_c[:, :, hl, CH * g:CH * g + CH]),
                    (gfb[1].rearrange("p t d -> p (t d)").rearrange("p (a b) -> p a b", a=K),
                     lambda hl: k_c[:, :, hl, CH * g:CH * g + CH]),
                    (vf, lambda hl: G[:, r:r + TC, hl, 0:D]))):
                dve.wait_ge(f.post_a, 3 * g + i + 1)
                dve.tensor_copy(dst(0), src).then_inc(f.post_v, 1)
                dve.wait_ge(f.post_v, 6 * g + 2 * i + 1)
                dve.tensor_tensor(dst(1), src, dst(0), ALU.subtract).then_inc(f.post_v, 1)

        x_save = nc.dram_tensor("x_save", (N, D), F32, kind="Internal").ap().rearrange("(t p) d -> p t d", p=P)
        lay_ld, lay_late, xs_ld = sem("l3_rows_laid"), sem("l3_rows_laid_late"), sem("l3_x_saved")

        qk_dram = nc.dram_tensor("qk_rows", (2, K, 2, P, N), F16, kind="Internal").ap()
        qk_saved = sem("l3_qk_saved")

        def rows_of_heads(eng, dst, which, k, r, hl, cols, done):
            eng.dma_start(dst[DH * r:DH * r + DH, 4 * k:4 * k + 4, cols],
                          qk_dram[which, k, hl, :, cols].rearrange("(h p) c -> p h c", p=DH)).then_inc(done, 16)

        def l3_lay_sync(sp):
            for g in range(C):
                cols = slice(CH * g, CH * g + CH)
                for i, c in ((1, k_c), (0, q_c)):
                    sp.wait_ge(fronts[3].post_v, 6 * g + (2, 4)[i])
                    for k in range(K):
                        sp.dma_start(qk_dram[i, k, :, :, cols].rearrange("l p c -> p l c"), c[:, k, :, cols]
                                     ).then_inc(qk_saved, 16)
                sp.wait_ge(qk_saved, 16 * 4 * (g + 1))
                for r in range(4):
                    rows_of_heads(sp, q4, 0, 0, r, r // 2, cols, lay_ld)
                    for k in range(K):
                        rows_of_heads(sp, k4, 1, k, r, r % 2, cols, lay_ld)
                if g == 0:
                    sp.dma_start(x_save, xs).then_inc(xs_ld, 16)
            sp.wait_ge(xs_ld, 16)

        HB = 2 * CH
        SLOTS = [(0, 0)] + [s for h in range(1, H) for s in ((h, 0), (h - 1, 1))] + [(H - 1, 1)]
        FIRST, SECOND = ({h: SLOTS.index((h, q)) for h in range(H)} for q in range(2))
        m3 = [at(A_F + 8192 * b, [N], F32) for b in range(2)]
        hb = [at(A_F + 16384 + 4096 * b, [T, P], U16) for b in range(2)]
        bits = at(A_W, [N], U16)
        x_in = [at(A_W + 4096 + 1024 * b, [D], F32) for b in range(2)]
        res = [at(A_W + 6144 + 1024 * b, [D], F32) for b in range(2)]
        o_hi = at(A_W + 8192, [D], F32)
        ms = [at(o, [N], F32) for o in (A_X, A_X + 8192, A_W + 9216)]
        picks = [at(A_SG + 16384 * b, [H, N], F8) for b in range(2)]
        names = ("scores", "row_min", "picks", "packed", "bits", "unpacked", "values", "out_hi", "out",
                 "mask")
        sc_ok, tt_ok, sg_ok, pk_ok, pe_ok, up_ok, av_ok, oa_ok, od_ok, m3_ok = (
            sem("l3_" + n) for n in names)
        xt_ld, st_ok = [sem("l3_x0"), sem("l3_x1")], [sem("l3_stored0"), sem("l3_stored1")]
        gate_v, gate_t = sem("dve_gate"), sem("pe_gate")
        row_min = sb("row_min", [P, 2, H], F32)
        PS_OFF, MS_OFF = (0, 1), (0, 2)

        def ms_of(par, h):
            return (h + MS_OFF[par]) % 3

        def steps(eng, step):
            step(0, 0, 0)
            step(1, 0, 1)
            with eng.Fori(1, T // 2 - 1) as i:
                step(i * 2, i, 0)
                step(i * 2 + 1, i, 1)
            step(T - 2, T // 2 - 1, 0)
            step(T - 1, T // 2 - 1, 1)
            step(T, T // 2, 0)
            step(T + 1, T // 2, 1)

        def l3_tensor(pe):
            def step(n, k, par):
                def scores(s):
                    h, q = SLOTS[s]
                    buf = (s + PS_OFF[par]) % 3
                    if isinstance(n, int) and n == 0 and q == 0 and h == H // 2:
                        pe.wait_ge(lay_late, 16 * 4)
                    if s >= 3:
                        need(pe, tt_ok, n * 16 + s - 2)
                    else:
                        old = max(o for o in range(13, 16) if (o + PS_OFF[1 - par]) % 3 == buf)
                        need(pe, tt_ok, n * 16 + old - 15)
                    for c in range(2):
                        last = pe.matmul(psum[:, 2 * buf + c, :], q4[:, h, bass.ds(n * P, P)],
                                         k4[:, h, HB * q + CH * c:HB * q + CH * c + CH], start=True, stop=True)
                    last.then_inc(sc_ok, 1)

                def pack(g):
                    need(pe, sg_ok, n * 8)
                    need(pe, pe_ok, n * 4 - 4 + g)
                    pe.sem_inc(gate_t, 1)
                    for kb in range(TC):
                        for h in range(H):
                            j = TC * g + kb
                            c = P * kb
                            last = pe.matmul(psum[:, 6, c:c + P], picks[1 - par][:, h, P * j:P * j + P],
                                             head_bit[:, h], start=(h == 0), stop=(h == H - 1))
                    last.then_inc(pk_ok, 1)

                def values(d, h):
                    need(pe, up_ok, n * 8 - 8 * d + h + 1)
                    if h == 0:
                        need(pe, od_ok, n * 2 - 2 * d + 4)
                    for j in range(T):
                        last = pe.matmul(psum[:, 7, 64 * h:64 * h + 64], hb[h % 2][:, j].bitcast(F16),
                                         G[:, j, :, DH * h:DH * h + DH], start=(j == 0), stop=(j == T - 1))
                    last.then_inc(av_ok, 1)

                for s in range(16):
                    if has(n, 0):
                        scores(s)
                    for h in range(H):
                        if PE_VALUES[h] == 16 + s and has(n, 2):
                            values(2, h)
                    for g in range(C):
                        if PE_PACK[g] == s and has(n, 1):
                            pack(g)
                    for h in range(H):
                        if PE_VALUES[h] == s and has(n, 1):
                            values(1, h)
            pe.wait_ge(lay_ld, 16 * 12 * C)
            steps(pe, step)

        PE_PACK, PE_VALUES = (4, 7, 9, 11), (14, 15, 16, 17, 18, 18, 19, 20)
        DVE_UNPACK, DVE_TAKE, ACT_MASK = (11, 12, 13, 14, 15, 15, 16, 17), 6, 5

        def l3_vector(dve):
            def step(n, k, par):
                def scan(s):
                    h, q = SLOTS[s]
                    buf = (s + PS_OFF[par]) % 3
                    need(dve, sc_ok, n * 16 + s + 1)
                    if q == 0:
                        if h >= 3:
                            need(dve, sg_ok, n * 8 + h - 2)
                        else:
                            old = max(o for o in range(5, 8) if ms_of(1 - par, o) == ms_of(par, h))
                            need(dve, sg_ok, n * 8 + old - 7)
                    else:
                        need(dve, tt_ok, n * 16 + FIRST[h] + 1)
                    if s == 0:
                        need(dve, m3_ok, n + 1)
                    dve.sem_inc(gate_v, 1)
                    part = slice(HB * q, HB * q + HB)
                    dve.tensor_tensor_reduce(ms[ms_of(par, h)][:, part],
                                             psum[:, 2 * buf:2 * buf + 2, :].rearrange("p a b -> p (a b)"),
                                             m3[par][:, part], 1.0, -0.5 * NEG if q == 0 else row_min[:, 0, h:h + 1],
                                             ALU.add, ALU.min, row_min[:, q, h:h + 1]).then_inc(tt_ok, 1)

                def unpack(d, h):
                    need(dve, pe_ok, n * 4 + 4 - 4 * d)
                    need(dve, av_ok, n * 8 - 8 * d + h - 1)
                    dve.tensor_scalar(hb[h % 2].rearrange("p j i -> p (j i)"), bits, 14 - h, 0x4000,
                                      ALU.logical_shift_left, ALU.bitwise_and).then_inc(up_ok, 1)

                def take():
                    need(dve, oa_ok, n - 1)
                    lo = psum[:, 7, :].rearrange("p (h a d) -> p h a d", h=H, a=2)[:, :, 1, :]
                    dve.scalar_tensor_tensor(o_hi.rearrange("p (h d) -> p h d", h=H), lo, sc[:, 6:7],
                                             o_hi.rearrange("p (h d) -> p h d", h=H), ALU.mult, ALU.add
                                             ).then_inc(od_ok, 1)

                def add_x():
                    need(dve, od_ok, n * 2 - 4 + 5)
                    need(dve, xt_ld[par], k * 16)
                    need(dve, st_ok[par], k * 16)
                    dve.tensor_tensor(res[par], o_hi, x_in[par], ALU.add).then_inc(od_ok, 1)

                for s in range(16):
                    if has(n, 0):
                        scan(s)
                    if s == DVE_TAKE and has(n, 2):
                        take()
                    if s == DVE_TAKE + 1 and has(n, 2):
                        add_x()
                    for h in range(H):
                        if DVE_UNPACK[h] == 16 + s and has(n, 2):
                            unpack(2, h)
                        if DVE_UNPACK[h] == s and has(n, 1):
                            unpack(1, h)
            dve.tensor_scalar(sc[:, 6:7], kG[:, WV:WV + 1], 1.0 / 16, None, ALU.mult).then_inc(l3c, 1)
            dve.tensor_scalar(sc[:, 7:8], bec[:], -1.0, None, ALU.mult).then_inc(l3c, 1)
            dve.wait_ge(l3c, 2)
            dve.sem_inc(od_ok, 4)
            steps(dve, step)

        l3c = sem("l3_const")

        def l3_scalar(act):
            def step(n, k, par):
                def sign(h):
                    need(act, tt_ok, n * 16 + SECOND[h] + 1)
                    if h == 0:
                        need(act, pk_ok, n * 4 - 4)
                    act.sem_inc(gate, 1)
                    act.activation(picks[par][:, h], ms[ms_of(par, h)], ACT.Sign, bias=row_min[:, 1, h:h + 1],
                                   scale=-1.0, saturate=False).then_inc(sg_ok, 1)

                def to_bits(g):
                    need(act, pk_ok, n * 4 - 4 + g + 1)
                    need(act, up_ok, n * 8 - 8)
                    act.activation(bits[:, CH * g:CH * g + CH], psum[:, 6, :], ACT.Copy, bias=float(2 ** H - 1)
                                   ).then_inc(pe_ok, 1)

                def mask(m):
                    if m > 1 or not isinstance(m, int):
                        act.wait_ge(tt_ok, m * 16 - 16)
                    act.sem_inc(gate, 1)
                    act.activation(m3[m % 2 if isinstance(m, int) else 1 - par],
                                   no_edge[:, bass.ds(m, 1), :].rearrange("p a j -> p (a j)"), ACT.Identity,
                                   scale=-NEG, bias=sc[:, 7:8]).then_inc(m3_ok, 1)

                if isinstance(n, int) and n == 0:
                    mask(0)
                for h in range(H):
                    if has(n, 0):
                        sign(h)
                    if h == ACT_MASK and has(n, -1):
                        mask(n + 1)
                    if h == 1 and has(n, 2):
                        need(act, av_ok, n * 8 - 8)
                        need(act, od_ok, n * 2 - 4 + 4)
                        hi = psum[:, 7, :].rearrange("p (h a d) -> p h a d", h=H, a=2)[:, :, 0, :]
                        act.activation(o_hi.rearrange("p (h d) -> p h d", h=H), hi, ACT.Identity, scale=sc[:, 6:7]
                                       ).then_inc(oa_ok, 1)
                    if h < 4 and has(n, 1):
                        to_bits(h)
            act.wait_ge(l3c, 2)
            steps(act, step)

        def l3_sync(sp):
            for r in range(4):
                rows_of_heads(sp, q4, 0, 1, r, r // 2, slice(0, N), lay_late)
            sp.wait_ge(lay_late, 16 * 4)
            for s in st_ok:
                sp.sem_inc(s, 16)
            with sp.Fori(0, T // 2) as i:
                for par in range(2):
                    n = i * 2 + par
                    sp.wait_ge(od_ok, n * 2 + 2)
                    sp.dma_start(x_in[par], x_save[:, bass.ds(n, 1), :]).then_inc(xt_ld[par], 16)
                    sp.wait_ge(od_ok, n * 2 + 6)
                    sp.dma_start(out_t[:, bass.ds(n, 1), :], res[par]).then_inc(st_ok[par], 16)
            for s in st_ok:
                sp.wait_ge(s, 16 + 16 * (T // 2))

        fronts = {}

        def new_front(i, name, copies, adds_to_x, w, n, pa, pv, linear=None):
            f = Front(name)
            f.copies, f.adds_to_x = copies, adds_to_x
            f.post_act, f.post_dve = pa, pv
            f.linear = linear or linear_rows(w, n, lambda: fronts[i])
            fronts[i] = f

        new_front(0, "f0", 1, 0, ws0, D, l0_post_act, l0_post_dve)
        new_front(1, "f1", 1, 8, ws1, 2 * D, split_post_act(1), split_post_dve(1))
        new_front(2, "f2", 2, 0, ws2, D + 2, split_post_act(2), split_post_dve(2))
        new_front(3, "f3", 3, 0, None, 0, l3_post_act, l3_post_dve, l3_linear)
        fronts[1].per_v, fronts[2].per_v = 8, 2

        block = ctx.enter_context(nc.Block())

        def finish_sync(sp):
            sp.dma_start(out_t, xs).then_inc(x_ld, 16)
            sp.wait_ge(x_ld, 32)

        def restore_vector(dve):
            dve.wait_ge(dg, 2)
            dve.tensor_scalar(diag_blocks, diag_save, NEG, None, ALU.mult).then_inc(dg, 1)

        def front_stage(i):
            return dict(vector=fronts[i].vector, scalar=fronts[i].scalar, tensor=fronts[i].tensor)

        stages = [
            dict(sync=load_sync, pool=load_pool, vector=load_vector, scalar=load_scalar, tensor=load_tensor),
            front_stage(0),
            dict(vector=l0_unit_vector, scalar=l0_unit_scalar, tensor=l0_unit_tensor),
            dict(vector=l0_vector, scalar=l0_scalar, tensor=l0_tensor),
            dict(sync=l1_load, vector=lambda e: (restore_vector(e), fronts[1].vector(e)), scalar=fronts[1].scalar,
                 tensor=fronts[1].tensor),
            dict(pool=l1_pool, vector=l1_vector, scalar=l1_scalar, tensor=l1_tensor),
            front_stage(2),
            dict(vector=l2_pre_vector, scalar=l2_pre_scalar, tensor=l2_pre_tensor),
            dict(vector=l2_vector, scalar=l2_scalar, tensor=l2_tensor),
            dict(sync=l3_lay_sync, **front_stage(3)),
            dict(sync=l3_sync, vector=l3_vector, scalar=l3_scalar, tensor=l3_tensor),
        ]
        if stop:
            stages = stages[:stop]

        def run_stages(eng, name):
            for k, s in enumerate(stages):
                if name in s:
                    s[name](eng)
                stage_end(eng, k + 1)

        @block.sync
        def _(sp):
            run_stages(sp, "sync")
            if stop:
                finish_sync(sp)

        @block.gpsimd
        def _(pool):
            run_stages(pool, "pool")

        @block.vector
        def _(dve):
            run_stages(dve, "vector")

        @block.scalar
        def _(act):
            run_stages(act, "scalar")

        @block.tensor
        def _(pe):
            run_stages(pe, "tensor")


def kernel(**inputs):
    import numpy as np
    import concourse.bacc as bacc
    from concourse.bass_utils import run_bass_kernel_spmd

    nc = bacc.Bacc("TRN2", target_bir_lowering=False, num_devices=1)
    arrays = {}

    def given(name, array):
        arrays[name] = np.ascontiguousarray(array)
        return nc.dram_tensor(name, array.shape, mybir.dt.from_np(array.dtype), kind="ExternalInput").ap()

    g = {k: np.asarray(v) for k, v in inputs.items()}
    x, adj = given("x", g["x"]), given("adj", g["adj"])
    weights = [given("w0_T", g["L0_gnn_W"].T), given("w_nb_T", g["L1_gnn_W_nb"].T),
               given("w_line_T", g["L1_gnn_W_line"].T), given("w2", g["L2_gnn_W"]),
               given("wq_T", g["L3_gnn_WQ"].T), given("wk_T", g["L3_gnn_WK"].T), given("wv_T", g["L3_gnn_WV"].T)]
    attn, b_nb, b_line = given("attn", g["L2_gnn_attn"]), given("b_nb", g["L1_gnn_b_nb"]), given("b_line", g["L1_gnn_b_line"])
    we, be = given("we", g["L3_gnn_we"]), given("be", g["L3_gnn_be"])
    out = nc.dram_tensor("out", (N, D), F32, kind="ExternalOutput").ap()
    adjacency_net(nc, x, adj, weights, attn, b_nb, b_line, we, be, out, 0)
    r = run_bass_kernel_spmd(nc, [arrays], core_ids=[0])
    return r.results[0]["out"]
```

```python
from contextlib import ExitStack

import numpy as np

import concourse.bass as bass
from concourse import mybir

ALU = mybir.AluOpType
ACT = mybir.ActivationFunctionType
F32 = mybir.dt.float32
F16 = mybir.dt.float16
BF16 = mybir.dt.bfloat16
F8 = mybir.dt.float8e4
U8 = mybir.dt.uint8
U16 = mybir.dt.uint16
I32 = mybir.dt.int32
U32 = mybir.dt.uint32
AX_X = mybir.AxisListType.X
ABSMAX = bass.bass_isa.ReduceOp.absmax

P = 128
N, D, H = 2048, 256, 8
DH = D // H
T = N // P
K = D // P
CH = 512
C = N // CH
TC = CH // P
NEIGHBORS = 64
EPS = 1e-5
L0_EPS = 1e-8
NEG = -(2.0 ** 120)
SCALING = float(DH) ** -0.5

H_UP = 2.0 ** 11
W_UP = 2.0 ** 13
G_DOWN = 2.0 ** -18
UNIT_UP = 2.0 ** 13
E_UP = 2.0 ** 14
UNIT_DOWN = 0.5 / UNIT_UP ** 2
TINY = 2.0 ** -40
LN2 = float(np.log(2.0))

W0, WNB, WLINE, W2, WQ, WK, WV, WS, WE = range(9)

A_M = 0
A_MT = A_M + T * N
A_SG, A_K4 = A_MT, A_MT + 2 * H * N
A_G = A_MT + 2 * T * N
A_R3 = A_G + T * 2 * (D + 2) * 2
A_UB = A_R3 + 2 * K * N * 2
A_XB = A_UB + 4 * N
A_F = A_XB + 4 * N
A_X = A_F + 24576
A_W = A_X + T * D * 4
A_D = A_W + 16384
A_END = A_D + 2048


def adjacency_net(nc, x, adj, weights, attn, b_nb, b_line, we, be, out, stop):
    with ExitStack() as ctx:
        def sb(name, shape, dt):
            return ctx.enter_context(nc.sbuf_tensor(name, shape, dt))

        def sem(name):
            return ctx.enter_context(nc.semaphore(name))

        arena = sb("arena", [P, A_END], U8)
        SIZE = {F32: 4, F16: 2, BF16: 2, F8: 1, U8: 1, U16: 2, I32: 4, U32: 4}

        def at(offset, shape, dt):
            n = SIZE[dt]
            for s in shape:
                n *= s
            a = arena[:, offset:offset + n]
            if dt is not U8:
                a = a.bitcast(dt)
            if len(shape) == 2:
                a = a.rearrange("p (a b) -> p a b", a=shape[0])
            if len(shape) == 3:
                a = a.rearrange("p (a b c) -> p a b c", a=shape[0], b=shape[1])
            if len(shape) == 4:
                a = a.rearrange("p (a b c d) -> p a b c d", a=shape[0], b=shape[1], c=shape[2])
            return a

        no_edge = at(A_M, [T, N], U8)
        no_edge_T = at(A_MT, [T, N], BF16)
        diag_blocks = at(A_MT, [T, N + P], BF16)[:, :, 0:P]
        G = at(A_G, [T, 2, D + 2], F16)
        xs = at(A_X, [T, D], F32)
        ws0 = at(A_W, [2, K, D], F16)
        ws1 = at(A_W + 2048, [2, K, 2 * D], F16)
        ws2 = at(A_W + 6144, [2, K, D + 2], F16)
        wsq = at(A_W + 8208, [2, K, D], F16)
        wsk = at(A_W + 10256, [2, K, D], F16)
        wsv = at(A_W + 12304, [2, K, D], F16)
        h32 = [at(A_F + 4096 * b, [TC, D], F32) for b in range(2)]
        hn = [at(A_F + 8192 + 4096 * b, [2, TC, D], F16) for b in range(2)]
        hT = [at(A_F + 16384 + 4096 * b, [2, K, CH], F16) for b in range(2)]

        ident = sb("ident", [P, P], BF16)
        ident16 = sb("ident16", [P, P], F16)
        ident32 = sb("ident32", [P, P], F32)
        off_diag = sb("off_diag", [P, P], BF16)
        ones32 = sb("ones32", [P, P], F32)
        ones16 = sb("ones16", [P, P], F16)
        head_bit = sb("head_bit", [P, H, P], BF16)
        wsc = sb("wsc", [P, 6, 9], F32)
        sc = sb("sc", [P, 8], F32)
        w12 = sb("w12", [P, K, 2], F32)
        wec = sb("wec", [P, 1], F32)
        bec = sb("bec", [P, 1], F32)
        st6 = sb("st6", [P, T, 6], F32)
        mv = sb("mv", [P, T, 2], F32)
        cols = sb("cols", [P, 8, T], F32)
        s12 = sb("s12", [P, T, 2], F32)
        tiny = sb("tiny", [P, 16], F32)
        wmax, wpow, wup, kG, kL, kI = (wsc[:, i, :] for i in range(6))
        veps, std, r2, nbias, nsq, ucol, acol, bcol = (cols[:, i, :] for i in range(8))

        psum = ctx.enter_context(nc.psum_tensor("psum", [P, 8, CH], F32))

        def tp(b, dt=F16):
            return psum[:, 2 * b:2 * b + 2, :].rearrange("p a b -> p (a b)").bitcast(dt)

        x_t = x.rearrange("(t p) d -> p t d", p=P)
        out_t = out.rearrange("(t p) d -> p t d", p=P)
        adj_t = adj.rearrange("(t p) j -> p t j", p=P)

        barrier_sem = sem("stage_done")

        def stage_end(eng, k):
            eng.drain().then_inc(barrier_sem, 1)
            eng.wait_ge(barrier_sem, 5 * k)

        wraw = at(A_F, [7, K, D], F32)
        ab = at(A_F + 14336, [2, D], F32)
        wtmp = at(A_F + 16384, [2 * D], F32)
        adjb = [at(o, [N], I32) for o in (A_UB, A_XB, A_R3 + 8192, A_G)]
        bb = [at(A_R3 + 4096 * b, [N], BF16) for b in range(2)]
        diag_save = at(A_D, [T, P], U8)

        w_ld, x_ld = sem("weights_loaded"), sem("x_loaded")
        adj_ld = [sem(f"adj_loaded{b}") for b in range(4)]
        consts_ok, wmax_ok, wall_ok = sem("consts_ok"), sem("weight_max"), sem("weight_max_all")
        bb_ok, m_ok, tp_ok, mt_ok = sem("mask_tile"), sem("mask_kept"), sem("mask_turned"), sem("mask_T_kept")
        wp, m_odd = sem("weight_prep"), sem("mask_kept_odd")
        dg = sem("diagonal")
        gate, gate_sp = sem("act_gate"), sem("sync_gate")

        def load_sync(sp):
            with sp.Fori(0, T // 4) as i:
                for b in range(4):
                    sp.wait_ge(bb_ok, i * 4 + b + 1)
                    sp.sem_inc(gate_sp, 1)
                    if b % 2 == 1:
                        sp.wait_ge(m_odd, i * 2 + b // 2 + 1)
                        sp.sem_inc(gate_sp, 1)
                    sp.dma_start(adjb[b], adj_t[:, bass.ds(i * 4 + b, 1), :]).then_inc(adj_ld[b], 16)

        def load_weights(eng):
            for i, w in enumerate(weights):
                eng.dma_start(wraw[:, i], w.rearrange("(k p) o -> p k o", p=P)).then_inc(w_ld, 16)
            a = attn.rearrange("(a d) o -> (o a) d", a=2)
            for i in range(2):
                eng.dma_start(ab[:, i], a[i].partition_broadcast(P)).then_inc(w_ld, 16)
            for i in range(4):
                eng.dma_start(wec[DH * i:DH * i + DH, :], we.rearrange("o d -> d o")).then_inc(w_ld, 16)
            eng.dma_start(bec[:], be.partition_broadcast(P)).then_inc(w_ld, 16)
            eng.dma_start(xs, x_t).then_inc(x_ld, 16)

        def load_pool(pool):
            nc.gpsimd.memset(ones32[:], 1.0).then_inc(consts_ok, 1)
            pool.wait_ge(consts_ok, 1)
            nc.gpsimd.affine_select(out=ident32[:], in_=ones32[:], pattern=[[-1, P]], compare_op=ALU.is_equal,
                                    fill=0.0, base=0, channel_multiplier=1).then_inc(consts_ok, 1)
            pool.wait_ge(consts_ok, 2)
            nc.gpsimd.tensor_copy(ident[:], ident32[:]).then_inc(consts_ok, 1)
            nc.gpsimd.tensor_copy(ident16[:], ident32[:]).then_inc(consts_ok, 1)
            nc.gpsimd.tensor_copy(ones16[:], ones32[:]).then_inc(consts_ok, 1)
            nc.gpsimd.tensor_scalar(off_diag[:], ident32[:], -1.0, 1.0, ALU.mult, ALU.add).then_inc(consts_ok, 1)
            for h in range(H):
                nc.gpsimd.tensor_scalar(head_bit[:, h], ident32[:], 2.0 ** h, 0.0, ALU.mult, ALU.add
                                        ).then_inc(consts_ok, 1)
            pool.wait_ge(wmax_ok, 1)
            nc.gpsimd.partition_all_reduce(wsc[:, 1, :], wsc[:, 0, :], P, ABSMAX).then_inc(wall_ok, 1)

        def load_tensor(pe):
            pe.wait_ge(consts_ok, 3)
            pe.sem_inc(tp_ok, 2)
            with pe.Fori(0, T // 2) as i:
                for b in range(2):
                    pe.wait_ge(bb_ok, i * 2 + b + 5)
                    pe.wait_ge(mt_ok, i * 2 + b + 1)
                    for j in range(T):
                        last = pe.transpose(tp(b, BF16)[:, P * j:P * j + P], bb[b][:, P * j:P * j + P], ident[:])
                    last.then_inc(tp_ok, 1)

        def load_scalar(act):
            load_weights(act)
            act.sem_inc(mt_ok, 2)
            act.sem_inc(m_ok, 1)
            with act.Fori(0, T // 4) as i:
                for b in range(4):
                    if b % 2 == 0:
                        act.wait_ge(bb_ok, i * 4 + b + 5)
                        act.sem_inc(gate, 1)
                        act.activation(no_edge[:, bass.ds(i * 4 + b, 1), :].rearrange("p a j -> p (a j)"), bb[0],
                                       ACT.Copy).then_inc(m_ok, 1)
                    act.wait_ge(tp_ok, i * 4 + b + 3)
                    act.sem_inc(gate, 1)
                    act.activation(no_edge_T[:, :, bass.ds(i * 512 + b * P, P)],
                                   tp(b % 2, BF16).rearrange("p (j i) -> p j i", j=T), ACT.Copy, scale=NEG
                                   ).then_inc(mt_ok, 1)

        def load_vector(dve):
            count = [0]

            def step(ins):
                count[0] += 1
                ins.then_inc(wp, 1)
                dve.wait_ge(wp, count[0])

            dve.sem_inc(bb_ok, 4)
            dve.sem_inc(m_odd, 2)

            def mask_tiles(first, last):
                for n in range(first, last):
                    i, b = n // 4, n % 4
                    dve.wait_ge(adj_ld[b], i * 16 + 16)
                    dve.wait_ge(tp_ok, n + 1)
                    if b % 2 == 0:
                        dve.wait_ge(m_ok, i * 2 + b // 2 + 1)
                    else:
                        dve.tensor_scalar(no_edge[:, n], adjb[b], 0, None, ALU.is_le).then_inc(m_odd, 1)
                    dve.tensor_scalar(bb[b % 2], adjb[b], 0, None, ALU.is_le).then_inc(bb_ok, 1)
            mask_tiles(0, 4)
            dve.wait_ge(w_ld, 16 * 14)
            step(dve.tensor_reduce(wmax[:, 0:7], wraw.rearrange("p w k o -> p w (k o)"), AX_X, ALU.max,
                                   apply_absolute_value=True))
            mask_tiles(4, 6)
            for k in range(K):
                for a in range(2):
                    step(dve.tensor_tensor_reduce(wtmp[:, 0:D], wraw[:, W2, k], ab[:, a], 1.0, 0.0, ALU.mult,
                                                  ALU.add, w12[:, k, a:a + 1]))
            step(dve.tensor_reduce(wmax[:, WS:WS + 1], w12[:].rearrange("p k a -> p (k a)"), AX_X, ALU.max,
                                   apply_absolute_value=True))
            dve.tensor_reduce(wmax[:, WE:WE + 1], wec[:], AX_X, ALU.max, apply_absolute_value=True
                              ).then_inc(wmax_ok, 1)
            mask_tiles(6, 8)
            dve.wait_ge(wall_ok, 1)
            step(dve.tensor_scalar(sc[:, 0:1], wpow[:, WE:WE + 1], 1.0, None, ALU.mult))
            step(dve.tensor_scalar(kI, wpow, TINY, None, ALU.max))
            step(dve.tensor_scalar(wpow.bitcast(U32), kI.bitcast(U32), 0x7F800000, None, ALU.bitwise_and))
            step(dve.reciprocal(kI, wpow))
            step(dve.tensor_scalar(wup, kI, W_UP, None, ALU.mult))
            step(dve.tensor_scalar(kG, wpow, 1.0 / (W_UP * H_UP * G_DOWN), None, ALU.mult))
            step(dve.tensor_scalar(kL, wpow, 1.0 / (W_UP * H_UP), None, ALU.mult))
            step(dve.tensor_scalar(kI, wup, H_UP * G_DOWN, None, ALU.mult))
            step(dve.tensor_scalar(sc[:, 1:2], wpow[:, WK:WK + 1], SCALING * 512.0, sc[:, 0:1], ALU.mult, ALU.add))
            step(dve.tensor_scalar(sc[:, 3:4].bitcast(U32), sc[:, 1:2].bitcast(U32), 0x7F800000, None,
                                   ALU.bitwise_and))
            step(dve.reciprocal(sc[:, 4:5], sc[:, 3:4]))
            step(dve.tensor_scalar(sc[:, 2:3], sc[:, 4:5], 2.0 ** 14, None, ALU.mult))
            step(dve.tensor_scalar(sc[:, 5:6], sc[:, 2:3], kL[:, WK:WK + 1], SCALING, ALU.mult, ALU.mult))
            step(dve.tensor_scalar(wec[:], wec[:], sc[:, 2:3], None, ALU.mult))
            step(dve.tensor_scalar(bec[:], bec[:], sc[:, 2:3], kI[:, WQ:WQ + 1], ALU.mult, ALU.mult))

            def split_weights(some):
                for w, dst in some:
                    step(dve.tensor_scalar(dst[:, 0], wraw[:, w], wup[:, w:w + 1], None, ALU.mult))
                    step(dve.scalar_tensor_tensor(dst[:, 1], wraw[:, w], wup[:, w:w + 1], dst[:, 0], ALU.mult,
                                                  ALU.subtract))
            mask_tiles(8, 10)
            split_weights(((W0, ws0), (WNB, ws1[:, :, :, 0:D])))
            mask_tiles(10, 12)
            split_weights(((WLINE, ws1[:, :, :, D:]), (W2, ws2[:, :, :, 0:D])))
            mask_tiles(12, 14)
            split_weights(((WQ, wsq), (WK, wsk), (WV, wsv)))
            step(dve.tensor_scalar(ws2[:, 0, :, D:], w12[:], wup[:, WS:WS + 1], None, ALU.mult))
            step(dve.scalar_tensor_tensor(ws2[:, 1, :, D:], w12[:], wup[:, WS:WS + 1], ws2[:, 0, :, D:],
                                          ALU.mult, ALU.subtract))
            mask_tiles(14, 16)
            dve.wait_ge(bb_ok, T + 4)
            step(dve.memset(G[:, :, 0, D:], 1.0))
            step(dve.memset(G[:, :, 1, D:], 0.0))
            dve.wait_ge(x_ld, 16)
            for t in range(T):
                row_stats(dve, fronts[0], t)
            dve.wait_ge(consts_ok, 6 + H)

        def set_diagonal_aside(dve):
            dve.tensor_scalar(diag_save, diag_blocks, 1.0 / NEG, None, ALU.mult).then_inc(dg, 1)
            dve.wait_ge(dg, 1)
            dve.tensor_tensor(diag_blocks, diag_blocks, off_diag[:].unsqueeze(1).to_broadcast([P, T, P]), ALU.mult
                              ).then_inc(dg, 1)

        def row_stats(dve, front, i):
            dve.bn_stats(st6[:, bass.ds(i, 1), :].rearrange("p a d -> p (a d)"),
                         xs[:, bass.ds(i, 1), :].rearrange("p a d -> p (a d)")).then_inc(front.stats, 1)

        class Front:
            def __init__(self, name):
                self.stats = sem(name + "_stats")
                self.h_ok = sem(name + "_h")
                self.split_ok = sem(name + "_split")
                self.turned = sem(name + "_turned")
                self.hT_ok = sem(name + "_hT")
                self.lin_ok = sem(name + "_linear")
                self.post_a = sem(name + "_post_act")
                self.post_v = sem(name + "_post_dve")
                self.std_ok = sem(name + "_std")

            def vector(self, dve):
                dve.wait_ge(self.stats, T)
                for t in range(T):
                    dve.bn_aggr(mv[:, t], st6[:, t]).then_inc(self.stats, 1)
                dve.wait_ge(self.stats, 2 * T)
                dve.tensor_scalar(veps, mv[:, :, 1], EPS, None, ALU.add).then_inc(self.stats, 1)
                dve.wait_ge(self.std_ok, 1)
                dve.reciprocal(nsq, std).then_inc(self.stats, 1)
                dve.wait_ge(self.stats, 2 * T + 2)
                dve.tensor_scalar(r2, nsq, H_UP, None, ALU.mult).then_inc(self.stats, 1)
                dve.wait_ge(self.stats, 2 * T + 3)
                dve.scalar_tensor_tensor(nbias, mv[:, :, 0], -1.0, r2, ALU.mult, ALU.mult).then_inc(self.stats, 1)

                def split(g):
                    dve.wait_ge(self.h_ok, TC * (g + 1))
                    if g >= 2:
                        dve.wait_ge(self.turned, g - 1)
                    dve.tensor_copy(hn[g % 2][:, 0], h32[g % 2]).then_inc(self.split_ok, 1)
                    dve.wait_ge(self.split_ok, 2 * g + 1)
                    dve.tensor_tensor(hn[g % 2][:, 1], h32[g % 2], hn[g % 2][:, 0], ALU.subtract
                                      ).then_inc(self.split_ok, 1)
                split(0)
                split(1)
                split(2)
                self.post_dve(dve, 0)
                split(3)
                for g in range(1, C):
                    self.post_dve(dve, g)

            def scalar(self, act):
                act.wait_ge(self.stats, 2 * T + 1)
                act.activation(std, veps, ACT.Sqrt).then_inc(self.std_ok, 1)
                act.wait_ge(self.stats, 2 * T + 4)

                def relu(g):
                    if g >= 2:
                        act.wait_ge(self.split_ok, 2 * (g - 1))
                    for t in range(TC):
                        i = TC * g + t
                        act.activation(h32[g % 2][:, t], xs[:, i], ACT.Relu, scale=r2[:, i:i + 1],
                                       bias=nbias[:, i:i + 1]).then_inc(self.h_ok, 1)

                def turn(g):
                    act.wait_ge(self.turned, g + 1)
                    if g >= 2:
                        act.wait_ge(self.lin_ok, g - 1)
                    act.activation(hT[g % 2].rearrange("p a b c -> p (a b c)"), tp(g % 2), ACT.Copy
                                   ).then_inc(self.hT_ok, 1)
                relu(0)
                relu(1)
                turn(0)
                relu(2)
                turn(1)
                self.post_act(act, 0)
                relu(3)
                turn(2)
                self.post_act(act, 1)
                turn(3)
                self.post_act(act, 2)
                self.post_act(act, 3)

            def tensor(self, pe):
                def turn(g):
                    pe.wait_ge(self.split_ok, 2 * g + 2)
                    if g >= 2:
                        pe.wait_ge(self.hT_ok, g - 1)
                    for hl in range(2):
                        for k in range(K):
                            for t in range(TC):
                                c = ((hl * K + k) * TC + t) * P
                                last = pe.transpose(tp(g % 2)[:, c:c + P], hn[g % 2][:, hl, t, P * k:P * k + P],
                                                    ident16[:])
                    last.then_inc(self.turned, 1)

                def lin(g):
                    pe.wait_ge(self.hT_ok, g + 1)
                    self.linear(pe, g).then_inc(self.lin_ok, 1)
                turn(0)
                turn(1)
                lin(0)
                turn(2)
                lin(1)
                turn(3)
                lin(2)
                lin(3)

        TERMS = ((0, 0), (0, 1), (1, 0))

        def product(pe, dst, lhs, rhs):
            n = 0
            for a, b in TERMS:
                for k in range(K):
                    last = pe.matmul(dst, lhs(a, k), rhs(b, k), start=(n == 0), stop=(n == len(TERMS) * K - 1))
                    n += 1
            return last

        def lin_bank(t):
            return psum[:, 4 + t, :]

        def linear_rows(w, n, front):
            def linear(pe, g):
                if g >= 1:
                    pe.wait_ge(front().post_a, front().copies * g)
                for t in range(TC):
                    last = product(pe, lin_bank(t)[:, 0:n], lambda hl, k: hT[g % 2][:, hl, k, P * t:P * t + P],
                                   lambda hl, k: w[:, hl, k, 0:n])
                return last
            return linear

        gf = at(A_UB, [T, D], F32)
        WhnT = at(A_R3, [2, K, N], F16)
        u_b = at(A_UB, [N], F32)
        whn32 = [at(A_F + 4096 * b, [TC, D], F32) for b in range(2)]
        whn = [at(A_F + 8192 + 4096 * b, [2, TC, D], F16) for b in range(2)]
        junk = [at(A_R3 + 1024 * b, [D], F32) for b in range(2)]
        sq = acol
        l0b_v, l0b_a, l0b_t = sem("l0_unit_rows"), sem("l0_unit_kept"), sem("l0_unit_turned")
        l0n, l0n_a, l0u = sem("l0_norms"), sem("l0_sqrt"), sem("l0_u")
        l0u_a = sem("l0_u_kept")

        def l0_post_act(act, g):
            f = fronts[0]
            act.wait_ge(f.lin_ok, g + 1)
            act.activation(gf[:, TC * g:TC * g + TC], psum[:, 4:8, 0:D], ACT.Copy, scale=G_DOWN).then_inc(f.post_a, 1)

        def l0_post_dve(dve, g):
            f = fronts[0]
            dve.wait_ge(f.post_a, g + 1)
            i = TC * g
            dve.tensor_copy(G[:, i:i + TC, 0, 0:D], gf[:, i:i + TC]).then_inc(f.post_v, 1)
            dve.wait_ge(f.post_v, 2 * g + 1)
            dve.tensor_tensor(G[:, i:i + TC, 1, 0:D], gf[:, i:i + TC], G[:, i:i + TC, 0, 0:D], ALU.subtract
                              ).then_inc(f.post_v, 1)
            for t in range(i, i + TC):
                if t >= 2:
                    dve.wait_ge(l0n, t - 1)
                dve.tensor_tensor_reduce(junk[t % 2], gf[:, t], gf[:, t], 1.0, 0.0, ALU.mult, ALU.add, sq[:, t:t + 1]
                                         ).then_inc(l0n, 1)

        def l0_unit_vector(dve):
            dve.wait_ge(l0n, T)
            dve.tensor_scalar(veps, sq, 2.0 ** -62, None, ALU.max).then_inc(l0n, 1)
            dve.tensor_scalar(tiny[:, 2:3], kG[:, W0:W0 + 1].bitcast(I32), 2.0 ** -23, -127.0, ALU.mult, ALU.add
                              ).then_inc(l0n, 1)
            set_diagonal_aside(dve)
            dve.wait_ge(l0n_a, 2)
            dve.reciprocal(ucol, std).then_inc(l0n, 1)
            dve.wait_ge(l0n, T + 3)
            dve.tensor_scalar(tiny[:, 3:4], tiny[:, 2:3], LN2 / 2, None, ALU.mult).then_inc(l0n, 1)
            dve.wait_ge(l0n, T + 4)
            dve.tensor_scalar(acol, bcol, 0.25, tiny[:, 3:4], ALU.mult, ALU.add).then_inc(l0n, 1)
            dve.wait_ge(l0n, T + 5)
            dve.tensor_scalar(bcol, acol, -0.5 * float(np.log(L0_EPS)), None, ALU.add).then_inc(l0n, 1)
            for g in range(C):
                b = g % 2
                for t in range(TC):
                    i = TC * g + t
                    dve.tensor_scalar(whn32[b][:, t], gf[:, i], ucol[:, i:i + 1], UNIT_UP, ALU.mult, ALU.mult
                                      ).then_inc(l0b_v, 1)
                if g >= 2:
                    dve.wait_ge(l0b_t, g - 1)
                dve.wait_ge(l0b_v, 6 * g + 4)
                dve.tensor_copy(whn[b][:, 0], whn32[b]).then_inc(l0b_v, 1)
                dve.wait_ge(l0b_v, 6 * g + 5)
                dve.tensor_tensor(whn[b][:, 1], whn32[b], whn[b][:, 0], ALU.subtract).then_inc(l0b_v, 1)
                dve.wait_ge(l0b_v, 6 * g + 6)

        def l0_unit_tensor(pe):
            pe.wait_ge(l0n, T + 5)
            for g in range(C):
                for t in range(TC):
                    i = TC * g + t
                    last = pe.matmul(psum[:, 4 + g, P * t:P * t + P], acol[:, i:i + 1].to_broadcast([P, P]), ident32[:],
                                     start=True, stop=True)
                last.then_inc(l0u, 1)
            for g in range(C):
                pe.wait_ge(l0b_v, 6 * g + 6)
                if g >= 2:
                    pe.wait_ge(l0b_a, g - 1)
                for hl in range(2):
                    for k in range(K):
                        for t in range(TC):
                            c = ((hl * K + k) * TC + t) * P
                            last = pe.transpose(tp(g % 2)[:, c:c + P], whn[g % 2][:, hl, t, P * k:P * k + P],
                                                ident16[:])
                last.then_inc(l0b_t, 1)

        def l0_unit_scalar(act):
            act.wait_ge(l0n, T + 1)
            act.activation(std, veps, ACT.Sqrt).then_inc(l0n_a, 1)
            act.activation(bcol, veps, ACT.Ln).then_inc(l0n_a, 1)
            for g in range(C):
                act.wait_ge(l0b_t, g + 1)
                act.activation(WhnT[:, :, :, CH * g:CH * g + CH], tp(g % 2).rearrange("p (a b c) -> p a b c", a=2, b=K),
                               ACT.Copy).then_inc(l0b_a, 1)
            for g in range(C):
                act.wait_ge(l0u, g + 1)
                act.wait_ge(l0b_v, 6 * C)
                act.activation(u_b[:, CH * g:CH * g + CH], psum[:, 4 + g, :], ACT.Copy).then_inc(l0u_a, 1)

        den = [at(A_F + 2048 * b, [CH], F32) for b in range(2)]
        sim = [at(A_F + 4096 + 2048 * b, [CH], F32) for b in range(2)]
        num = [at(A_F + 8192 + 2048 * b, [CH], F32) for b in range(2)]
        num_hl = [at(A_F + 12288 + 2048 * b, [2, CH], F16) for b in range(4)]
        el_tmp = at(A_F + 20480, [D + 2], F32)
        el_tmp2 = at(A_F + 20480 + 1040, [D], F32)
        el_tmp3 = at(A_F + 20480 + 2064, [D], F32)

        class Attention:

            def __init__(self, name):
                self.scores = sem(name + "_scores")
                self.den = sem(name + "_den")
                self.rec = sem(name + "_rec")
                self.sim = sem(name + "_sim")
                self.num = sem(name + "_num")
                self.hi = sem(name + "_hi")
                self.lo = sem(name + "_lo")
                self.summed = sem(name + "_summed")
                self.taken = sem(name + "_taken")
                self.ep = sem(name + "_epilogue")
                self.ep_a = sem(name + "_elu")

        A0 = Attention("l0")

        def av_step(pe, A, c, j, bank=0):
            n = c * T + j
            pe.wait_ge(A.lo, n + 4)
            if j == 0:
                pe.wait_ge(A.taken, c + 1)
            e = num_hl[j % 4]
            for t in range(TC):
                o = psum[:, bank + t, 0:D + 1]
                pe.matmul(o, e[:, 0, P * t:P * t + P], G[:, j, 0, 0:D + 1], start=(j == 0), stop=False)
                pe.matmul(o, e[:, 0, P * t:P * t + P], G[:, j, 1, 0:D + 1], start=False, stop=False)
                last = pe.matmul(o, e[:, 1, P * t:P * t + P], G[:, j, 0, 0:D + 1], start=False, stop=(j == T - 1))
            last.then_inc(A.summed, 1)

        sums0 = at(A_XB, [TC, D + 1], F32)

        def l0_chunks(eng, chunk):
            chunk(0, True, False)
            with eng.Fori(1, C - 1) as c:
                chunk(c, False, False)
            chunk(C - 1, False, True)

        def l0_tensor(pe):
            A = A0
            pe.sem_inc(A.scores, 3)
            pe.sem_inc(A.summed, 3)

            def scores(c, j):
                pe.wait_ge(A.rec, c * T + j + 1)
                dst = psum[:, 4 + j % 4, :]
                m = 0
                for a, b in TERMS:
                    for k in range(K):
                        m += 1
                        last = pe.matmul(dst, WhnT[:, a, k, P * j:P * j + P], WhnT[:, b, k, bass.ds(c * CH, CH)],
                                         start=(m == 1), stop=(m == 3 * K))
                last.then_inc(A.scores, 1)

            def chunk(c, first, last):
                for j in range(T):
                    if j + 2 < T:
                        scores(c, j + 2)
                    elif not last:
                        scores(c + 1, j + 2 - T)
                    av_step(pe, A, c, j)
            scores(0, 0)
            scores(0, 1)
            l0_chunks(pe, chunk)

        def l0_scalar(act):
            A = A0
            for s in (A.den, A.num, A.hi):
                act.sem_inc(s, 3)
            act.sem_inc(A.taken, 1)

            def den_(c, j):
                act.wait_ge(A.rec, c * T + j + 2)
                act.sem_inc(gate, 1)
                act.activation(den[j % 2], u_b[:, bass.ds(c * CH, CH)], ACT.Tanh, bias=bcol[:, j:j + 1]
                               ).then_inc(A.den, 1)

            def take(c):
                act.wait_ge(A.summed, c * T + T + 3)
                act.wait_ge(A.ep, c * TC * 3 + 1)
                act.activation(sums0, psum[:, 0:TC, 0:D + 1], ACT.Copy).then_inc(A.taken, 1)

            def chunk(c, first, last):
                for j in range(T):
                    n = c * T + j
                    act.wait_ge(A.sim, n + 4)
                    act.wait_ge(A.lo, n + 2)
                    act.activation(num[j % 2], sim[j % 2], ACT.Exp, scale=UNIT_DOWN).then_inc(A.num, 1)
                    act.wait_ge(A.summed, n + 1)
                    act.activation(num_hl[j % 4][:, 0], sim[j % 2], ACT.Exp, scale=UNIT_DOWN).then_inc(A.hi, 1)
                    if j == 0 and not first:
                        take(c - 1)
                    if j + 2 < T:
                        den_(c, j + 2)
                    elif not last:
                        den_(c + 1, j + 2 - T)
            den_(0, 0)
            den_(0, 1)
            l0_chunks(act, chunk)
            take(C - 1)

        def l0_vector(dve):
            A = A0
            for s in (A.rec, A.sim, A.lo):
                dve.sem_inc(s, 3)
            dve.sem_inc(A.ep, 1)

            def finish(c, part):
                t, k = part // 3, part % 3
                i = c * TC + t
                if part == 0:
                    dve.wait_ge(A.taken, c + 2)
                if k == 0 and t:
                    dve.wait_ge(A.ep, i * 3 + 1)
                    row_stats(dve, fronts[1], i - 1)
                if t == TC:
                    return
                dve.wait_ge(A.ep, i * 3 + k + 1)
                if k == 0:
                    dve.reciprocal(tiny[:, 0:1], sums0[:, t, D:D + 1]).then_inc(A.ep, 1)
                if k == 1:
                    dve.tensor_scalar(tiny[:, 1:2], tiny[:, 0:1], kG[:, W0:W0 + 1], None, ALU.mult).then_inc(A.ep, 1)
                if k == 2:
                    x_i = xs[:, bass.ds(i, 1), :].rearrange("p a d -> p (a d)")
                    dve.scalar_tensor_tensor(x_i, sums0[:, t, 0:D], tiny[:, 1:2], x_i, ALU.mult, ALU.add
                                             ).then_inc(A.ep, 1)

            def chunk(c, first, last):
                def lo_(j):
                    n = c * T + j
                    dve.wait_ge(A.hi, n + 4)
                    dve.tensor_tensor(num_hl[j % 4][:, 1], num[j % 2], num_hl[j % 4][:, 0], ALU.subtract
                                      ).then_inc(A.lo, 1)
                for j in range(T):
                    n = c * T + j
                    dve.wait_ge(A.den, n + 4)
                    dve.wait_ge(A.scores, n + 4)
                    dve.wait_ge(A.hi, n + 2)
                    dve.scalar_tensor_tensor(sim[j % 2], den[j % 2], 1.0, psum[:, 4 + j % 4, :],
                                             ALU.add, ALU.mult).then_inc(A.rec, 1)
                    dve.wait_ge(A.rec, n + 4)
                    dve.tensor_tensor(sim[j % 2], sim[j % 2], no_edge_T[:, j, bass.ds(c * CH, CH)], ALU.add
                                      ).then_inc(A.sim, 1)
                    if j >= 1:
                        lo_(j - 1)
                    if j >= 2 and j < 15 and not first:
                        finish(c - 1, j - 2)
                lo_(T - 1)
            l0_chunks(dve, chunk)
            for part in range(3 * TC + 1):
                finish(C - 1, part)

        class Spread:
            def __init__(self, name, bank):
                self.bank, self.out, self.kept = bank, sem(name + "_out"), sem(name + "_kept")

            def tensor(self, pe, col):
                for g in range(C):
                    for t in range(TC):
                        last = pe.matmul(psum[:, self.bank + g, P * t:P * t + P],
                                         col(TC * g + t).to_broadcast([P, P]), ident32[:], start=True, stop=True)
                    last.then_inc(self.out, 1)

            def scalar(self, act, dst):
                for g in range(C):
                    act.wait_ge(self.out, g + 1)
                    act.activation(dst[:, CH * g:CH * g + CH], psum[:, self.bank + g, :], ACT.Copy
                                   ).then_inc(self.kept, 1)

        gfb = [at(A_UB + 4096 * b, [TC, D], F32) for b in range(2)]
        zline = at(A_XB, [TC, D], F32)
        b_rows = at(A_XB + 4096, [2, D], F32)
        z_t = at(A_XB + 6144, [D], F32)
        b_ld = sem("bias_loaded")

        def l1_load(sp):
            sp.dma_start(b_rows[:, 0], b_nb.partition_broadcast(P)).then_inc(b_ld, 16)
            sp.dma_start(b_rows[:, 1], b_line.partition_broadcast(P)).then_inc(b_ld, 16)

        def split_post_act(i):
            def post(act, g):
                f = fronts[i]
                act.wait_ge(f.lin_ok, g + 1)
                if g >= 2:
                    act.wait_ge(f.post_v, f.per_v * (g - 1))
                act.activation(gfb[g % 2], psum[:, 4:8, 0:D], ACT.Copy, scale=G_DOWN).then_inc(f.post_a, 1)
                if i == 1:
                    if g >= 1:
                        act.wait_ge(f.post_v, f.per_v * g)
                    act.activation(zline, psum[:, 4:8, D:2 * D], ACT.Identity, scale=kL[:, WLINE:WLINE + 1]
                                   ).then_inc(f.post_a, 1)
                if i == 2:
                    act.activation(s12[:, TC * g:TC * g + TC, :], psum[:, 4:8, D:D + 2], ACT.Identity,
                                   scale=kL[:, WS:WS + 1]).then_inc(f.post_a, 1)
            return post

        def split_post_dve(i):
            def post(dve, g):
                f = fronts[i]
                n, r = f.per_v * g, TC * g
                dve.wait_ge(f.post_a, f.copies * g + 1)
                dve.tensor_copy(G[:, r:r + TC, 0, 0:D], gfb[g % 2]).then_inc(f.post_v, 1)
                dve.wait_ge(f.post_v, n + 1)
                dve.tensor_tensor(G[:, r:r + TC, 1, 0:D], gfb[g % 2], G[:, r:r + TC, 0, 0:D], ALU.subtract
                                  ).then_inc(f.post_v, 1)
                if i == 1:
                    if g == 0:
                        dve.wait_ge(b_ld, 32)
                    dve.wait_ge(f.post_a, f.copies * g + 2)
                    dve.tensor_tensor(zline, zline, b_rows[:, 1:2, :].to_broadcast([P, TC, D]), ALU.add
                                      ).then_inc(f.post_v, 1)
                    dve.wait_ge(f.post_v, n + 3)
                    dve.scalar_tensor_tensor(zline, zline, 0.01, zline, ALU.mult, ALU.max).then_inc(f.post_v, 1)
                    dve.wait_ge(f.post_v, n + 4)
                    dve.tensor_tensor(xs[:, r:r + TC], xs[:, r:r + TC], zline, ALU.add).then_inc(f.post_v, 1)
                    dve.wait_ge(f.post_v, n + 5)
            return post

        edge = [at(A_F + 4096 * b, [N], BF16) for b in range(2)]
        run = [at(A_F + 8192 + 4112 * b, [N + 2], BF16) for b in range(2)]
        keep = [at(A_R3 + 4096 * b, [N], BF16) for b in range(2)]
        keepT = [at(A_R3 + 8192 + 4096 * b, [T, P], BF16) for b in range(2)]
        cap = at(A_UB, [N], BF16)
        e_ok, run_ok, keep_ok = sem("l1_edges"), sem("l1_count"), sem("l1_keep")
        kt_ok, ktc_ok, agg_ok = sem("l1_keep_turned"), sem("l1_keepT"), sem("l1_summed")
        l1_c, l1_share, l1_out = sem("l1_consts"), sem("l1_share"), sem("l1_out")
        rate, some = ucol, std

        def need(eng, s, v):
            if not isinstance(v, int) or v > 0:
                eng.wait_ge(s, v)

        def has(n, delay):
            return not isinstance(n, int) or 0 <= n - delay < T

        def l1_steps(eng, step):
            for n in range(4):
                step(n, n % 2)
            with eng.Fori(2, T // 2 - 1) as i:
                step(i * 2, 0)
                step(i * 2 + 1, 1)
            for n in range(T - 2, T + 3):
                step(n, n % 2)

        def l1_scalar(act):
            def edges(n, b):
                need(act, run_ok, n - 1)
                act.sem_inc(gate, 1)
                act.activation(edge[b], no_edge[:, bass.ds(n, 1), :].rearrange("p a j -> p (a j)"), ACT.Copy,
                               scale=-1.0, bias=1.0).then_inc(e_ok, 1)

            def step(n, b):
                if has(n, -1):
                    edges(n + 1, 1 - b)
                if has(n, 1):
                    need(act, kt_ok, n)
                    need(act, agg_ok, n - 2)
                    act.activation(keepT[1 - b].rearrange("p j i -> p (j i)"), tp(1 - b, BF16), ACT.Copy
                                   ).then_inc(ktc_ok, 1)
            edges(0, 0)
            l1_steps(act, step)

        def l1_vector(dve):
            def step(n, b):
                total = run[b][:, N:N + 1]
                if has(n, 0):
                    need(dve, e_ok, n + 1)
                    need(dve, keep_ok, n - 1)
                    need(dve, l1_share, n * 4 - 4)
                    dve.tensor_tensor_scan(run[b][:, 1:N + 1], edge[b], cap, 0.0, ALU.add, ALU.min
                                           ).then_inc(run_ok, 1)
                if has(n, 3):
                    need(dve, agg_ok, n - 2)
                    need(dve, l1_share, n * 4 - 8)
                    need(dve, l1_out, n * 3 - 9)
                    dve.scalar_tensor_tensor(z_t, psum[:, 5 - b, 0:D], rate[:, bass.ds(n - 3, 1)], b_rows[:, 0],
                                             ALU.mult, ALU.add).then_inc(l1_out, 1)
                if has(n, 0):
                    need(dve, run_ok, n + 1)
                    dve.tensor_scalar(tiny[:, 0:1], total, 1.0, None, ALU.max).then_inc(l1_share, 1)
                if has(n, 3):
                    need(dve, l1_out, n * 3 - 8)
                    dve.scalar_tensor_tensor(z_t, z_t, 0.01, z_t, ALU.mult, ALU.max).then_inc(l1_out, 1)
                if has(n, 0):
                    need(dve, l1_share, n * 4 + 1)
                    dve.reciprocal(tiny[:, 1:2], tiny[:, 0:1]).then_inc(l1_share, 1)
                if has(n, 3):
                    x_i = xs[:, bass.ds(n - 3, 1), :].rearrange("p a d -> p (a d)")
                    need(dve, l1_out, n * 3 - 7)
                    dve.scalar_tensor_tensor(x_i, z_t, some[:, bass.ds(n - 3, 1)], x_i, ALU.mult, ALU.add
                                             ).then_inc(l1_out, 1)
                if has(n, 0):
                    need(dve, l1_share, n * 4 + 2)
                    dve.tensor_scalar(rate[:, bass.ds(n, 1)], tiny[:, 1:2], kG[:, WNB:WNB + 1], None, ALU.mult
                                      ).then_inc(l1_share, 1)
                    dve.tensor_scalar(some[:, bass.ds(n, 1)], total, 1.0, None, ALU.min).then_inc(l1_share, 1)
                if has(n, 3):
                    need(dve, l1_out, n * 3 - 6)
                    row_stats(dve, fronts[2], n - 3)
            dve.memset(cap, float(NEIGHBORS)).then_inc(l1_c, 1)
            for b in range(2):
                dve.memset(run[b][:, 0:1], 0.0).then_inc(l1_c, 1)
            dve.wait_ge(l1_c, 3)
            l1_steps(dve, step)

        def l1_pool(pool):
            def step(n, b):
                if has(n, 0):
                    need(pool, run_ok, n + 1)
                    need(pool, kt_ok, n - 1)
                    nc.gpsimd.tensor_tensor(keep[b], run[b][:, 1:N + 1], run[b][:, 0:N], ALU.subtract
                                            ).then_inc(keep_ok, 1)
            l1_steps(pool, step)

        def l1_tensor(pe):
            def step(n, b):
                if has(n, 1):
                    need(pe, keep_ok, n)
                    need(pe, ktc_ok, n - 2)
                    for j in range(T):
                        last = pe.transpose(tp(1 - b, BF16)[:, P * j:P * j + P], keep[1 - b][:, P * j:P * j + P],
                                            ident[:])
                    last.then_inc(kt_ok, 1)
                if has(n, 2):
                    need(pe, ktc_ok, n - 1)
                    need(pe, l1_out, n * 3 - 11)
                    for j in range(T):
                        for hl in range(2):
                            last = pe.matmul(psum[:, 4 + b, 0:D], keepT[b][:, j], G[:, j, hl, 0:D],
                                             start=(j == 0 and hl == 0), stop=(j == T - 1 and hl == 1))
                    last.then_inc(agg_ok, 1)
            l1_steps(pe, step)

        s2_b = at(A_UB, [N], F32)
        a_b = at(A_R3, [N], F32)
        b_b = at(A_R3 + 8192, [N], F32)
        colsum = at(A_XB, [D + 2], F32)
        mneg = [at(A_F + 4096 * b, [N], BF16) for b in range(2)]
        mjunk = [at(A_F + 8192 * (b + 1), [N], F32) for b in range(2)]
        mxcol, s2fifth, empty = nsq, r2, nbias
        spread_s2, spread_a, spread_b = Spread("l2_s2", 4), Spread("l2_a", 4), Spread("l2_b", 0)
        mneg_ok, mx_ok, l2p, cs_ok, csk_ok = (sem("l2_mneg"), sem("l2_max"), sem("l2_cols"), sem("l2_colsum"),
                                              sem("l2_colsum_kept"))

        def l2_pre_vector(dve):
            dve.wait_ge(spread_s2.kept, C)
            for t in range(T):
                dve.wait_ge(mneg_ok, t + 1)
                if t >= 2:
                    dve.wait_ge(mx_ok, t - 1)
                dve.tensor_tensor_reduce(mjunk[t % 2], mneg[t % 2], s2_b, 1.0, 2 * NEG, ALU.add, ALU.max,
                                         mxcol[:, t:t + 1]).then_inc(mx_ok, 1)
            dve.wait_ge(mx_ok, T)
            count = [0]

            def step(ins):
                count[0] += 1
                ins.then_inc(l2p, 1)
                dve.wait_ge(l2p, count[0])
            s1 = s12[:, :, 0]
            step(dve.tensor_tensor(acol, s1, mxcol, ALU.add))
            step(dve.scalar_tensor_tensor(bcol, acol, 0.2, acol, ALU.mult, ALU.max))
            step(dve.tensor_tensor(acol, s1, bcol, ALU.subtract))
            step(dve.scalar_tensor_tensor(bcol, s1, 0.2, bcol, ALU.mult, ALU.subtract))
            step(dve.tensor_scalar(empty, mxcol, 0.5 * NEG, None, ALU.is_lt))
            step(dve.tensor_scalar(s2fifth, s12[:, :, 1], 0.2, None, ALU.mult))

        def l2_pre_tensor(pe):
            spread_s2.tensor(pe, lambda i: s12[:, i, 1:2])
            for j in range(T):
                for hl in range(2):
                    last = pe.matmul(psum[:, 0, 0:D + 1], ones16[:], G[:, j, hl, 0:D + 1],
                                     start=(j == 0 and hl == 0), stop=(j == T - 1 and hl == 1))
            last.then_inc(cs_ok, 1)
            pe.wait_ge(spread_s2.kept, C)
            pe.wait_ge(l2p, 4)
            spread_a.tensor(pe, lambda i: acol[:, i:i + 1])
            pe.wait_ge(csk_ok, 1)
            spread_b.tensor(pe, lambda i: bcol[:, i:i + 1])

        def l2_pre_scalar(act):
            spread_s2.scalar(act, s2_b)
            for t in range(T):
                if t >= 2:
                    act.wait_ge(mx_ok, t - 1)
                act.activation(mneg[t % 2], no_edge[:, t], ACT.Copy, scale=NEG).then_inc(mneg_ok, 1)
            act.wait_ge(cs_ok, 1)
            act.activation(colsum[:, 0:D + 1], psum[:, 0, 0:D + 1], ACT.Copy).then_inc(csk_ok, 1)
            spread_a.scalar(act, a_b)
            spread_b.scalar(act, b_b)

        A2 = Attention("l2")
        nums = num + [at(A_XB + 4096 + 2048 * b, [CH], F32) for b in range(2)]

        def l2_tensor(pe):
            pe.sem_inc(A2.summed, 3)
            with pe.Fori(0, C // 2) as i:
                for half in range(2):
                    for j in range(T):
                        av_step(pe, A2, i * 2 + half, j, 4 * half)

        def l2_scalar(act):
            A = A2
            for s in (A.den, A.num, A.hi):
                act.sem_inc(s, 3)

            def chunk(c, half):
                def fifth(j):
                    act.wait_ge(A.rec, c * T + j + 2)
                    act.sem_inc(gate, 1)
                    act.activation(den[j % 2], b_b[:, bass.ds(c * CH, CH)], ACT.Identity, bias=s2fifth[:, j:j + 1]
                                   ).then_inc(A.den, 1)
                fifth(0)
                fifth(1)
                for j in range(T):
                    n = c * T + j
                    if half >= 0 and j % 4 == 3:
                        elu(c * TC - TC + j // 4)
                    act.wait_ge(A.sim, n + 4)
                    act.wait_ge(A.lo, n + 1)
                    act.activation(nums[j % 4], sim[j % 2], ACT.Exp).then_inc(A.num, 1)
                    act.wait_ge(A.num, n + 4)
                    act.wait_ge(A.summed, n + 1)
                    act.activation(num_hl[j % 4][:, 0], nums[j % 4], ACT.Copy, scale=E_UP).then_inc(A.hi, 1)
                    if j + 2 < T:
                        fifth(j + 2)

            def elu(i):
                act.wait_ge(A.ep, i * 7 + 7)
                act.activation(el_tmp3, el_tmp2, ACT.Exp).then_inc(A.ep_a, 1)
            l2_chunks(act, chunk)
            for t in range(TC):
                elu(T - TC + t)

        def l2_chunks(eng, chunk):
            chunk(0, -1)
            chunk(1, 1)
            with eng.Fori(1, C // 2) as i:
                chunk(i * 2, 0)
                chunk(i * 2 + 1, 1)

        num_up, gate_p = sem("l2_num_scaled"), sem("pool_gate")

        def l2_pool(pool):
            A = A2
            pool.sem_inc(A.lo, 3)
            with pool.Fori(0, C) as c:
                for j in range(T):
                    pool.wait_ge(A.hi, c * T + j + 4)
                    pool.sem_inc(gate_p, 1)
                    nc.gpsimd.tensor_scalar(nums[j % 4], nums[j % 4], E_UP, 0.0, ALU.mult, ALU.add
                                            ).then_inc(num_up, 1)
                    pool.wait_ge(num_up, c * T + j + 1)
                    nc.gpsimd.tensor_tensor(num_hl[j % 4][:, 1], nums[j % 4], num_hl[j % 4][:, 0], ALU.subtract
                                            ).then_inc(A.lo, 1)

        def l2_vector(dve):
            A = A2
            for s in (A.rec, A.sim):
                dve.sem_inc(s, 3)
            dve.sem_inc(A.taken, 2)
            dve.sem_inc(A.ep, 2)

            def finish(i, t, bank):
                o = psum[:, bank + t, 0:D + 1]
                k0 = i * 7 + 2
                x_i = xs[:, bass.ds(i, 1), :].rearrange("p a d -> p (a d)")

                def a():
                    dve.wait_ge(A.ep, k0)
                    dve.scalar_tensor_tensor(el_tmp[:, 0:D + 1], colsum[:, 0:D + 1], empty[:, bass.ds(i, 1)], o,
                                             ALU.mult, ALU.add).then_inc(A.ep, 1)
                    if t == TC - 1:
                        dve.wait_ge(A.ep, k0 + 1)
                        dve.sem_inc(A.taken, 1)
                    dve.wait_ge(A.ep, k0 + 1)
                    dve.reciprocal(tiny[:, 0:1], el_tmp[:, D:D + 1]).then_inc(A.ep, 1)

                def b():
                    dve.wait_ge(A.ep, k0 + 2)
                    dve.tensor_scalar(tiny[:, 1:2], tiny[:, 0:1], kG[:, W2:W2 + 1], None, ALU.mult).then_inc(A.ep, 1)
                    dve.wait_ge(A.ep, k0 + 3)
                    dve.tensor_scalar(el_tmp[:, 0:D], el_tmp[:, 0:D], tiny[:, 1:2], None, ALU.mult
                                      ).then_inc(A.ep, 1)

                def c():
                    dve.wait_ge(A.ep, k0 + 4)
                    dve.tensor_scalar(el_tmp2, el_tmp[:, 0:D], 0.0, None, ALU.min).then_inc(A.ep, 1)
                    dve.wait_ge(A.ep, k0 + 5)
                    dve.scalar_tensor_tensor(el_tmp[:, 0:D], el_tmp[:, 0:D], 0.0, x_i, ALU.max, ALU.add
                                             ).then_inc(A.ep, 1)

                def d():
                    dve.wait_ge(A.ep, k0 + 6)
                    dve.wait_ge(A.ep_a, i + 1)
                    dve.scalar_tensor_tensor(x_i, el_tmp3, -1.0, el_tmp[:, 0:D], ALU.add, ALU.add).then_inc(A.ep, 1)
                    dve.wait_ge(A.ep, k0 + 7)
                    row_stats(dve, fronts[3], i)
                return a, b, c, d

            def chunk(c, half):
                for j in range(T):
                    n = c * T + j
                    dve.wait_ge(A.den, n + 4)
                    dve.wait_ge(A.num, n + 2)
                    dve.scalar_tensor_tensor(sim[j % 2], a_b[:, bass.ds(c * CH, CH)], s12[:, j, 1:2], den[j % 2],
                                             ALU.add, ALU.max).then_inc(A.rec, 1)
                    if half >= 0:
                        if j == 0:
                            dve.wait_ge(A.summed, c * T + 3)
                        parts = finish(c * TC - TC + j // 4, j // 4, 4 * (1 - half))
                        if j % 4 < 3:
                            if j % 4 == 0 and j:
                                finish(c * TC - TC + j // 4 - 1, j // 4 - 1, 4 * (1 - half))[3]()
                            parts[j % 4]()
                    dve.wait_ge(A.rec, n + 4)
                    dve.tensor_tensor(sim[j % 2], sim[j % 2],
                                      no_edge_T[:, j, bass.ds(c * CH, CH)], ALU.add
                                      ).then_inc(A.sim, 1)
                if half >= 0:
                    finish(c * TC - 1, TC - 1, 4 * (1 - half))[3]()
            l2_chunks(dve, chunk)
            dve.wait_ge(A.summed, C * T + 3)
            for t in range(TC):
                for part in finish(T - TC + t, t, 4):
                    part()

        q_c = at(A_SG, [K, 2, N], F16)
        k_c = at(A_SG + 16384, [K, 2, N], F16)
        q4 = at(A_R3, [H, N], F16)
        k4 = at(A_K4, [H, N], F16)
        q_lin = sem("f3_qk_linear")
        vf = zline

        def l3_linear(pe, g):
            f = fronts[3]
            if g >= 1:
                pe.wait_ge(f.post_a, 3 * g)
            for w, bank in ((wsq, 4), (wsk, 6)):
                for d in range(K):
                    last = product(pe, psum[:, bank + d, :], lambda hl, k: w[:, hl, k, P * d:P * d + P],
                                   lambda hl, k: hT[g % 2][:, hl, k])
            last.then_inc(q_lin, 1)
            pe.wait_ge(f.post_a, 3 * g + 1)
            for t in range(TC):
                last = product(pe, psum[:, 4 + t // 2, D * (t % 2):D * (t % 2) + D],
                               lambda hl, k: hT[g % 2][:, hl, k, P * t:P * t + P], lambda hl, k: wsv[:, hl, k])
            return last

        def l3_post_act(act, g):
            f = fronts[3]
            act.wait_ge(q_lin, g + 1)
            if g >= 1:
                act.wait_ge(f.post_v, 6 * g)
            act.activation(gfb[0].rearrange("p t d -> p (t d)"), psum[:, 4:6, :].rearrange("p a b -> p (a b)"),
                           ACT.Copy, scale=-G_DOWN).then_inc(f.post_a, 1)
            act.activation(gfb[1].rearrange("p t d -> p (t d)"), psum[:, 6:8, :].rearrange("p a b -> p (a b)"),
                           ACT.Identity, scale=sc[:, 5:6], bias=wec[:, 0:1]).then_inc(f.post_a, 1)
            act.wait_ge(f.lin_ok, g + 1)
            act.activation(vf.rearrange("p t d -> p (t d)"), psum[:, 4:6, :].rearrange("p a b -> p (a b)"),
                           ACT.Copy, scale=G_DOWN).then_inc(f.post_a, 1)

        def l3_post_dve(dve, g):
            f = fronts[3]
            r = TC * g
            for i, (src, dst) in enumerate((
                    (gfb[0].rearrange("p t d -> p (t d)").rearrange("p (a b) -> p a b", a=K),
                     lambda hl: q_c[:, :, hl, CH * g:CH * g + CH]),
                    (gfb[1].rearrange("p t d -> p (t d)").rearrange("p (a b) -> p a b", a=K),
                     lambda hl: k_c[:, :, hl, CH * g:CH * g + CH]),
                    (vf, lambda hl: G[:, r:r + TC, hl, 0:D]))):
                dve.wait_ge(f.post_a, 3 * g + i + 1)
                dve.tensor_copy(dst(0), src).then_inc(f.post_v, 1)
                dve.wait_ge(f.post_v, 6 * g + 2 * i + 1)
                dve.tensor_tensor(dst(1), src, dst(0), ALU.subtract).then_inc(f.post_v, 1)

        x_save = nc.dram_tensor("x_save", (N, D), F32, kind="Internal").ap().rearrange("(t p) d -> p t d", p=P)
        lay_ld, lay_late, xs_ld = sem("l3_rows_laid"), sem("l3_rows_laid_late"), sem("l3_x_saved")

        qk_dram = nc.dram_tensor("qk_rows", (2, 2, K * P, N), F16, kind="Internal").ap()
        qk_saved = sem("l3_qk_saved")

        def rows_of_heads(eng, dst, which, h0, h1, r, hl, cols, done):
            eng.dma_start(dst[DH * r:DH * r + DH, h0:h1, cols],
                          qk_dram[which, hl, DH * h0:DH * h1, cols].rearrange("(h p) c -> p h c", p=DH)
                          ).then_inc(done, 16)

        def l3_lay_sync(sp):
            for g in range(C):
                cols = slice(CH * g, CH * g + CH)
                for i, c in ((1, k_c), (0, q_c)):
                    sp.wait_ge(fronts[3].post_v, 6 * g + (2, 4)[i])
                    for k in range(K):
                        sp.dma_start(qk_dram[i, :, P * k:P * k + P, cols].rearrange("l p c -> p l c"), c[:, k, :, cols]
                                     ).then_inc(qk_saved, 16)
                sp.wait_ge(qk_saved, 16 * 4 * (g + 1))
                for r in range(4):
                    rows_of_heads(sp, q4, 0, 0, H // 2, r, r // 2, cols, lay_ld)
                    rows_of_heads(sp, k4, 1, 0, H, r, r % 2, cols, lay_ld)
                if g == 0:
                    sp.dma_start(x_save, xs).then_inc(xs_ld, 16)
            sp.wait_ge(xs_ld, 16)

        HB = 2 * CH
        SLOTS = [(0, 0)] + [s for h in range(1, H) for s in ((h, 0), (h - 1, 1))] + [(H - 1, 1)]
        FIRST, SECOND = ({h: SLOTS.index((h, q)) for h in range(H)} for q in range(2))
        m3 = [at(A_F + 8192 * b, [N], F32) for b in range(2)]
        hb = [at(A_F + 16384 + 2048 * b, [N], U8) for b in range(2)]
        bits = at(A_W, [N], U8)
        o_hl = at(A_W + 2048, [2, D], F32)
        x_in = [at(A_W + 4096 + 1024 * b, [D], F32) for b in range(2)]
        ms_row = (A_END - (A_F + 24576)) // 4
        ms = [at(o, [2, HB], F32) for o in (A_X, A_X + 8192, A_W + 6144)]
        ms.append(at(A_END - 8 * ms_row, [2, ms_row], F32)[:, :, ms_row - HB:])
        picks = [at(A_SG + 16384 * b, [H, N], F8) for b in range(2)]
        names = ("scores", "row_min", "picks", "packed", "bits", "unpacked", "values", "out_hi", "out",
                 "mask")
        sc_ok, tt_ok, sg_ok, pk_ok, pe_ok, up_ok, av_ok, oa_ok, od_ok, m3_ok = (
            sem("l3_" + n) for n in names)
        xt_ld, st_ok = [sem("l3_x0"), sem("l3_x1")], [sem("l3_stored0"), sem("l3_stored1")]
        gate_v, gate_t = sem("dve_gate"), sem("pe_gate")
        gate_p3 = sem("l3_pool_gate")
        row_min = sb("row_min", [P, 2, H], F32)
        PS_OFF = (0, 1)

        def steps(eng, step):
            step(0, 0, 0)
            step(1, 0, 1)
            with eng.Fori(1, T // 2 - 1) as i:
                step(i * 2, i, 0)
                step(i * 2 + 1, i, 1)
            step(T - 2, T // 2 - 1, 0)
            step(T - 1, T // 2 - 1, 1)
            step(T, T // 2, 0)
            step(T + 1, T // 2, 1)

        def l3_tensor(pe):
            def step(n, k, par):
                def scores(s):
                    h, q = SLOTS[s]
                    buf = (s + PS_OFF[par]) % 3
                    if isinstance(n, int) and n == 0 and q == 0 and h == H // 2:
                        pe.wait_ge(lay_late, 16 * 4)
                    if s >= 3:
                        need(pe, tt_ok, n * 16 + s - 2)
                    else:
                        old = max(o for o in range(13, 16) if (o + PS_OFF[1 - par]) % 3 == buf)
                        need(pe, tt_ok, n * 16 + old - 15)
                    for c in range(2):
                        last = pe.matmul(psum[:, 2 * buf + c, :], q4[:, h, bass.ds(n * P, P)],
                                         k4[:, h, HB * q + CH * c:HB * q + CH * c + CH], start=True, stop=True)
                    last.then_inc(sc_ok, 1)

                def pack(g):
                    need(pe, sg_ok, n * 8)
                    need(pe, pe_ok, n * 4 - 4 + g)
                    pe.sem_inc(gate_t, 1)
                    for kb in range(TC):
                        for h in range(H):
                            j = TC * g + kb
                            c = P * kb
                            last = pe.matmul(psum[:, 6, c:c + P], picks[1 - par][:, h, P * j:P * j + P],
                                             head_bit[:, h], start=(h == 0), stop=(h == H - 1))
                    last.then_inc(pk_ok, 1)

                def values(d, h):
                    need(pe, up_ok, n * 8 - 8 * d + h + 1)
                    if h == 0:
                        need(pe, oa_ok, n - d)
                    pe.sem_inc(gate_t, 1)
                    for j in range(T):
                        last = pe.matmul(psum[:, 7, 64 * h:64 * h + 64], hb[h % 2].bitcast(F8)[:, P * j:P * j + P],
                                         G[:, j, :, DH * h:DH * h + DH], start=(j == 0), stop=(j == T - 1))
                    last.then_inc(av_ok, 1)

                for s in range(16):
                    if has(n, 0):
                        scores(s)
                    for h in range(H):
                        if PE_VALUES[h] == 16 + s and has(n, 2):
                            values(2, h)
                    for g in range(C):
                        if PE_PACK[g] == s and has(n, 1):
                            pack(g)
                    for h in range(H):
                        if PE_VALUES[h] == s and has(n, 1):
                            values(1, h)
            pe.wait_ge(lay_ld, 16 * 8 * C)
            steps(pe, step)

        PE_PACK, PE_VALUES = (4, 7, 9, 11), (14, 15, 16, 17, 18, 19, 20, 21)
        DVE_UNPACK, ACT_TAKE, ACT_MASK = (11, 12, 13, 14, 15, 16, 17, 18), 1, 5

        def l3_vector(dve):
            def step(n, k, par):
                def scan(s):
                    h, q = SLOTS[s]
                    buf = (s + PS_OFF[par]) % 3
                    need(dve, sc_ok, n * 16 + s + 1)
                    if q == 0:
                        need(dve, sg_ok, n * 8 + h - 3)
                    else:
                        need(dve, tt_ok, n * 16 + FIRST[h] + 1)
                    if s == 0:
                        need(dve, m3_ok, n + 1)
                    dve.sem_inc(gate_v, 1)
                    dve.tensor_tensor_reduce(ms[h % 4][:, q],
                                             psum[:, 2 * buf:2 * buf + 2, :].rearrange("p a b -> p (a b)"),
                                             m3[par][:, HB * q:HB * q + HB], 1.0, -0.5 * NEG if q == 0 else row_min[:, 0, h:h + 1],
                                             ALU.add, ALU.min, row_min[:, q, h:h + 1]).then_inc(tt_ok, 1)

                def unpack(d, h):
                    need(dve, pe_ok, n * 4 + 4 - 4 * d)
                    need(dve, av_ok, n * 8 - 8 * d + h - 1)
                    dve.tensor_scalar(hb[h % 2].bitcast(U16), bits.bitcast(U16), abs(6 - h), 0x4040,
                                      ALU.logical_shift_left if h <= 6 else ALU.logical_shift_right,
                                      ALU.bitwise_and).then_inc(up_ok, 1)

                for s in range(16):
                    if has(n, 0):
                        scan(s)
                    for h in range(H):
                        if DVE_UNPACK[h] == 16 + s and has(n, 2):
                            unpack(2, h)
                        if DVE_UNPACK[h] == s and has(n, 1):
                            unpack(1, h)
            dve.tensor_scalar(sc[:, 6:7], kG[:, WV:WV + 1], 1.0 / 16, None, ALU.mult).then_inc(l3c, 1)
            dve.tensor_scalar(sc[:, 7:8], bec[:], -1.0, None, ALU.mult).then_inc(l3c, 1)
            dve.wait_ge(l3c, 2)
            steps(dve, step)

        l3c = sem("l3_const")

        def l3_scalar(act):
            def step(n, k, par):
                def sign(h):
                    need(act, tt_ok, n * 16 + SECOND[h] + 1)
                    if h == 0:
                        need(act, pk_ok, n * 4 - 4)
                    act.sem_inc(gate, 1)
                    act.activation(picks[par][:, h].rearrange("p (a b) -> p a b", a=2), ms[h % 4], ACT.Sign, bias=row_min[:, 1, h:h + 1],
                                   scale=-1.0, saturate=False).then_inc(sg_ok, 1)

                def to_bits(g):
                    need(act, pk_ok, n * 4 - 4 + g + 1)
                    need(act, up_ok, n * 8 - 8)
                    act.activation(bits[:, CH * g:CH * g + CH], psum[:, 6, :], ACT.Copy, bias=float(2 ** H - 1)
                                   ).then_inc(pe_ok, 1)

                def mask(m):
                    if m > 1 or not isinstance(m, int):
                        act.wait_ge(tt_ok, m * 16 - 16)
                    act.sem_inc(gate, 1)
                    act.activation(m3[m % 2 if isinstance(m, int) else 1 - par],
                                   no_edge[:, bass.ds(m, 1), :].rearrange("p a j -> p (a j)"), ACT.Identity,
                                   scale=-NEG, bias=sc[:, 7:8]).then_inc(m3_ok, 1)

                if isinstance(n, int) and n == 0:
                    mask(0)
                for h in range(H):
                    if has(n, 0):
                        sign(h)
                    if h == ACT_MASK and has(n, -1):
                        mask(n + 1)
                    if h == ACT_TAKE and has(n, 2):
                        need(act, av_ok, n * 8 - 8)
                        need(act, od_ok, n * 2 - 4)
                        act.activation(o_hl.rearrange("p a (h d) -> p h a d", h=H),
                                       psum[:, 7, :].rearrange("p (h a d) -> p h a d", h=H, a=2), ACT.Identity,
                                       scale=sc[:, 6:7]).then_inc(oa_ok, 1)
                    if h < 4 and has(n, 1):
                        to_bits(h)
            act.wait_ge(l3c, 2)
            steps(act, step)

        def l3_pool(pool):
            def take(n, k, par):
                pool.wait_ge(oa_ok, n + 1)
                nc.gpsimd.tensor_tensor(o_hl[:, 0], o_hl[:, 0], o_hl[:, 1], ALU.add).then_inc(od_ok, 1)
                pool.wait_ge(od_ok, n * 2 + 1)
                pool.wait_ge(xt_ld[par], k * 16 + 16)
                pool.sem_inc(gate_p3, 1)
                nc.gpsimd.tensor_tensor(x_in[par], o_hl[:, 0], x_in[par], ALU.add).then_inc(od_ok, 1)
            with pool.Fori(0, T // 2) as i:
                take(i * 2, i, 0)
                take(i * 2 + 1, i, 1)

        def l3_sync(sp):
            for r in range(4):
                rows_of_heads(sp, q4, 0, H // 2, H, r, r // 2, slice(0, N), lay_late)
            sp.wait_ge(lay_late, 16 * 4)

            def load(n, par):
                sp.dma_start(x_in[par], x_save[:, bass.ds(n, 1), :]).then_inc(xt_ld[par], 16)

            def store(n, par, stores):
                sp.wait_ge(od_ok, n * 2 + 2)
                sp.dma_start(out_t[:, bass.ds(n, 1), :], x_in[par]).then_inc(st_ok[par], 16)
                sp.wait_ge(st_ok[par], stores * 16)
            for par in range(2):
                load(par, par)
            with sp.Fori(0, T // 2 - 1) as i:
                for par in range(2):
                    store(i * 2 + par, par, i + 1)
                    load(i * 2 + par + 2, par)
            for par in range(2):
                store(T - 2 + par, par, T // 2)

        fronts = {}

        def new_front(i, name, copies, w, n, pa, pv, linear=None):
            f = Front(name)
            f.copies = copies
            f.post_act, f.post_dve = pa, pv
            f.linear = linear or linear_rows(w, n, lambda: fronts[i])
            fronts[i] = f

        new_front(0, "f0", 1, ws0, D, l0_post_act, l0_post_dve)
        new_front(1, "f1", 2, ws1, 2 * D, split_post_act(1), split_post_dve(1))
        new_front(2, "f2", 2, ws2, D + 2, split_post_act(2), split_post_dve(2))
        new_front(3, "f3", 3, None, 0, l3_post_act, l3_post_dve, l3_linear)
        fronts[1].per_v, fronts[2].per_v = 5, 2

        block = ctx.enter_context(nc.Block())

        def finish_sync(sp):
            sp.dma_start(out_t, xs).then_inc(x_ld, 16)
            sp.wait_ge(x_ld, 32)

        def restore_vector(dve):
            dve.wait_ge(dg, 2)
            dve.tensor_scalar(diag_blocks, diag_save, NEG, None, ALU.mult).then_inc(dg, 1)

        def front_stage(i):
            return dict(vector=fronts[i].vector, scalar=fronts[i].scalar, tensor=fronts[i].tensor)

        stages = [
            dict(sync=load_sync, pool=load_pool, vector=load_vector, scalar=load_scalar, tensor=load_tensor),
            front_stage(0),
            dict(vector=l0_unit_vector, scalar=l0_unit_scalar, tensor=l0_unit_tensor),
            dict(vector=l0_vector, scalar=l0_scalar, tensor=l0_tensor),
            dict(sync=l1_load, vector=lambda e: (restore_vector(e), fronts[1].vector(e)), scalar=fronts[1].scalar,
                 tensor=fronts[1].tensor),
            dict(pool=l1_pool, vector=l1_vector, scalar=l1_scalar, tensor=l1_tensor),
            front_stage(2),
            dict(vector=l2_pre_vector, scalar=l2_pre_scalar, tensor=l2_pre_tensor),
            dict(pool=l2_pool, vector=l2_vector, scalar=l2_scalar, tensor=l2_tensor),
            dict(sync=l3_lay_sync, **front_stage(3)),
            dict(sync=l3_sync, pool=l3_pool, vector=l3_vector, scalar=l3_scalar, tensor=l3_tensor),
        ]
        if stop:
            stages = stages[:stop]

        def run_stages(eng, name):
            for k, s in enumerate(stages):
                if name in s:
                    s[name](eng)
                stage_end(eng, k + 1)

        @block.sync
        def _(sp):
            run_stages(sp, "sync")
            if stop:
                finish_sync(sp)

        @block.gpsimd
        def _(pool):
            run_stages(pool, "pool")

        @block.vector
        def _(dve):
            run_stages(dve, "vector")

        @block.scalar
        def _(act):
            run_stages(act, "scalar")

        @block.tensor
        def _(pe):
            run_stages(pe, "tensor")


def kernel(**inputs):
    import numpy as np
    import concourse.bacc as bacc
    from concourse.bass_utils import run_bass_kernel_spmd

    nc = bacc.Bacc("TRN2", target_bir_lowering=False, num_devices=1)
    arrays = {}

    def given(name, array):
        arrays[name] = np.ascontiguousarray(array)
        return nc.dram_tensor(name, array.shape, mybir.dt.from_np(array.dtype), kind="ExternalInput").ap()

    g = {k: np.asarray(v) for k, v in inputs.items()}
    x, adj = given("x", g["x"]), given("adj", g["adj"])
    weights = [given("w0_T", g["L0_gnn_W"].T), given("w_nb_T", g["L1_gnn_W_nb"].T),
               given("w_line_T", g["L1_gnn_W_line"].T), given("w2", g["L2_gnn_W"]),
               given("wq_T", g["L3_gnn_WQ"].T), given("wk_T", g["L3_gnn_WK"].T), given("wv_T", g["L3_gnn_WV"].T)]
    attn, b_nb, b_line = given("attn", g["L2_gnn_attn"]), given("b_nb", g["L1_gnn_b_nb"]), given("b_line", g["L1_gnn_b_line"])
    we, be = given("we", g["L3_gnn_we"]), given("be", g["L3_gnn_be"])
    out = nc.dram_tensor("out", (N, D), F32, kind="ExternalOutput").ap()
    adjacency_net(nc, x, adj, weights, attn, b_nb, b_line, we, be, out, 0)
    r = run_bass_kernel_spmd(nc, [arrays], core_ids=[0])
    return r.results[0]["out"]
```
